# Optimizing a Trainium2 kernel written in Bass

```python
import numpy as np
import jax
import jax.numpy as jnp

def _softmax(x, axis=-1):
    return jax.nn.softmax(x, axis=axis)

def _gelu(x):
    return jax.nn.gelu(x, approximate=True)

def _silu(x):
    return jax.nn.silu(x)

def _sigmoid(x):
    return jax.nn.sigmoid(x)

def _layernorm(x, axis=-1, eps=1e-05):
    m = jnp.mean(x, axis=axis, keepdims=True)
    v = jnp.var(x, axis=axis, keepdims=True)
    return (x - m) / jnp.sqrt(v + eps)

def _scatter_add(tgt, idx, src, axis=0):
    return tgt.at[idx].add(src)

def _segment_sum(src, seg, n):
    return jax.ops.segment_sum(src, seg, n)
kernel_name = 'mk_decoder_preln_d1_seqx_r8_e74f07'

def setup_inputs(seed: int=0):
    np.random.seed(seed)
    _w = jnp.asarray

    def _rec_inputs():
        import jax
        import jax.numpy as jnp
        _rk = jax.random.key(seed)
        x = 7.22e-05 + 1 * jax.random.normal(jax.random.fold_in(_rk, 1), (128, 64, 128), jnp.float32)
        _lenS = 64 - jax.random.randint(jax.random.fold_in(_rk, 7), (128,), 0, max(1, 64 // 4) + 1, jnp.int32)
        _lenS2 = 64 - jax.random.randint(jax.random.fold_in(_rk, 8), (128,), 0, max(1, 64 // 4) + 1, jnp.int32)
        _ctx_1024P = jax.random.normal(jax.random.fold_in(_rk, 11), (128, 16, 128), jnp.float32)
        _ctx_1024c = jax.random.dirichlet(jax.random.fold_in(_rk, 511), 0.3 * jnp.ones((16,), jnp.float32), (128, 64))
        _ctx_1024t = jnp.einsum('bsk,bkd->bsd', _ctx_1024c, _ctx_1024P)
        _ctx_1024t = _ctx_1024t * jax.lax.rsqrt(jnp.mean(jnp.square(_ctx_1024t)) + 1e-12) * 0.953939
        ctx_1024 = 4.13588e-05 + 0.999923 * (_ctx_1024t + 0.3 * jax.random.normal(jax.random.fold_in(_rk, 611), (128, 64, 128), jnp.float32))
        return (x, ctx_1024)
    x, ctx_1024 = _rec_inputs()

    def _L0_attn_setup():
        import jax, jax.numpy as jnp
        import numpy as np
        SEQ, BATCH, DIM = (256, 8, 128)
        key = jax.random.key(seed)
        k1, k2, k3 = jax.random.split(key, 3)
        x = jax.random.normal(k1, (SEQ, BATCH, DIM), dtype=jnp.float32)
        Wq = jax.random.normal(k2, (DIM, DIM), dtype=jnp.float32) * DIM ** (-0.5)
        Wk = jax.random.normal(k3, (DIM, DIM), dtype=jnp.float32) * DIM ** (-0.5)
        return {'x': x, 'Wq': Wq, 'Wk': Wk}
    _L0_attn_all = _L0_attn_setup()
    _L0_attn_in = {k: v for k, v in _L0_attn_all.items() if k in ('Wq', 'Wk')}
    del _L0_attn_all

    def _L0_xattn_setup():
        import jax, jax.numpy as jnp
        import numpy as np
        EMBED = 128
        HEADS = 16
        HEAD_DIM = EMBED // HEADS
        key = jax.random.key(seed)
        ks = jax.random.split(key, 10)
        B, N, M = (4, 256, 256)
        s = 1.0 / np.sqrt(EMBED)
        return {'xq': jax.random.normal(ks[0], (B, N, EMBED), jnp.float32), 'xk': jax.random.normal(ks[1], (B, M, EMBED), jnp.float32), 'xv': jax.random.normal(ks[2], (B, M, EMBED), jnp.float32), 'Wq': jax.random.normal(ks[3], (EMBED, EMBED), jnp.float32) * s, 'bq': jnp.zeros((EMBED,), jnp.float32), 'Wk': jax.random.normal(ks[4], (EMBED, EMBED), jnp.float32) * s, 'bk': jnp.zeros((EMBED,), jnp.float32), 'Wv': jax.random.normal(ks[5], (EMBED, EMBED), jnp.float32) * s, 'bv': jnp.zeros((EMBED,), jnp.float32), 'Wo': jax.random.normal(ks[6], (EMBED, EMBED), jnp.float32) * s}
    _L0_xattn_all = _L0_xattn_setup()
    _L0_xattn_in = {k: v for k, v in _L0_xattn_all.items() if k in ('Wq', 'bq', 'Wk', 'bk', 'Wv', 'bv', 'Wo')}
    del _L0_xattn_all

    def _L0_ffn_setup():
        import jax, jax.numpy as jnp
        import numpy as np
        LN_EPS = 1e-05
        NORM_EPS = 1e-12

        def _layernorm(x, gamma, beta):
            mu = x.mean(axis=-1, keepdims=True)
            var = ((x - mu) ** 2).mean(axis=-1, keepdims=True)
            return (x - mu) * jax.lax.rsqrt(var + LN_EPS) * gamma + beta

        def _l2norm(x, axis):
            n = jnp.sqrt((x ** 2).sum(axis=axis, keepdims=True))
            return x / jnp.maximum(n, NORM_EPS)
        key = jax.random.key(seed)
        ks = jax.random.split(key, 4)
        B, N, D, E, S, H = (64, 32, 128, 16, 16, 32)
        x = jax.random.normal(ks[0], (B, N, D), dtype=jnp.float32)
        mu = jax.random.normal(ks[1], (D, E, S), dtype=jnp.float32) / np.sqrt(D)
        w1 = jax.random.normal(ks[2], (E, D, H), dtype=jnp.float32) * np.sqrt(2.0 / D)
        w2 = jax.random.normal(ks[3], (E, H, D), dtype=jnp.float32) * np.sqrt(2.0 / (H + D))
        return {'x': x, 'ln_gamma': jnp.ones((D,), jnp.float32), 'ln_beta': jnp.zeros((D,), jnp.float32), 'mu': mu, 'scale': jnp.ones((1,), jnp.float32), 'w1': w1, 'b1': jnp.zeros((E, H), jnp.float32), 'w2': w2, 'b2': jnp.zeros((E, D), jnp.float32)}
    _L0_ffn_all = _L0_ffn_setup()
    _L0_ffn_in = {k: v for k, v in _L0_ffn_all.items() if k in ('ln_gamma', 'ln_beta', 'mu', 'scale', 'w1', 'b1', 'w2', 'b2')}
    del _L0_ffn_all
    return {'x': x, 'ctx_1024': ctx_1024, 'L0_attn_Wq': _L0_attn_in['Wq'], 'L0_attn_Wk': _L0_attn_in['Wk'], 'L0_xattn_Wq': _L0_xattn_in['Wq'], 'L0_xattn_bq': _L0_xattn_in['bq'], 'L0_xattn_Wk': _L0_xattn_in['Wk'], 'L0_xattn_bk': _L0_xattn_in['bk'], 'L0_xattn_Wv': _L0_xattn_in['Wv'], 'L0_xattn_bv': _L0_xattn_in['bv'], 'L0_xattn_Wo': _L0_xattn_in['Wo'], 'L0_ffn_ln_gamma': _L0_ffn_in['ln_gamma'], 'L0_ffn_ln_beta': _L0_ffn_in['ln_beta'], 'L0_ffn_mu': _L0_ffn_in['mu'], 'L0_ffn_scale': _L0_ffn_in['scale'], 'L0_ffn_w1': _L0_ffn_in['w1'], 'L0_ffn_b1': _L0_ffn_in['b1'], 'L0_ffn_w2': _L0_ffn_in['w2'], 'L0_ffn_b2': _L0_ffn_in['b2']}

def reference(x, ctx_1024, L0_attn_Wq, L0_attn_Wk, L0_xattn_Wq, L0_xattn_bq, L0_xattn_Wk, L0_xattn_bk, L0_xattn_Wv, L0_xattn_bv, L0_xattn_Wo, L0_ffn_ln_gamma, L0_ffn_ln_beta, L0_ffn_mu, L0_ffn_scale, L0_ffn_w1, L0_ffn_b1, L0_ffn_w2, L0_ffn_b2):
    import jax
    import jax.numpy as jnp

    def _L0_attn_ref(x, Wq, Wk):
        import jax, jax.numpy as jnp
        import numpy as np
        SEQ, BATCH, DIM = (256, 8, 128)
        q = jnp.einsum('sbd,ed->sbe', x, Wq)
        k = jnp.einsum('sbd,ed->sbe', x, Wk)
        scale = jnp.asarray(x.shape[2], x.dtype) ** 0.5
        scores = jnp.einsum('sbd,tbd->bst', q, k) / scale
        align = jax.nn.softmax(jnp.tanh(scores), axis=2)
        out = jnp.einsum('bst,tbd->sbd', align, x)
        return out

    def _L0_xattn_ref(xq, xk, xv, Wq, bq, Wk, bk, Wv, bv, Wo):
        import jax, jax.numpy as jnp
        import numpy as np
        EMBED = 128
        HEADS = 16
        HEAD_DIM = EMBED // HEADS
        B, N, _ = xq.shape
        M = xk.shape[1]
        scale = HEAD_DIM ** (-0.5)
        q = (xq @ Wq.T + bq).reshape(B, N, HEADS, HEAD_DIM).transpose(0, 2, 1, 3)
        k = (xk @ Wk.T + bk).reshape(B, M, HEADS, HEAD_DIM).transpose(0, 2, 1, 3)
        v = (xv @ Wv.T + bv).reshape(B, M, HEADS, HEAD_DIM).transpose(0, 2, 1, 3)
        scores = jnp.einsum('bhnd,bhmd->bhnm', q, k) * scale
        weights = jax.nn.softmax(scores, axis=-1)
        out = jnp.einsum('bhnm,bhmd->bhnd', weights, v)
        out = out.transpose(0, 2, 1, 3).reshape(B, N, EMBED)
        return out @ Wo.T

    def _L0_ffn_ref(x, ln_gamma, ln_beta, mu, scale, w1, b1, w2, b2):
        import jax, jax.numpy as jnp
        import numpy as np
        LN_EPS = 1e-05
        NORM_EPS = 1e-12

        def _layernorm(x, gamma, beta):
            mu = x.mean(axis=-1, keepdims=True)
            var = ((x - mu) ** 2).mean(axis=-1, keepdims=True)
            return (x - mu) * jax.lax.rsqrt(var + LN_EPS) * gamma + beta

        def _l2norm(x, axis):
            n = jnp.sqrt((x ** 2).sum(axis=axis, keepdims=True))
            return x / jnp.maximum(n, NORM_EPS)
        B, N, D = x.shape
        _, E, S = mu.shape
        xn = _layernorm(x, ln_gamma, ln_beta)
        x_unit = _l2norm(xn, axis=-1)
        mu_unit = _l2norm(mu, axis=0)
        logits = jnp.einsum('bnd,des->bnes', x_unit * scale, mu_unit)
        dispatch = jax.nn.softmax(logits, axis=1)
        combine = jax.nn.softmax(logits.reshape(B, N, E * S), axis=-1).reshape(B, N, E, S)
        slot_in = jnp.einsum('bnd,bnes->besd', xn, dispatch)
        h = jax.nn.gelu(jnp.einsum('besd,edh->besh', slot_in, w1) + b1[None, :, None, :], approximate=False)
        slot_out = jnp.einsum('besh,ehd->besd', h, w2) + b2[None, :, None, :]
        out = jnp.einsum('besd,bnes->bnd', slot_out, combine)
        return out
    x = x + _L0_attn_ref(_layernorm(x, axis=-1), L0_attn_Wq, L0_attn_Wk)
    x = x + _L0_xattn_ref(_layernorm(x, axis=-1), ctx_1024, ctx_1024, L0_xattn_Wq, L0_xattn_bq, L0_xattn_Wk, L0_xattn_bk, L0_xattn_Wv, L0_xattn_bv, L0_xattn_Wo)
    x = x + _L0_ffn_ref(_layernorm(x, axis=-1), L0_ffn_ln_gamma, L0_ffn_ln_beta, L0_ffn_mu, L0_ffn_scale, L0_ffn_w1, L0_ffn_b1, L0_ffn_w2, L0_ffn_b2)
    return x

_drawn_inputs = setup_inputs


def setup_inputs(seed=0):
    import zlib

    import numpy as np

    out = dict(_drawn_inputs(seed))
    spreads = {'L0_xattn_bq': (0.0, 0.35),
     'L0_xattn_bk': (0.0, 0.8),
     'L0_xattn_bv': (0.0, 0.1),
     'L0_ffn_ln_gamma': (1.0, 0.6),
     'L0_ffn_ln_beta': (0.0, 0.669),
     'L0_ffn_b1': (0.0, 0.8),
     'L0_ffn_b2': (0.0, 0.391)}
    factors = {'L0_ffn_mu': 8.0}
    for name, (base, spread) in spreads.items():
        noise = np.random.default_rng([zlib.crc32(name.encode()), seed]).standard_normal(out[name].shape)
        drawn = base * np.exp(spread * noise) if base else spread * noise
        out[name] = jnp.asarray(drawn.astype(out[name].dtype))
    for name, factor in factors.items():
        out[name] = (out[name] * factor).astype(out[name].dtype)
    return out
```

```python
from contextlib import ExitStack

import concourse.bass as bass
from concourse import mybir

F32 = mybir.dt.float32
BF16 = mybir.dt.bfloat16
ALU = mybir.AluOpType
ACT = mybir.ActivationFunctionType
AX_X = mybir.AxisListType.X

P = 128
S, N, D = 128, 64, 128
HEADS, HD = 16, 8
EXPERTS, SLOTS, HID = 16, 16, 32
ES = EXPERTS * SLOTS
LN_EPS, NORM_EPS = 1e-5, 1e-12
CHUNKS = 16
TOK = S * N // CHUNKS
BC = N // CHUNKS
SC = S // CHUNKS
PC = SC // 2


class Chunk:

    def __init__(self, i, k):
        self.i, self.k = i, k
        self.m4, self.m2 = k % 4, k % 2
        self.v = k if i is None else i * 4 + k
        self.round = k // 4 if i is None else i + k // 4

    def plus(self, j):
        if self.i is None and not 0 <= self.k + j < CHUNKS:
            return None
        return Chunk(self.i, self.k + j)


class Signal:

    def __init__(self, sem, per=1):
        self.sem, self.per = sem, per

    def at(self, c, k=None):
        return c.v * self.per + (self.per if k is None else k)


class Landings:

    def __init__(self, sems, per=1):
        self.sems, self.per = sems, per

    def of(self, c):
        return self.sems[c.m4]

    def at(self, c):
        return (c.round + 1) * (16 * self.per)


def walk(eng, step, first, last, lo, hi):
    hi = lo + (hi - lo) // 4 * 4
    for t in range(first, lo):
        step(Chunk(None, t))
    with eng.Fori(0, (hi - lo) // 4) as i:
        for r in range(4):
            step(Chunk(i, lo + r))
    for t in range(hi, last):
        step(Chunk(None, t))


class Kit:

    def __init__(self, nc, forever, ctx):
        self.nc, self.forever, self.ctx = nc, forever, ctx

    def sb(self, name, shape, dt=F32):
        return self.ctx.enter_context(self.nc.sbuf_tensor(name, shape, dt))

    def sem(self, name):
        return self.forever.enter_context(self.nc.semaphore(name))

    def landings(self, name, per=1):
        return Landings([self.sem(f"{name}{i}") for i in range(4)], per)

    def sig(self, name, per=1):
        return Signal(self.sem(name), per)


def self_attention(nc, kit, ps, w, x, x1_dram):
    x_sb = kit.sb("x_sb", [P, N, D])
    stats = kit.sb("a_stats", [P, 2, BC, 6])
    mv = kit.sb("a_mv", [P, 2, BC, 2])
    rstd = kit.sb("a_rstd", [P, 2, BC])
    xn = kit.sb("a_xn", [P, 4, BC, D + 1])
    xT = kit.sb("a_xT", [P, 2, TOK])
    yT = kit.sb("a_yT", [P, 2, TOK])
    th = kit.sb("a_th", [P, 2, TOK])
    pr = kit.sb("a_pr", [P, 2, TOK])
    rden = kit.sb("a_rden", [P, 2, BC])
    x1 = kit.sb("a_x1", [P, 2, BC, D])

    x_in = kit.landings("a_x_in")
    ones_set = kit.sem("a_ones_set")
    stat = kit.sig("a_stat", 2)
    rooted = kit.sig("a_rooted", 2)
    normed = kit.sig("a_normed")
    xT_ps, xT_sb = kit.sig("a_xT_ps"), kit.sig("a_xT_sb")
    y_ps, y_sb = kit.sig("a_y_ps"), kit.sig("a_y_sb")
    s_ps, th_sb, p_sb = kit.sig("a_s_ps"), kit.sig("a_th_sb"), kit.sig("a_p_sb")
    o_ps, den = kit.sig("a_o_ps"), kit.sig("a_den")
    x1_sb, x1_out = kit.sig("a_x1_sb"), kit.landings("a_x1_out")

    def o_bank(c):
        return 4 + 2 * c.m2

    first, last, lo, hi = -3, CHUNKS, 2, CHUNKS - 3

    with nc.Block() as block:
        @block.sync
        def _(sp):
            def step(t):
                c = t.plus(8)
                if c:
                    if c.plus(-4): sp.wait_ge(x_in.of(c.plus(-4)), x_in.at(c.plus(-4)))
                    sp.dma_start(x_sb[:, bass.ts(c.v, BC), :], x[:, bass.ts(c.v, BC), :]).then_inc(x_in.of(c), 16)
                c = t.plus(0)
                if c:
                    sp.wait_ge(x1_sb.sem, x1_sb.at(c))
                    sp.dma_start(x1_dram[:, bass.ts(c.v, BC), :], x1[:, c.m2]).then_inc(x1_out.of(c), 16)
            walk(sp, step, -8, CHUNKS, 0, CHUNKS - 8)
            for k in range(CHUNKS - 4, CHUNKS):
                sp.wait_ge(x1_out.of(Chunk(None, k)), x1_out.at(Chunk(None, k)))

        @block.gpsimd
        def _(pool):
            def step(t):
                c = t.plus(3)
                if c:
                    pool.wait_ge(stat.sem, stat.at(c))
                    if c.plus(-2): pool.wait_ge(normed.sem, normed.at(c.plus(-2)))
                    nc.gpsimd.tensor_tensor(rstd[:, c.m2, :], mv[:, c.m2, :, 1], w["ln_eps"][:], ALU.add).then_inc(rooted.sem, 1)
                    pool.wait_ge(rooted.sem, rooted.at(c, 1))
                    nc.gpsimd.tensor_tensor(rstd[:, c.m2, :], rstd[:, c.m2, :], w["neg_half"][:, 0:BC],
                                            ALU.pow).then_inc(rooted.sem, 1)
            walk(pool, step, first, last, lo, hi)

        @block.vector
        def _(dve):
            nc.vector.memset(xn[:, :, :, D:D + 1], 1.0).then_inc(ones_set, 1)

            def step(t):
                c = t.plus(3)
                if c:
                    dve.wait_ge(x_in.of(c), x_in.at(c))
                    if c.plus(-2): dve.wait_ge(stat.sem, stat.at(c.plus(-2)))
                    if c.plus(-2): dve.wait_ge(normed.sem, normed.at(c.plus(-2)))
                    if c.plus(-2): dve.wait_ge(rooted.sem, rooted.at(c.plus(-2)))
                    xc = x_sb[:, bass.ts(c.v, BC), :]
                    for b in range(BC):
                        ins = nc.vector.bn_stats(stats[:, c.m2, b, :], xc[:, b, :])
                    ins.then_inc(stat.sem, 1)
                c = t.plus(2)
                if c:
                    xc = x_sb[:, bass.ts(c.v, BC), :]
                    dve.wait_ge(rooted.sem, rooted.at(c))
                    if c.plus(-4): dve.wait_ge(o_ps.sem, o_ps.at(c.plus(-4)))
                    if c.plus(1): dve.wait_ge(stat.sem, stat.at(c.plus(1), 1))
                    for b in range(BC):
                        ins = nc.vector.tensor_scalar(xn[:, c.m4, b, 0:D], xc[:, b, :], mv[:, c.m2, b, 0:1],
                                                      rstd[:, c.m2, b:b + 1], ALU.subtract, ALU.mult)
                    ins.then_inc(normed.sem, 1)
                c = t.plus(3)
                if c:
                    if t.plus(2) is None:
                        dve.wait_ge(stat.sem, stat.at(c, 1))
                    for b in range(BC):
                        ins = nc.vector.bn_aggr(mv[:, c.m2, b, :], stats[:, c.m2, b, :])
                    ins.then_inc(stat.sem, 1)
                c = t.plus(0)
                if c:
                    dve.wait_ge(o_ps.sem, o_ps.at(c))
                    if c.plus(-2): dve.wait_ge(x1_sb.sem, x1_sb.at(c.plus(-2)))
                    o = ps[:, o_bank(c):o_bank(c) + 2, 0:2 * (D + 1)].rearrange("p a (b e) -> p a b e", b=2)
                    nc.vector.reciprocal(rden[:, c.m2, :].rearrange("p (a b) -> p a b", a=2),
                                         o[:, :, :, D]).then_inc(den.sem, 1)
                    dve.wait_ge(den.sem, den.at(c))
                    if c.plus(-2): dve.wait_ge(x1_out.of(c.plus(-2)), x1_out.at(c.plus(-2)))
                    for b in range(BC):
                        ins = nc.vector.scalar_tensor_tensor(
                            out=x1[:, c.m2, b, :], in0=o[:, b // 2, b % 2, 0:D], scalar=rden[:, c.m2, b:b + 1],
                            in1=x_sb[:, bass.ds(c.v * BC + b, 1), :].rearrange("p a d -> p (a d)"), op0=ALU.mult, op1=ALU.add)
                    ins.then_inc(x1_sb.sem, 1)
            walk(dve, step, first, last, lo, hi)

        @block.scalar
        def _(act):
            def step(t):
                c = t.plus(1)
                if c:
                    act.wait_ge(y_ps.sem, y_ps.at(c))
                    nc.scalar.activation(yT[:, c.m2, :], ps[:, 1, :], ACT.Copy).then_inc(y_sb.sem, 1)
                c = t.plus(2)
                if c:
                    act.wait_ge(xT_ps.sem, xT_ps.at(c))
                    if c.plus(-2): act.wait_ge(s_ps.sem, s_ps.at(c.plus(-2)))
                    nc.scalar.activation(xT[:, c.m2, :], ps[:, 0, :], ACT.Copy).then_inc(xT_sb.sem, 1)
                c = t.plus(1)
                if c:
                    act.wait_ge(s_ps.sem, s_ps.at(c))
                    nc.scalar.activation(th[:, c.m2, :], ps[:, 2 + c.m2, :], ACT.Tanh,
                                         scale=float(D) ** -0.5).then_inc(th_sb.sem, 1)
                    act.wait_ge(th_sb.sem, th_sb.at(c))
                    if c.plus(-2): act.wait_ge(o_ps.sem, o_ps.at(c.plus(-2)))
                    nc.scalar.activation(pr[:, c.m2, :], th[:, c.m2, :], ACT.Exp).then_inc(p_sb.sem, 1)
            walk(act, step, first, last, lo, hi)

        @block.tensor
        def _(pe):
            pe.wait_ge(ones_set, 1)

            def step(t):
                c = t.plus(1)
                if c:
                    pe.wait_ge(xT_sb.sem, xT_sb.at(c))
                    if c.plus(-1): pe.wait_ge(y_sb.sem, y_sb.at(c.plus(-1)))
                    nc.tensor.matmul(ps[:, 1, :], w["L"][:], xT[:, c.m2, :], start=True, stop=True).then_inc(y_ps.sem, 1)
                c = t.plus(0)
                if c:
                    pe.wait_ge(p_sb.sem, p_sb.at(c))
                    if c.plus(-2): pe.wait_ge(x1_sb.sem, x1_sb.at(c.plus(-2)))
                    for b in range(BC):
                        ins = nc.tensor.matmul(ps[:, o_bank(c) + b // 2, (b % 2) * (D + 1):(b % 2 + 1) * (D + 1)],
                                               pr[:, c.m2, b * P:(b + 1) * P], xn[:, c.m4, b, :],
                                               start=True, stop=True)
                    ins.then_inc(o_ps.sem, 1)
                c = t.plus(2)
                if c:
                    pe.wait_ge(normed.sem, normed.at(c))
                    if c.plus(-1): pe.wait_ge(xT_sb.sem, xT_sb.at(c.plus(-1)))
                    for b in range(BC):
                        ins = nc.tensor.transpose(ps[:, 0, b * P:(b + 1) * P], xn[:, c.m4, b, 0:D], w["ident"][:])
                    ins.then_inc(xT_ps.sem, 1)
                c = t.plus(1)
                if c:
                    pe.wait_ge(y_sb.sem, y_sb.at(c))
                    if c.plus(-2): pe.wait_ge(th_sb.sem, th_sb.at(c.plus(-2)))
                    for b in range(BC):
                        ins = nc.tensor.matmul(ps[:, 2 + c.m2, b * P:(b + 1) * P], xT[:, c.m2, b * P:(b + 1) * P],
                                               yT[:, c.m2, b * P:(b + 1) * P], start=True, stop=True)
                    ins.then_inc(s_ps.sem, 1)
            walk(pe, step, first, last, lo, hi)


def prepare(nc, kit, ps, w, a):
    for name, shape in (("ident", [P, P]), ("ones", [P, P]), ("half", [P, ES]), ("neg_half", [P, PC]), ("ln_eps", [P, PC]), ("L", [P, P]), ("wqT", [P, P]), ("wkT", [P, P]),
                        ("wvT", [P, P]), ("woT", [P, P]), ("bq", [P, 1]), ("bk", [P, 1]), ("bv", [P, D]),
                        ("gamma", [P, D]), ("beta", [P, D]), ("mu", [P, ES]), ("scale", [P, 1]),
                        ("w1", [P, EXPERTS, HID]), ("b1", [P, 4]), ("w2", [P, 4, D]), ("b2", [P, 2, D])):
        w[name] = kit.sb("w_" + name, shape)
    with ExitStack() as ctx:
        tmp = Kit(nc, kit.forever, ctx)
        raw = {n: tmp.sb("raw_" + n, [P, P]) for n in ("aq", "ak", "q", "k", "v", "o")}
        wop = tmp.sb("raw_op", [P, P])
        mu = tmp.sb("raw_mu", [P, ES])
        sq = tmp.sb("raw_sq", [P, ES])
        loaded, ident_made = kit.sem("w_loaded"), kit.sem("w_ident")
        dve_step, products, copied = kit.sem("w_dve"), kit.sem("w_products"), kit.sem("w_copied")
        rooted = kit.sem("w_rooted")

        loads = [(raw["aq"][:], a["L0_attn_Wq"]), (raw["ak"][:], a["L0_attn_Wk"]), (raw["q"][:], a["L0_xattn_Wq"]),
                 (raw["k"][:], a["L0_xattn_Wk"]), (raw["v"][:], a["L0_xattn_Wv"]), (raw["o"][:], a["L0_xattn_Wo"]),
                 (w["bq"][:], a["L0_xattn_bq"].rearrange("(p o) -> p o", o=1)),
                 (w["bk"][:], a["L0_xattn_bk"].rearrange("(p o) -> p o", o=1)),
                 (w["bv"][:], a["L0_xattn_bv"].rearrange("(o d) -> o d", o=1).to_broadcast([P, D])),
                 (w["gamma"][:], a["L0_ffn_ln_gamma"].rearrange("(o d) -> o d", o=1).to_broadcast([P, D])),
                 (w["beta"][:], a["L0_ffn_ln_beta"].rearrange("(o d) -> o d", o=1).to_broadcast([P, D])),
                 (w["scale"][:], a["L0_ffn_scale"].rearrange("(o d) -> o d", o=1).to_broadcast([P, 1])),
                 (mu[:], a["L0_ffn_mu"].rearrange("d e s -> d (e s)")),
                 (w["w1"][:], a["L0_ffn_w1"].rearrange("e d h -> d e h"))]
        for g in range(4):
            loads.append((w["b1"][:, g:g + 1], a["L0_ffn_b1"][4 * g:4 * g + 4, :].rearrange("c (h o) -> (c h) o", o=1)))
            loads.append((w["w2"][:, g, :], a["L0_ffn_w2"][4 * g:4 * g + 4].rearrange("c h d -> (c h) d")))
        for e in range(EXPERTS):
            loads.append((w["b2"][SLOTS * (e % 8):SLOTS * (e % 8 + 1), e // 8, :],
                          a["L0_ffn_b2"][e:e + 1, :].to_broadcast([SLOTS, D])))

        with nc.Block() as block:
            @block.sync
            def _(sp):
                for dst, src in loads:
                    sp.dma_start(dst, src).then_inc(loaded, 16)

            @block.gpsimd
            def _(pool):
                nc.gpsimd.memset(w["ident"][:], 0.0).then_inc(ident_made, 1)
                pool.wait_ge(ident_made, 1)
                nc.gpsimd.affine_select(out=w["ident"][:], in_=w["ident"][:], compare_op=ALU.not_equal, fill=1.0,
                                        base=0, pattern=[[-1, P]], channel_multiplier=1).then_inc(ident_made, 1)
                pool.wait_ge(dve_step, 7)
                nc.gpsimd.tensor_tensor(sq[:], sq[:], w["half"][:], ALU.pow).then_inc(rooted, 1)

            @block.vector
            def _(dve):
                nc.vector.memset(w["ones"][:], 1.0).then_inc(dve_step, 1)
                nc.vector.memset(w["half"][:], 0.5).then_inc(dve_step, 1)
                nc.vector.memset(w["neg_half"][:], -0.5).then_inc(dve_step, 1)
                nc.vector.memset(w["ln_eps"][:], LN_EPS).then_inc(dve_step, 1)
                dve.wait_ge(loaded, 16 * len(loads))
                nc.vector.tensor_copy(wop[:].rearrange("p (j g d) -> p j g d", j=2, g=8),
                                      raw["o"][:].rearrange("p (g j d) -> p j g d", g=8, j=2)).then_inc(dve_step, 1)
                nc.vector.tensor_tensor(sq[:], mu[:], mu[:], ALU.mult).then_inc(dve_step, 1)
                dve.wait_ge(products, 2)
                nc.vector.tensor_copy(sq[:], ps[:, 1, 0:ES]).then_inc(dve_step, 1)
                dve.wait_ge(rooted, 1)
                nc.vector.tensor_scalar(sq[:], sq[:], NORM_EPS, None, ALU.max).then_inc(dve_step, 1)
                dve.wait_ge(dve_step, 8)
                nc.vector.reciprocal(sq[:], sq[:]).then_inc(dve_step, 1)
                dve.wait_ge(dve_step, 9)
                nc.vector.tensor_tensor(w["mu"][:], mu[:], sq[:], ALU.mult).then_inc(dve_step, 1)

            @block.tensor
            def _(pe):
                pe.wait_ge(loaded, 16 * len(loads))
                pe.wait_ge(ident_made, 2)
                pe.wait_ge(dve_step, 6)
                nc.tensor.matmul(ps[:, 0, 0:P], raw["aq"][:], raw["ak"][:], start=True, stop=True).then_inc(products, 1)
                nc.tensor.matmul(ps[:, 1, 0:ES], w["ones"][:], sq[:], start=True, stop=True).then_inc(products, 1)
                for i, n in enumerate(("q", "k", "v")):
                    nc.tensor.transpose(ps[:, 2 + i, 0:P], raw[n][:], w["ident"][:]).then_inc(products, 1)
                nc.tensor.transpose(ps[:, 5, 0:P], wop[:], w["ident"][:]).then_inc(products, 1)

            @block.scalar
            def _(act):
                for bank, n, k in ((0, "L", 1), (2, "wqT", 3), (3, "wkT", 4), (4, "wvT", 5), (5, "woT", 6)):
                    act.wait_ge(products, k)
                    nc.scalar.activation(w[n][:], ps[:, bank, 0:P], ACT.Copy).then_inc(copied, 1)


def cross_attention(nc, kit, ps, w, x1_dram, ctx_in, x_all):
    SPLITS = 6
    KROWS = ((0, 0, 3), (1, 3, 5), (2, 5, 6))
    QROWS = ((0, 3), (3, 5), (5, 6))
    MROW = 2 * SPLITS * HD
    G = HEADS // 2
    HT = TOK // 2
    V1 = HD + 1

    ctx_sb = kit.sb("c_ctx", [P, 4, PC, D])
    stats = kit.sb("c_stats", [P, 2, PC, 6])
    mv = kit.sb("c_mv", [P, 2, PC, 2])
    rstd = kit.sb("c_rstd", [P, 2, PC])
    xn = kit.sb("c_xn", [P, 2, PC, D])
    xT = kit.sb("c_xT", [P, 2, TOK])
    cT = kit.sb("c_cT", [P, 2, TOK])
    full = {n: kit.sb(f"c_{n}32", [P, 2, TOK]) for n in "qk"}
    rest = {n: kit.sb(f"c_{n}rest", [P, 2, TOK]) for n in "qk"}
    lead = {n: kit.sb(f"c_{n}lead", [P, 4, TOK], BF16) for n in "qk"}
    part = {n: kit.sb(f"c_{n}part", [P, 2, 2, TOK], BF16) for n in "qk"}
    part_dram = {n: nc.dram_tensor(f"{n}_parts", [CHUNKS, 3, P, TOK], BF16).ap() for n in "qk"}
    max_dram = nc.dram_tensor("maxima", [CHUNKS, 2, 2 * HEADS, P], BF16).ap()
    q_st = kit.sb("c_q_st", [P, 2, G, 2, TOK], BF16)
    k_st = kit.sb("c_k_st", [P, 2, G, TOK], BF16)
    k_bd = kit.sb("c_k_bd", [P, 2, HEADS, HT], BF16)
    mx = kit.sb("c_mx", [P, 4, 2 * HEADS])
    negmax = kit.sb("c_negmax", [2 * HEADS, 4, P], BF16)
    prob = kit.sb("c_prob", [P, 2, HEADS * N])
    v_bd = kit.sb("c_v_bd", [P, 4, PC, HEADS, 2, V1])
    rden = kit.sb("c_rden", [P, 2, 4 * G])
    o_sb = kit.sb("c_o", [P, 2, PC, 2, G * HD])
    o_tok = kit.sb("c_o_tok", [P, 2, PC, D])
    oT = kit.sb("c_oT", [P, 2, TOK])

    zeroed = kit.sem("c_zeroed")
    x_in, ctx_in_s = kit.landings("c_x_in"), kit.landings("c_ctx_in")
    stat, rooted, normed = kit.sig("c_stat", 2), kit.sig("c_rooted", 2), kit.sig("c_normed")
    xT_ps, cT_ps, xcT_sb = kit.sig("c_xT_ps"), kit.sig("c_cT_ps"), kit.sig("c_xcT_sb", 2)
    q_ps, k_ps, v_ps = kit.sig("c_q_ps"), kit.sig("c_k_ps"), kit.sig("c_v_ps")
    qk_sb = kit.sig("c_qk_sb", 4)
    split = kit.sig("c_split", 6)
    parts_out = {n: kit.landings(f"c_{n}_out", 2) for n in "qk"}
    spread = [kit.landings(f"c_spread{h}_", HEADS) for h in range(2)]
    filled = [kit.landings(f"c_filled{h}_", 4 * SPLITS) for h in range(2)]
    sc_ps, mx_sb = kit.sig("c_sc_ps", 4), kit.sig("c_mx_sb", 4)
    mT_ps, mT_sb = kit.sig("c_mT_ps", 2), kit.sig("c_mT_sb", 2)
    max_out = kit.sig("c_max_out", 32)
    max_in = [kit.landings(f"c_max_in{h}_", 4) for h in range(2)]
    st_ps, p_sb, o_ps = kit.sig("c_st_ps", 4), kit.sig("c_p_sb", 4), kit.sig("c_o_ps", 4)
    v_sb = kit.sig("c_v_sb")
    den, o_norm = kit.sig("c_den", 2), kit.sig("c_o_norm", 4)
    shuffled = kit.landings("c_shuffled", 4)
    oT_ps, oT_sb, wo_ps, x2_sb = kit.sig("c_oT_ps"), kit.sig("c_oT_sb"), kit.sig("c_wo_ps"), kit.sig("c_x2_sb")

    x1_v = x1_dram.rearrange("(c p r) n d -> c (r n) p d", p=PC, r=2)
    ctx_v = ctx_in.rearrange("(c p r) n d -> c (r n) p d", p=PC, r=2)
    first, last, lo, hi = -4, CHUNKS + 1, 3, CHUNKS - 4

    def dram(ap, c):
        return ap[bass.ds(c.v, 1)].rearrange("o a b d -> (o a) b d")

    with nc.Block() as block:
        @block.sync
        def _(sp):
            def fill(c, h):
                if not c:
                    return
                if c.plus(-2): sp.wait_ge(st_ps.sem, st_ps.at(c.plus(-2), 2 * h + 2))
                done = filled[h].of(c)
                src_q, src_k = dram(part_dram["q"], c), dram(part_dram["k"], c)
                at = slice(h * HT, (h + 1) * HT)
                for j in range(2):
                    row = j * SPLITS * HD
                    for p, u0, u1 in KROWS:
                        src = src_k[p:p + 1].rearrange("o (g j d) t -> (o j) d g t", j=2, d=HD)[j][:, :, at]
                        for u in range(u0, u1):
                            sp.dma_start(k_st[row + u * HD:row + (u + 1) * HD, c.m2, :, at], src).then_inc(done, 16)
                    for u0, u1 in QROWS:
                        for u in range(u0, u1):
                            src = src_q[u - u0:u - u0 + 1].rearrange("o (g j d) t -> (o j) d g t", j=2, d=HD)[j][:, :, at]
                            sp.dma_start(q_st[row + u * HD:row + (u + 1) * HD, c.m2, :, j, at], src).then_inc(done, 16)

            def spread_k(c, h):
                if not c:
                    return
                if h == 0:
                    sp.wait_ge(parts_out["q"].of(c), parts_out["q"].at(c))
                    sp.wait_ge(parts_out["k"].of(c), parts_out["k"].at(c))
                if c.plus(-1): sp.wait_ge(sc_ps.sem, sc_ps.at(c.plus(-1), 2 * h + 2))
                for head in range(HEADS):
                    at = slice(head * HD, (head + 1) * HD)
                    sp.dma_start(k_bd[at, h, head, :], dram(part_dram["k"], c)[0, at, h * HT:(h + 1) * HT]).then_inc(
                        spread[h].of(c), 16)

            def maxima(c, h):
                if not c:
                    return
                sp.wait_ge(mT_sb.sem, mT_sb.at(c, h + 1))
                dst = max_dram[bass.ds(c.v, 1)].rearrange("o a b d -> (o a) b d")[h]
                sp.dma_start(dst, negmax[:, 2 * c.m2 + h, :]).then_inc(max_out.sem, 16)
                sp.wait_ge(max_out.sem, max_out.at(c, 16 * (h + 1)))
                for j in range(2):
                    src = dst.rearrange("(o p g j) t -> j o p g t", g=G, o=1, j=2)[j]
                    for p in range(2):
                        at = slice(h * HT + p * P, h * HT + (p + 1) * P)
                        sp.dma_start(q_st[MROW + j:MROW + j + 1, c.m2, :, j, at], src[:, p]).then_inc(max_in[h].of(c), 16)

            def step(t):
                c = t.plus(8)
                if c:
                    if c.plus(-4): sp.wait_ge(x_in.of(c.plus(-4)), x_in.at(c.plus(-4)))
                    sp.dma_start(x_all[:, bass.ts(c.v, PC), :],
                                 x1_v[bass.ds(c.v, 1)].rearrange("o a b d -> (o a) b d")).then_inc(x_in.of(c), 16)
                c = t.plus(6)
                if c:
                    if c.plus(-4): sp.wait_ge(cT_ps.sem, cT_ps.at(c.plus(-4)))
                    sp.dma_start(ctx_sb[:, c.m4], ctx_v[bass.ds(c.v, 1)].rearrange("o a b d -> (o a) b d")).then_inc(
                        ctx_in_s.of(c), 16)
                c = t.plus(-1)
                if c:
                    sp.wait_ge(o_norm.sem, o_norm.at(c))
                    if c.plus(-2): sp.wait_ge(oT_ps.sem, oT_ps.at(c.plus(-2)))
                    for j in range(2):
                        for r in range(2):
                            sp.dma_start(o_tok[N * r:N * (r + 1), c.m2, :, G * HD * j:G * HD * (j + 1)],
                                         o_sb[N * j:N * (j + 1), c.m2, :, r, :]).then_inc(shuffled.of(c), 16)
                fill(t.plus(1), 1)
                maxima(t.plus(0), 1)
                spread_k(t.plus(2), 0)
                fill(t.plus(2), 0)
                maxima(t.plus(1), 0)
                c = t.plus(3)
                if c:
                    for k, n in enumerate("qk"):
                        sp.wait_ge(split.sem, split.at(c, 3 * k + 3))
                        sp.dma_start(dram(part_dram[n], c)[0], lead[n][:, c.m4]).then_inc(parts_out[n].of(c), 16)
                        sp.dma_start(dram(part_dram[n], c)[1:3].rearrange("a p t -> p a t"), part[n][:, c.m2]).then_inc(
                            parts_out[n].of(c), 16)
                spread_k(t.plus(2), 1)
            walk(sp, step, -8, last, lo, CHUNKS - 8)

        @block.gpsimd
        def _(pool):
            nc.gpsimd.memset(q_st[:], 0.0).then_inc(zeroed, 1)
            nc.gpsimd.memset(k_bd[:], 0.0).then_inc(zeroed, 1)

            def step(t):
                c = t.plus(4)
                if c:
                    pool.wait_ge(stat.sem, stat.at(c))
                    if c.plus(-2): pool.wait_ge(normed.sem, normed.at(c.plus(-2)))
                    nc.gpsimd.tensor_tensor(rstd[:, c.m2, :], mv[:, c.m2, :, 1], w["ln_eps"][:], ALU.add).then_inc(rooted.sem, 1)
                    pool.wait_ge(rooted.sem, rooted.at(c, 1))
                    nc.gpsimd.tensor_tensor(rstd[:, c.m2, :], rstd[:, c.m2, :], w["neg_half"][:, 0:PC],
                                            ALU.pow).then_inc(rooted.sem, 1)
                c = t.plus(3)
                if c:
                    for k, n in enumerate("qk"):
                        pool.wait_ge(qk_sb.sem, qk_sb.at(c, 2 * k + 2))
                        if c.plus(-2): pool.wait_ge(parts_out[n].of(c.plus(-2)), parts_out[n].at(c.plus(-2)))
                        if c.plus(-1): pool.wait_ge(split.sem, split.at(c.plus(-1)))
                        a, one, p, r = full[n][:, c.m2], lead[n][:, c.m4], part[n][:, c.m2], rest[n][:, c.m2]
                        nc.gpsimd.tensor_tensor(p[:, 0], a, one, ALU.subtract).then_inc(split.sem, 1)
                        nc.gpsimd.tensor_tensor(r, a, one, ALU.subtract).then_inc(split.sem, 1)
                        pool.wait_ge(split.sem, split.at(c, 3 * k + 2))
                        nc.gpsimd.tensor_tensor(p[:, 1], r, p[:, 0], ALU.subtract).then_inc(split.sem, 1)
            walk(pool, step, first, last, lo, hi)

        @block.vector
        def _(dve):
            nc.vector.memset(k_st[MROW:MROW + 2], 1.0).then_inc(zeroed, 1)
            nc.vector.memset(v_bd[:], 0.0).then_inc(zeroed, 1)
            dve.wait_ge(zeroed, 4)
            for r in range(2):
                nc.vector.memset(v_bd[N * r:N * (r + 1), :, :, :, r, HD:V1], 1.0).then_inc(zeroed, 1)

            def row_max(c, p, of=None):
                if not c:
                    return
                if of: dve.wait_ge(stat.sem, stat.at(of, 1))
                h = p // 2
                if c.plus(-2): dve.wait_ge(mT_ps.sem, mT_ps.at(c.plus(-2), h + 1))
                dve.wait_ge(sc_ps.sem, sc_ps.at(c, p + 1))
                nc.vector.reduce_max(mx[:, 2 * c.m2 + h, (p % 2) * HEADS:(p % 2 + 1) * HEADS],
                                     ps[:, 2:4, :].rearrange("p a (h m) -> p (a h) m", m=N), AX_X).then_inc(mx_sb.sem, 1)

            def normalise(c, h):
                if not c:
                    return
                if c.plus(-2): dve.wait_ge(shuffled.of(c.plus(-2)), shuffled.at(c.plus(-2)))
                dve.wait_ge(o_ps.sem, o_ps.at(c, 2 * h + 2))
                if c.plus(-1): dve.wait_ge(o_norm.sem, o_norm.at(c.plus(-1), 2 * h + 2))
                o = ps[:, 6 + h, 0:4 * G * V1].rearrange("p (a g r e) -> p a g r e", a=2, r=2, e=V1)
                nc.vector.reciprocal(rden[:, h], o[:, :, :, :, HD].rearrange("p a g r -> p (a g r)")).then_inc(den.sem, 1)
                dve.wait_ge(den.sem, den.at(c, h + 1))
                for p in range(2):
                    nc.vector.tensor_tensor(
                        o_sb[:, c.m2, 2 * h + p].rearrange("p r (g d) -> p g r d", g=G), o[:, p, :, :, 0:HD],
                        rden[:, h, 2 * G * p:2 * G * (p + 1)].rearrange("p (g r o) -> p g r o", r=2, o=1).to_broadcast([P, G, 2, HD]),
                        ALU.mult).then_inc(o_norm.sem, 1)

            def step(t):
                c = t.plus(4)
                if c:
                    dve.wait_ge(x_in.of(c), x_in.at(c))
                    if c.plus(-2): dve.wait_ge(stat.sem, stat.at(c.plus(-2)))
                    if c.plus(-2): dve.wait_ge(normed.sem, normed.at(c.plus(-2)))
                    for p in range(PC):
                        ins = nc.vector.bn_stats(stats[:, c.m2, p, :], x_all[:, bass.ds(c.v * PC + p, 1), :].rearrange("p a d -> p (a d)"))
                    ins.then_inc(stat.sem, 1)
                    if not t.plus(1):
                        dve.wait_ge(stat.sem, stat.at(c, 1))
                row_max(t.plus(1), 0, t.plus(4))
                if c:
                    for p in range(PC):
                        ins = nc.vector.bn_aggr(mv[:, c.m2, p, :], stats[:, c.m2, p, :])
                    ins.then_inc(stat.sem, 1)
                row_max(t.plus(1), 1)
                c = t.plus(4)
                if c:
                    dve.wait_ge(rooted.sem, rooted.at(c))
                    if c.plus(-2): dve.wait_ge(xT_ps.sem, xT_ps.at(c.plus(-2)))
                    for p in range(PC):
                        ins = nc.vector.tensor_scalar(xn[:, c.m2, p, :], x_all[:, bass.ds(c.v * PC + p, 1), :].rearrange("p a d -> p (a d)"),
                                                      mv[:, c.m2, p, 0:1], rstd[:, c.m2, p:p + 1], ALU.subtract, ALU.mult)
                    ins.then_inc(normed.sem, 1)
                c = t.plus(3)
                if c:
                    dve.wait_ge(v_ps.sem, v_ps.at(c))
                    if c.plus(-4): dve.wait_ge(o_ps.sem, o_ps.at(c.plus(-4)))
                    if c.i is None and c.k == 0:
                        dve.wait_ge(zeroed, 6)
                    for r in range(2):
                        at = slice(N * r, N * (r + 1))
                        ins = nc.vector.tensor_tensor(
                            v_bd[at, c.m4, :, :, r, 0:HD], ps[at, 0, :].rearrange("p (a h d) -> p a h d", a=PC, d=HD),
                            w["bv"][at].rearrange("p (o h d) -> p o h d", o=1, d=HD).to_broadcast([N, PC, HEADS, HD]), ALU.add)
                    ins.then_inc(v_sb.sem, 1)
                normalise(t.plus(0), 0)
                c = t.plus(-1)
                if c:
                    dve.wait_ge(wo_ps.sem, wo_ps.at(c))
                    nc.vector.tensor_tensor(x_all[:, bass.ts(c.v, PC), :], ps[:, 1, :].rearrange("p (a d) -> p a d", a=PC),
                                            x_all[:, bass.ts(c.v, PC), :], ALU.add).then_inc(x2_sb.sem, 1)
                row_max(t.plus(1), 2)
                normalise(t.plus(0), 1)
                row_max(t.plus(1), 3)
            walk(dve, step, first, last, lo, hi)

        @block.scalar
        def _(act):
            def exp(c, p):
                if not c:
                    return
                act.wait_ge(st_ps.sem, st_ps.at(c, p + 1))
                if p >= 2:
                    act.wait_ge(o_ps.sem, o_ps.at(c, p - 1))
                elif c.plus(-1):
                    act.wait_ge(o_ps.sem, o_ps.at(c.plus(-1), p + 3))
                nc.scalar.activation(prob[:, p % 2, :], ps[:, 4:6, :].rearrange("p a b -> p (a b)"), ACT.Exp,
                                     scale=float(HD) ** -0.5).then_inc(p_sb.sem, 1)

            def neg_max(c, h):
                if not c:
                    return
                act.wait_ge(mT_ps.sem, mT_ps.at(c, h + 1))
                if c.plus(-2): act.wait_ge(max_out.sem, max_out.at(c.plus(-2), 16 * (h + 1)))
                nc.scalar.activation(negmax[:, 2 * c.m2 + h, :], ps[0:2 * HEADS, 0, 0:P], ACT.Copy, scale=-1.0).then_inc(mT_sb.sem, 1)

            def step(t):
                exp(t.plus(0), 0)
                c = t.plus(3)
                if c:
                    act.wait_ge(xT_ps.sem, xT_ps.at(c))
                    if c.plus(-2): act.wait_ge(q_ps.sem, q_ps.at(c.plus(-2)))
                    nc.scalar.activation(xT[:, c.m2, :], ps[:, 0, :], ACT.Copy).then_inc(xcT_sb.sem, 1)
                    act.wait_ge(cT_ps.sem, cT_ps.at(c))
                    if c.plus(-2): act.wait_ge(v_ps.sem, v_ps.at(c.plus(-2)))
                    nc.scalar.activation(cT[:, c.m2, :], ps[:, 1, :], ACT.Copy).then_inc(xcT_sb.sem, 1)
                neg_max(t.plus(0), 1)
                exp(t.plus(0), 1)
                c = t.plus(3)
                if c:
                    for k, (n, ready, bias) in enumerate((("q", q_ps, "bq"), ("k", k_ps, "bk"))):
                        act.wait_ge(ready.sem, ready.at(c))
                        if c.plus(-2): act.wait_ge(split.sem, split.at(c.plus(-2), 3 * k + 3))
                        if c.plus(-4): act.wait_ge(parts_out[n].of(c.plus(-4)), parts_out[n].at(c.plus(-4)))
                        if k == 0:
                            if c.plus(-4): act.wait_ge(sc_ps.sem, sc_ps.at(c.plus(-4)))
                        nc.scalar.activation(full[n][:, c.m2, :], ps[:, k, :], ACT.Identity, bias=w[bias][:]).then_inc(qk_sb.sem, 1)
                        nc.scalar.activation(lead[n][:, c.m4, :], ps[:, k, :], ACT.Identity, bias=w[bias][:]).then_inc(qk_sb.sem, 1)
                c = t.plus(-1)
                if c:
                    act.wait_ge(oT_ps.sem, oT_ps.at(c))
                    if c.plus(-2): act.wait_ge(wo_ps.sem, wo_ps.at(c.plus(-2)))
                    nc.scalar.activation(oT[:, c.m2, :], ps[:, 1, :], ACT.Copy).then_inc(oT_sb.sem, 1)
                neg_max(t.plus(1), 0)
                exp(t.plus(0), 2)
                exp(t.plus(0), 3)
            walk(act, step, first, last, lo, hi)

        @block.tensor
        def _(pe):
            pe.wait_ge(zeroed, 6)

            def scores(c, p):
                if not c:
                    return
                if p % 2 == 0:
                    pe.wait_ge(spread[p // 2].of(c), spread[p // 2].at(c))
                if p:
                    pe.wait_ge(mx_sb.sem, mx_sb.at(c, p))
                else:
                    pe.wait_ge(qk_sb.sem, qk_sb.at(c, 2))
                    if c.plus(-1): pe.wait_ge(mx_sb.sem, mx_sb.at(c.plus(-1)))
                for b in range(2):
                    for r in range(2):
                        at = slice((2 * p + r) * N, (2 * p + r + 1) * N)
                        of = (p % 2 * 2 + r) * N
                        ins = nc.tensor.matmul(ps[N * r:N * (r + 1), 2 + b, :].rearrange("p (h m) -> p h m", m=N),
                                               lead["q"][:, c.m4, at],
                                               k_bd[:, p // 2, 8 * b:8 * b + 8, of:of + N], start=True, stop=True)
                ins.then_inc(sc_ps.sem, 1)

            def max_T(c, h):
                if not c:
                    return
                pe.wait_ge(mx_sb.sem, mx_sb.at(c, 2 * h + 2))
                if h == 0:
                    if c.plus(2): pe.wait_ge(v_sb.sem, v_sb.at(c.plus(2)))
                else:
                    if c.plus(3): pe.wait_ge(xcT_sb.sem, xcT_sb.at(c.plus(3), 1))
                nc.tensor.transpose(ps[0:2 * HEADS, 0, 0:P], mx[:, 2 * c.m2 + h, :], w["ident"][:]).then_inc(mT_ps.sem, 1)

            def scores_T(c, p):
                if not c:
                    return
                if p % 2 == 0:
                    pe.wait_ge(filled[p // 2].of(c), filled[p // 2].at(c))
                    pe.wait_ge(max_in[p // 2].of(c), max_in[p // 2].at(c))
                if p:
                    pe.wait_ge(p_sb.sem, p_sb.at(c, p))
                else:
                    if c.plus(-1): pe.wait_ge(p_sb.sem, p_sb.at(c.plus(-1)))
                for g in range(G):
                    for r in range(2):
                        at = slice((2 * p + r) * N, (2 * p + r + 1) * N)
                        ins = nc.tensor.matmul(
                            ps[N * r:N * (r + 1), 4 + g // 4, (g % 4) * P:(g % 4 + 1) * P].rearrange("p (j n) -> p j n", j=2),
                            k_st[0:MROW + 2, c.m2, g, at], q_st[0:MROW + 2, c.m2, g, :, at], start=True, stop=True)
                ins.then_inc(st_ps.sem, 1)

            def values(c, p):
                if not c:
                    return
                pe.wait_ge(p_sb.sem, p_sb.at(c, p + 1))
                if p == 0:
                    pe.wait_ge(v_sb.sem, v_sb.at(c))
                if p % 2 == 0:
                    if c.plus(-1): pe.wait_ge(o_norm.sem, o_norm.at(c.plus(-1), p + 2))
                for g in range(G):
                    for j in range(2):
                        at = (p % 2) * 2 * G * V1 + g * 2 * V1
                        ins = nc.tensor.matmul(ps[N * j:N * (j + 1), 6 + p // 2, at:at + 2 * V1].rearrange("p (r e) -> p r e", r=2),
                                               prob[:, p % 2, (2 * g + j) * N:(2 * g + j + 1) * N],
                                               v_bd[:, c.m4, p, 2 * g + j], start=True, stop=True)
                ins.then_inc(o_ps.sem, 1)

            def step(t):
                scores_T(t.plus(0), 0)
                c = t.plus(3)
                if c:
                    pe.wait_ge(normed.sem, normed.at(c))
                    if c.plus(-3): pe.wait_ge(mT_sb.sem, mT_sb.at(c.plus(-3), 1))
                    if c.plus(-1): pe.wait_ge(v_sb.sem, v_sb.at(c.plus(-1)))
                    for p in range(PC):
                        ins = nc.tensor.transpose(ps[:, 0, p * P:(p + 1) * P], xn[:, c.m2, p, :], w["ident"][:])
                    ins.then_inc(xT_ps.sem, 1)
                    pe.wait_ge(ctx_in_s.of(c), ctx_in_s.at(c))
                    if c.plus(-1): pe.wait_ge(qk_sb.sem, qk_sb.at(c.plus(-1)))
                    if c.plus(-5): pe.wait_ge(x2_sb.sem, x2_sb.at(c.plus(-5)))
                    for p in range(PC):
                        ins = nc.tensor.transpose(ps[:, 1, p * P:(p + 1) * P], ctx_sb[:, c.m4, p, :], w["ident"][:])
                    ins.then_inc(cT_ps.sem, 1)
                max_T(t.plus(0), 1)
                scores_T(t.plus(0), 1)
                values(t.plus(0), 0)
                scores(t.plus(1), 0)
                c = t.plus(3)
                if c:
                    pe.wait_ge(xcT_sb.sem, xcT_sb.at(c, 1))
                    if c.plus(-3): pe.wait_ge(mT_sb.sem, mT_sb.at(c.plus(-3)))
                    nc.tensor.matmul(ps[:, 0, :], w["wqT"][:], xT[:, c.m2, :], start=True, stop=True).then_inc(q_ps.sem, 1)
                    pe.wait_ge(xcT_sb.sem, xcT_sb.at(c))
                    nc.tensor.matmul(ps[:, 1, :], w["wkT"][:], cT[:, c.m2, :], start=True, stop=True).then_inc(k_ps.sem, 1)
                values(t.plus(0), 1)
                scores(t.plus(1), 1)
                c = t.plus(3)
                if c:
                    pe.wait_ge(qk_sb.sem, qk_sb.at(c, 2))
                    for p in range(PC):
                        ins = nc.tensor.matmul(ps[:, 0, p * P:(p + 1) * P], cT[:, c.m2, p * P:(p + 1) * P], w["wvT"][:],
                                               start=True, stop=True)
                    ins.then_inc(v_ps.sem, 1)
                c = t.plus(-1)
                if c:
                    pe.wait_ge(shuffled.of(c), shuffled.at(c))
                    if c.plus(4): pe.wait_ge(qk_sb.sem, qk_sb.at(c.plus(4)))
                    for p in range(PC):
                        ins = nc.tensor.transpose(ps[:, 1, p * P:(p + 1) * P], o_tok[:, c.m2, p, :], w["ident"][:])
                    ins.then_inc(oT_ps.sem, 1)
                max_T(t.plus(1), 0)
                scores_T(t.plus(0), 2)
                c = t.plus(-1)
                if c:
                    pe.wait_ge(oT_sb.sem, oT_sb.at(c))
                    for p in range(PC):
                        ins = nc.tensor.matmul(ps[:, 1, p * P:(p + 1) * P], oT[:, c.m2, p * P:(p + 1) * P], w["woT"][:],
                                               start=True, stop=True)
                    ins.then_inc(wo_ps.sem, 1)
                scores_T(t.plus(0), 3)
                values(t.plus(0), 2)
                scores(t.plus(1), 2)
                values(t.plus(0), 3)
                scores(t.plus(1), 3)
            walk(pe, step, first, last, lo, hi)


def experts_in(nc, kit, ps, w, x_all, hidden, comb_dram):
    stats = kit.sb("e_stats", [P, 2, PC, 6])
    mv = kit.sb("e_mv", [P, 2, PC, 2])
    rs = kit.sb("e_rs", [P, 2, PC])
    r1 = kit.sb("e_r1", [P, 2, PC])
    centred = kit.sb("e_centred", [P, 2, PC, D])
    xn = kit.sb("e_xn", [P, 4, PC, D])
    junk = kit.sb("e_junk", [P, PC, D])
    ss = kit.sb("e_ss", [P, 2, PC])
    sq = kit.sb("e_sq", [P, 2, PC])
    rn = kit.sb("e_rn", [P, 2, PC])
    xu = kit.sb("e_xu", [P, 2, PC, D])
    xuT = kit.sb("e_xuT", [P, 2, TOK])
    cm = kit.sb("e_cm", [P, 2, 2, SC])
    rm = kit.sb("e_rm", [P, 2, PC])
    neg_cm = kit.sb("e_neg_cm", [SC, 2, ES], BF16)
    neg_rm = kit.sb("e_neg_rm", [PC, 2, PC, P], BF16)
    sel32, sel = kit.sb("e_sel32", [SC, PC, P]), kit.sb("e_sel", [SC, PC, P], BF16)
    neg_diag = kit.sb("e_neg_diag", [PC, PC, P])
    ones4 = kit.sb("e_ones4", [PC, P], BF16)
    disp = kit.sb("e_disp", [P, 2, PC, ES])
    comb = kit.sb("e_comb", [P, 2, 2, TOK])
    slot_in = kit.sb("e_slot_in", [P, 2, SC, ES])
    rden = kit.sb("e_rden", [P, 2, 4, PC, 2, SLOTS])
    scaled = kit.sb("e_scaled", [P, 2, 4, SC * SLOTS])

    cleared, selected, ready = kit.sem("e_cleared"), kit.sem("e_selected"), kit.sem("e_ready")
    stat, root, normed = kit.sig("e_stat", 2), kit.sig("e_root", 7), kit.sig("e_normed", 2)
    squared, clamped, unit, xu_sb = kit.sig("e_squared"), kit.sig("e_clamped"), kit.sig("e_unit", 2), kit.sig("e_xu_sb")
    xuT_ps, xuT_sb = kit.sig("e_xuT_ps"), kit.sig("e_xuT_sb")
    lT_ps, lA_ps, max_sb = kit.sig("e_lT_ps"), kit.sig("e_lA_ps"), kit.sig("e_max_sb", 2)
    mT_ps, ncm_sb, nrm_sb = kit.sig("e_mT_ps"), kit.sig("e_ncm_sb"), kit.sig("e_nrm_sb")
    shA_ps, shT_ps, disp_sb, comb_sb = kit.sig("e_shA_ps"), kit.sig("e_shT_ps"), kit.sig("e_disp_sb"), kit.sig("e_comb_sb")
    in_ps, in_sb = kit.sig("e_in_ps", 2), kit.sig("e_in_sb", 2)
    den_ps, rden_sb, h_ps, h_sb, biased = kit.sig("e_den_ps"), kit.sig("e_rden_sb"), kit.sig("e_h_ps"), kit.sig("e_h_sb"), kit.sig("e_biased")
    comb_out = kit.landings("e_comb_out")
    first, last, lo, hi = -4, CHUNKS, 4, CHUNKS - 4

    def tok(c, p):
        return x_all[:, bass.ds(c.v * PC + p, 1), :].rearrange("p a d -> p (a d)")

    with nc.Block() as block:
        @block.sync
        def _(sp):
            def step(c):
                sp.wait_ge(comb_sb.sem, comb_sb.at(c))
                sp.dma_start(comb_dram[bass.ds(c.v, 1)].rearrange("o p t -> (o p) t"),
                             comb[:, c.m2].rearrange("p a t -> p (a t)")).then_inc(comb_out.of(c), 16)
            walk(sp, step, 0, CHUNKS, 4, CHUNKS)
            for k in range(CHUNKS - 4, CHUNKS):
                sp.wait_ge(comb_out.of(Chunk(None, k)), comb_out.at(Chunk(None, k)))

        @block.gpsimd
        def _(pool):
            nc.gpsimd.memset(sel32[:], 0.0).then_inc(cleared, 1)
            nc.gpsimd.memset(neg_diag[:], 0.0).then_inc(cleared, 1)
            pool.wait_ge(cleared, 2)
            nc.gpsimd.affine_select(out=sel32[:].rearrange("s p (r n) -> s p r n", r=2), in_=sel32[:].rearrange("s p (r n) -> s p r n", r=2),
                                    compare_op=ALU.not_equal, fill=1.0, base=0, pattern=[[-2, PC], [-1, 2], [0, N]],
                                    channel_multiplier=1).then_inc(selected, 1)
            nc.gpsimd.affine_select(out=neg_diag[:], in_=neg_diag[:], compare_op=ALU.not_equal, fill=-1.0, base=0,
                                    pattern=[[-1, PC], [0, P]], channel_multiplier=1).then_inc(selected, 1)

            def step(t):
                c = t.plus(4)
                if c:
                    pool.wait_ge(stat.sem, stat.at(c))
                    if c.plus(-2): pool.wait_ge(normed.sem, normed.at(c.plus(-2)))
                    v, a, b, half, eps = mv[:, c.m2, :, 1], r1[:, c.m2], rs[:, c.m2], w["neg_half"][:, 0:PC], w["ln_eps"][:]
                    for k, args in enumerate(((a, v, eps, ALU.add), (a, a, half, ALU.pow), (b, a, a, ALU.mult), (b, b, v, ALU.mult),
                                              (b, b, eps, ALU.add), (b, b, half, ALU.pow), (b, b, a, ALU.mult))):
                        if k:
                            pool.wait_ge(root.sem, root.at(c, k))
                        nc.gpsimd.tensor_tensor(*args).then_inc(root.sem, 1)
                c = t.plus(3)
                if c:
                    pool.wait_ge(clamped.sem, clamped.at(c))
                    if c.plus(-2): pool.wait_ge(xu_sb.sem, xu_sb.at(c.plus(-2)))
                    nc.gpsimd.tensor_tensor(rn[:, c.m2], sq[:, c.m2], w["neg_half"][:, 0:PC], ALU.pow).then_inc(unit.sem, 1)
                    pool.wait_ge(unit.sem, unit.at(c, 1))
                    nc.gpsimd.tensor_tensor(rn[:, c.m2], rn[:, c.m2], w["scale"][:].to_broadcast([P, PC]),
                                            ALU.mult).then_inc(unit.sem, 1)
                c = t.plus(0)
                if c:
                    pool.wait_ge(h_sb.sem, h_sb.at(c))
                    nc.gpsimd.tensor_tensor(hidden[:, :, bass.ts(c.v, SC * SLOTS)], scaled[:, c.m2],
                                            w["b1"][:].rearrange("p (g o) -> p g o", o=1).to_broadcast([P, 4, SC * SLOTS]),
                                            ALU.add).then_inc(biased.sem, 1)
            walk(pool, step, first, last, lo, hi)

        @block.vector
        def _(dve):
            nc.vector.memset(ones4[:], 1.0).then_inc(ready, 1)
            dve.wait_ge(selected, 2)
            nc.vector.tensor_copy(sel[:], sel32[:]).then_inc(ready, 1)

            def step(t):
                c = t.plus(4)
                if c:
                    if c.plus(-2): dve.wait_ge(stat.sem, stat.at(c.plus(-2)))
                    if c.plus(-2): dve.wait_ge(normed.sem, normed.at(c.plus(-2)))
                    for p in range(PC):
                        ins = nc.vector.bn_stats(stats[:, c.m2, p, :], tok(c, p))
                    ins.then_inc(stat.sem, 1)
                c = t.plus(3)
                if c:
                    dve.wait_ge(root.sem, root.at(c))
                    if c.plus(-2): dve.wait_ge(normed.sem, normed.at(c.plus(-2)))
                    if c.plus(-4): dve.wait_ge(in_ps.sem, in_ps.at(c.plus(-4)))
                    if c.plus(1): dve.wait_ge(stat.sem, stat.at(c.plus(1), 1))
                    if c.plus(-4): dve.wait_ge(xu_sb.sem, xu_sb.at(c.plus(-4)))
                    for p in range(PC):
                        ins = nc.vector.scalar_tensor_tensor(out=centred[:, c.m2, p], in0=tok(c, p), scalar=mv[:, c.m2, p, 0:1],
                                                             in1=w["gamma"][:], op0=ALU.subtract, op1=ALU.mult)
                    ins.then_inc(normed.sem, 1)
                c = t.plus(4)
                if c:
                    if not t.plus(3):
                        dve.wait_ge(stat.sem, stat.at(c, 1))
                    for p in range(PC):
                        ins = nc.vector.bn_aggr(mv[:, c.m2, p, :], stats[:, c.m2, p, :])
                    ins.then_inc(stat.sem, 1)
                c = t.plus(3)
                if c:
                    dve.wait_ge(normed.sem, normed.at(c, 1))
                    for p in range(PC):
                        ins = nc.vector.scalar_tensor_tensor(out=xn[:, c.m4, p], in0=centred[:, c.m2, p], scalar=rs[:, c.m2, p:p + 1],
                                                             in1=w["beta"][:], op0=ALU.mult, op1=ALU.add)
                    ins.then_inc(normed.sem, 1)
                c = t.plus(1)
                if c:
                    if c.plus(-2): dve.wait_ge(mT_ps.sem, mT_ps.at(c.plus(-2)))
                    dve.wait_ge(lT_ps.sem, lT_ps.at(c))
                    nc.vector.reduce_max(cm[:, c.m2].rearrange("p a s -> p (a s)"),
                                         ps[:, 3:5, :].rearrange("p a (s n) -> p (a s) n", n=N), AX_X).then_inc(max_sb.sem, 1)
                    dve.wait_ge(lA_ps.sem, lA_ps.at(c))
                    nc.vector.reduce_max(rm[:, c.m2], ps[:, 1:3, :].rearrange("p a (b e) -> p (a b) e", e=ES), AX_X).then_inc(max_sb.sem, 1)
                c = t.plus(3)
                if c:
                    dve.wait_ge(squared.sem, squared.at(c))
                    if c.plus(-2): dve.wait_ge(unit.sem, unit.at(c.plus(-2)))
                    nc.vector.tensor_scalar(sq[:, c.m2], ss[:, c.m2], NORM_EPS ** 2, None, ALU.max).then_inc(clamped.sem, 1)
                c = t.plus(1)
                if c:
                    dve.wait_ge(mT_ps.sem, mT_ps.at(c))
                    if c.plus(-2): dve.wait_ge(shT_ps.sem, shT_ps.at(c.plus(-2)))
                    nc.vector.tensor_tensor(neg_rm[:, c.m2], ps[0:PC, 5, 2 * P:3 * P].rearrange("q (o t) -> q o t", o=1).to_broadcast([PC, PC, P]),
                                            neg_diag[:], ALU.mult).then_inc(nrm_sb.sem, 1)
                c = t.plus(3)
                if c:
                    dve.wait_ge(unit.sem, unit.at(c))
                    if c.plus(-2): dve.wait_ge(xuT_ps.sem, xuT_ps.at(c.plus(-2)))
                    for p in range(PC):
                        ins = nc.vector.tensor_scalar(xu[:, c.m2, p], xn[:, c.m4, p], rn[:, c.m2, p:p + 1], None, ALU.mult)
                    ins.then_inc(xu_sb.sem, 1)
                c = t.plus(0)
                if c:
                    dve.wait_ge(den_ps.sem, den_ps.at(c))
                    if c.plus(-2): dve.wait_ge(h_sb.sem, h_sb.at(c.plus(-2)))
                    for r, bank in enumerate((0, 5)):
                        ins = nc.vector.reciprocal(rden[:, c.m2, :, :, r], ps[:, bank, 0:TOK // 2].rearrange("p (g a k) -> p g a k", g=4, a=PC))
                    ins.then_inc(rden_sb.sem, 1)
                    dve.wait_ge(rden_sb.sem, rden_sb.at(c))
                    dve.wait_ge(h_ps.sem, h_ps.at(c))
                    if c.plus(-2): dve.wait_ge(biased.sem, biased.at(c.plus(-2)))
                    nc.vector.tensor_tensor(scaled[:, c.m2], ps[:, 6, :].rearrange("p (g k) -> p g k", g=4),
                                            rden[:, c.m2].rearrange("p g a r k -> p g (a r k)"), ALU.mult).then_inc(h_sb.sem, 1)
            walk(dve, step, first, last, lo, hi)

        @block.scalar
        def _(act):
            def slots(c, h):
                if not c:
                    return
                act.wait_ge(in_ps.sem, in_ps.at(c, h + 1))
                if c.plus(-2): act.wait_ge(h_ps.sem, h_ps.at(c.plus(-2)))
                nc.scalar.activation(slot_in[:, c.m2, 4 * h:4 * h + 4].rearrange("p (a r) e -> p r a e", r=2),
                                     ps[:, 6:8, :].rearrange("p r (a e) -> p r a e", a=2), ACT.Copy).then_inc(in_sb.sem, 1)

            def step(t):
                slots(t.plus(0), 0)
                c = t.plus(3)
                if c:
                    act.wait_ge(normed.sem, normed.at(c))
                    if c.plus(-2): act.wait_ge(clamped.sem, clamped.at(c.plus(-2)))
                    if c.plus(-1): act.wait_ge(squared.sem, squared.at(c.plus(-1)))
                    for p in range(PC):
                        ins = nc.scalar.activation(junk[:, p], xn[:, c.m4, p], ACT.Square, accum_out=ss[:, c.m2, p:p + 1])
                    ins.then_inc(squared.sem, 1)
                slots(t.plus(0), 1)
                c = t.plus(1)
                if c:
                    act.wait_ge(mT_ps.sem, mT_ps.at(c))
                    if c.plus(-2): act.wait_ge(shA_ps.sem, shA_ps.at(c.plus(-2)))
                    act.wait_ge(nrm_sb.sem, nrm_sb.at(c))
                    nc.scalar.activation(neg_cm[:, c.m2], ps[0:SC, 5, 0:ES], ACT.Copy, scale=-1.0).then_inc(ncm_sb.sem, 1)
                    act.wait_ge(shA_ps.sem, shA_ps.at(c))
                    if c.plus(-2): act.wait_ge(in_ps.sem, in_ps.at(c.plus(-2)))
                    if c.plus(-2): act.wait_ge(den_ps.sem, den_ps.at(c.plus(-2)))
                    nc.scalar.activation(disp[:, c.m2].rearrange("p a e -> p (a e)"), ps[:, 1:3, :].rearrange("p a b -> p (a b)"),
                                         ACT.Exp).then_inc(disp_sb.sem, 1)
                    act.wait_ge(shT_ps.sem, shT_ps.at(c))
                    if c.plus(-2): act.wait_ge(comb_out.of(c.plus(-2)), comb_out.at(c.plus(-2)))
                    nc.scalar.activation(comb[:, c.m2].rearrange("p a e -> p (a e)"), ps[:, 3:5, :].rearrange("p a b -> p (a b)"),
                                         ACT.Exp).then_inc(comb_sb.sem, 1)
                c = t.plus(2)
                if c:
                    act.wait_ge(xuT_ps.sem, xuT_ps.at(c))
                    if c.plus(-2): act.wait_ge(lA_ps.sem, lA_ps.at(c.plus(-2)))
                    nc.scalar.activation(xuT[:, c.m2], ps[:, 0, :], ACT.Copy).then_inc(xuT_sb.sem, 1)
            walk(act, step, first, last, lo, hi)

        @block.tensor
        def _(pe):
            pe.wait_ge(ready, 2)

            def gather(c, h):
                if not c:
                    return
                pe.wait_ge(disp_sb.sem, disp_sb.at(c))
                if h:
                    pe.wait_ge(in_sb.sem, in_sb.at(c, 1))
                else:
                    if c.plus(-1): pe.wait_ge(in_sb.sem, in_sb.at(c.plus(-1)))
                    if c.plus(-1): pe.wait_ge(h_sb.sem, h_sb.at(c.plus(-1)))
                for a in range(2):
                    for r in range(2):
                        p, at = 2 * h + a, slice(N * r, N * (r + 1))
                        ins = nc.tensor.matmul(ps[:, 6 + r, a * ES:(a + 1) * ES], xn[at, c.m4, p, :], disp[at, c.m2, p, :],
                                               start=True, stop=True)
                ins.then_inc(in_ps.sem, 1)

            def step(t):
                gather(t.plus(0), 0)
                c = t.plus(1)
                if c:
                    pe.wait_ge(xuT_sb.sem, xuT_sb.at(c))
                    if c.plus(-1): pe.wait_ge(comb_sb.sem, comb_sb.at(c.plus(-1)))
                    for h in range(2):
                        ins = nc.tensor.matmul(ps[:, 3 + h, :], w["mu"][:, h * P:(h + 1) * P], xuT[:, c.m2, :],
                                               start=True, stop=False, skip_group_check=True)
                    ins.then_inc(lT_ps.sem, 1)
                    if c.plus(-1): pe.wait_ge(disp_sb.sem, disp_sb.at(c.plus(-1)))
                    for p in range(PC):
                        ins = nc.tensor.matmul(ps[:, 1 + p // 2, p % 2 * ES:(p % 2 + 1) * ES], xuT[:, c.m2, p * P:(p + 1) * P],
                                               w["mu"][:], start=p % 2 == 0, stop=False, skip_group_check=True)
                    ins.then_inc(lA_ps.sem, 1)
                gather(t.plus(0), 1)
                c = t.plus(1)
                if c:
                    pe.wait_ge(max_sb.sem, max_sb.at(c))
                    if c.plus(-2): pe.wait_ge(rden_sb.sem, rden_sb.at(c.plus(-2)))
                    for h in range(2):
                        nc.tensor.transpose(ps[0:SC, 5, h * P:(h + 1) * P], cm[:, c.m2, h, :], w["ident"][:])
                    nc.tensor.transpose(ps[0:PC, 5, 2 * P:3 * P], rm[:, c.m2, :], w["ident"][:]).then_inc(mT_ps.sem, 1)
                    pe.wait_ge(nrm_sb.sem, nrm_sb.at(c))
                    pe.wait_ge(ncm_sb.sem, ncm_sb.at(c))
                    for p in range(PC):
                        ins = nc.tensor.matmul(ps[:, 1 + p // 2, p % 2 * ES:(p % 2 + 1) * ES], sel[:, p, :], neg_cm[:, c.m2],
                                               start=False, stop=True, skip_group_check=True)
                    ins.then_inc(shA_ps.sem, 1)
                    for h in range(2):
                        ins = nc.tensor.matmul(ps[:, 3 + h, :], ones4[:], neg_rm[:, c.m2].rearrange("q a t -> q (a t)"),
                                               start=False, stop=True, skip_group_check=True)
                    ins.then_inc(shT_ps.sem, 1)
                c = t.plus(0)
                if c:
                    for r, bank in enumerate((0, 5)):
                        at = slice(N * r, N * (r + 1))
                        for p in range(PC):
                            for e in range(4):
                                ins = nc.tensor.matmul(
                                    ps[HID * e:HID * (e + 1), bank, 0:TOK // 2].rearrange("p (g a k) -> p g a k", g=4, a=PC)[:, :, p, :],
                                    w["ones"][at, 0:HID],
                                    disp[at, c.m2, p, :].rearrange("p (g e k) -> p g e k", g=4, e=4)[:, :, e, :],
                                    start=True, stop=True)
                    ins.then_inc(den_ps.sem, 1)
                    pe.wait_ge(in_sb.sem, in_sb.at(c))
                    for g in range(4):
                        for e in range(4):
                            x = 4 * g + e
                            ins = nc.tensor.matmul(ps[HID * e:HID * (e + 1), 6, g * P:(g + 1) * P].rearrange("p (s k) -> p s k", s=SC),
                                                   w["w1"][:, x, :], slot_in[:, c.m2, :, x * SLOTS:(x + 1) * SLOTS],
                                                   start=True, stop=True)
                    ins.then_inc(h_ps.sem, 1)
                c = t.plus(2)
                if c:
                    pe.wait_ge(xu_sb.sem, xu_sb.at(c))
                    if c.plus(-2): pe.wait_ge(rden_sb.sem, rden_sb.at(c.plus(-2)))
                    for p in range(PC):
                        ins = nc.tensor.transpose(ps[:, 0, p * P:(p + 1) * P], xu[:, c.m2, p, :], w["ident"][:])
                    ins.then_inc(xuT_ps.sem, 1)
            walk(pe, step, first, last, lo, hi)


def experts_out(nc, kit, ps, w, x_all, hidden, comb_dram, out):
    h_bd = kit.sb("o_h_bd", [P, 2, SC, 4, 4, SLOTS])
    slot_out = kit.sb("o_slot_out", [P, 2, SC, 2, D + 1])
    comb = kit.sb("o_comb", [P, 2, 2, TOK])
    rden = kit.sb("o_rden", [P, 2, PC])
    y = kit.sb("o_y", [P, 2, PC, D])

    zeroed = kit.sem("o_zeroed")
    act_sb = kit.sig("o_act_sb")
    s_ps, s_sb = kit.sig("o_s_ps", 4), kit.sig("o_s_sb", 4)
    comb_in = kit.landings("o_comb_in")
    y_ps, den, y_sb = kit.sig("o_y_ps", 4), kit.sig("o_den", 2), kit.sig("o_y_sb", 2)
    y_out = kit.landings("o_y_out")
    out_v = out.rearrange("(c p r) n d -> c (r n) p d", p=PC, r=2)
    first, last, lo, hi = -2, CHUNKS, 2, CHUNKS - 2

    with nc.Block() as block:
        @block.gpsimd
        def _(pool):
            nc.gpsimd.memset(h_bd[:], 0.0).then_inc(zeroed, 1)

        @block.sync
        def _(sp):
            def step(t):
                c = t.plus(2)
                if c:
                    if c.plus(-2): sp.wait_ge(y_ps.sem, y_ps.at(c.plus(-2)))
                    sp.dma_start(comb[:, c.m2].rearrange("p a t -> p (a t)"),
                                 comb_dram[bass.ds(c.v, 1)].rearrange("o p t -> (o p) t")).then_inc(comb_in.of(c), 16)
                c = t.plus(0)
                if c:
                    sp.wait_ge(y_sb.sem, y_sb.at(c))
                    sp.dma_start(out_v[bass.ds(c.v, 1)].rearrange("o a b d -> (o a) b d"), y[:, c.m2]).then_inc(y_out.of(c), 16)
            walk(sp, step, first, last, lo, hi)
            for k in range(CHUNKS - 4, CHUNKS):
                sp.wait_ge(y_out.of(Chunk(None, k)), y_out.at(Chunk(None, k)))

        @block.scalar
        def _(act):
            act.wait_ge(zeroed, 2)

            def step(t):
                c = t.plus(2)
                if c:
                    if c.plus(-2): act.wait_ge(s_ps.sem, s_ps.at(c.plus(-2)))
                    for e in range(4):
                        at = slice(HID * e, HID * (e + 1))
                        ins = nc.scalar.activation(
                            h_bd[at, c.m2, :, :, e, :].rearrange("p s g k -> p g s k"),
                            hidden[at, :, bass.ts(c.v, SC * SLOTS)].rearrange("p g (s k) -> p g s k", s=SC), ACT.Gelu)
                    ins.then_inc(act_sb.sem, 1)
            walk(act, step, first, last, lo, hi)

        @block.vector
        def _(dve):
            nc.vector.memset(slot_out[:, :, :, :, D:D + 1], 1.0).then_inc(zeroed, 1)

            def finish(c, h):
                if not c:
                    return
                dve.wait_ge(y_ps.sem, y_ps.at(c, 2 * h + 2))
                if c.plus(-2): dve.wait_ge(y_sb.sem, y_sb.at(c.plus(-2)))
                if c.plus(-2): dve.wait_ge(y_out.of(c.plus(-2)), y_out.at(c.plus(-2)))
                o = ps[:, 4 + h, 0:2 * (D + 1)].rearrange("p (a e) -> p a e", a=2)
                nc.vector.reciprocal(rden[:, c.m2, 2 * h:2 * h + 2], o[:, :, D]).then_inc(den.sem, 1)
                dve.wait_ge(den.sem, den.at(c, h + 1))
                for p in range(2):
                    q = 2 * h + p
                    ins = nc.vector.scalar_tensor_tensor(
                        out=y[:, c.m2, q], in0=o[:, p, 0:D], scalar=rden[:, c.m2, q:q + 1],
                        in1=x_all[:, bass.ds(c.v * PC + q, 1), :].rearrange("p a d -> p (a d)"), op0=ALU.mult, op1=ALU.add)
                ins.then_inc(y_sb.sem, 1)

            def step(t):
                for p in range(PC):
                    c = t.plus(1)
                    if c:
                        dve.wait_ge(s_ps.sem, s_ps.at(c, p + 1))
                        if c.plus(-2): dve.wait_ge(y_ps.sem, y_ps.at(c.plus(-2)))
                        nc.vector.tensor_tensor(slot_out[:, c.m2, 2 * p:2 * p + 2, :, 0:D],
                                                ps[:, p, :].rearrange("p (s a d) -> p s a d", s=2, a=2),
                                                w["b2"][:].rearrange("p (o a) d -> p o a d", o=1).to_broadcast([P, 2, 2, D]),
                                                ALU.add).then_inc(s_sb.sem, 1)
                    if p % 2:
                        finish(t.plus(0), p // 2)
            walk(dve, step, first, last, lo, hi)

        @block.tensor
        def _(pe):
            pe.wait_ge(zeroed, 2)

            def step(t):
                for p in range(PC):
                    c = t.plus(1)
                    if c:
                        if p == 0:
                            pe.wait_ge(act_sb.sem, act_sb.at(c))
                        if c.plus(-1): pe.wait_ge(s_sb.sem, s_sb.at(c.plus(-1), p + 1))
                        for s in range(2 * p, 2 * p + 2):
                            for g in range(4):
                                at = (s % 2) * 2 * D + (g // 2) * D
                                ins = nc.tensor.matmul(ps[64 * (g % 2):64 * (g % 2) + 64, p, at:at + D],
                                                       h_bd[:, c.m2, s, g].rearrange("p e k -> p (e k)"), w["w2"][:, g, :],
                                                       start=True, stop=True)
                        ins.then_inc(s_ps.sem, 1)
                    c = t.plus(0)
                    if c:
                        if p == 0:
                            pe.wait_ge(comb_in.of(c), comb_in.at(c))
                            pe.wait_ge(s_sb.sem, s_sb.at(c))
                        if p % 2 == 0:
                            if c.plus(-1): pe.wait_ge(y_sb.sem, y_sb.at(c.plus(-1), p // 2 + 1))
                        for r in range(2):
                            s = 2 * p + r
                            for h in range(2):
                                ins = nc.tensor.matmul(ps[N * r:N * (r + 1), 4 + p // 2, (p % 2) * (D + 1):(p % 2 + 1) * (D + 1)],
                                                       comb[:, c.m2, h, s * N:(s + 1) * N], slot_out[:, c.m2, s, h, :],
                                                       start=h == 0, stop=h == 1)
                        ins.then_inc(y_ps.sem, 1)
            walk(pe, step, first, last, lo, hi)


def build(nc, a, out):
    with ExitStack() as forever:
        ps = forever.enter_context(nc.psum_tensor("ps", [P, 8, TOK], F32))
        kit = Kit(nc, forever, forever)
        w = {}
        x1_dram = nc.dram_tensor("x1_scratch", [S, N, D], F32).ap()
        comb_dram = nc.dram_tensor("combine_scratch", [CHUNKS, P, 2 * TOK], F32).ap()
        prepare(nc, kit, ps, w, a)
        with ExitStack() as ctx:
            self_attention(nc, Kit(nc, forever, ctx), ps, w, a["x"], x1_dram)
        x_all = kit.sb("x_all", [P, S // 2, D])
        with ExitStack() as ctx:
            cross_attention(nc, Kit(nc, forever, ctx), ps, w, x1_dram, a["ctx_1024"], x_all)
        hidden = kit.sb("hidden", [P, 4, S * SLOTS])
        with ExitStack() as ctx:
            experts_in(nc, Kit(nc, forever, ctx), ps, w, x_all, hidden, comb_dram)
        with ExitStack() as ctx:
            experts_out(nc, Kit(nc, forever, ctx), ps, w, x_all, hidden, comb_dram, out)


_INS = ["x", "ctx_1024", "L0_attn_Wq", "L0_attn_Wk", "L0_xattn_Wq", "L0_xattn_bq", "L0_xattn_Wk", "L0_xattn_bk",
        "L0_xattn_Wv", "L0_xattn_bv", "L0_xattn_Wo", "L0_ffn_ln_gamma", "L0_ffn_ln_beta", "L0_ffn_mu", "L0_ffn_scale",
        "L0_ffn_w1", "L0_ffn_b1", "L0_ffn_w2", "L0_ffn_b2"]


def kernel(**inputs):
    import numpy as _np
    import concourse.bacc as _bacc
    from concourse import mybir as _mybir
    from concourse.bass_utils import run_bass_kernel_spmd as _run

    nc = _bacc.Bacc("TRN2", target_bir_lowering=False, num_devices=1)
    arrays, args = {}, {}
    for name in _INS:
        a = _np.ascontiguousarray(inputs[name])
        arrays[f"in_{name}"] = a
        args[name] = nc.dram_tensor(f"in_{name}", a.shape, _mybir.dt.from_np(a.dtype), kind="ExternalInput").ap()
    out = nc.dram_tensor("out_0", (S, N, D), F32, kind="ExternalOutput").ap()
    build(nc, args, out)
    r = _run(nc, [arrays], core_ids=[0])
    return r.results[0]["out_0"]
```

```python
from contextlib import ExitStack

import concourse.bass as bass
from concourse import mybir

F32 = mybir.dt.float32
BF16 = mybir.dt.bfloat16
ALU = mybir.AluOpType
ACT = mybir.ActivationFunctionType
AX_X = mybir.AxisListType.X

P = 128
S, N, D = 128, 64, 128
HEADS, HD = 16, 8
EXPERTS, SLOTS, HID = 16, 16, 32
ES = EXPERTS * SLOTS
LN_EPS, NORM_EPS = 1e-5, 1e-12
CHUNKS = 16
TOK = S * N // CHUNKS
BC = N // CHUNKS
SC = S // CHUNKS
PC = SC // 2


class Chunk:

    def __init__(self, i, k):
        self.i, self.k = i, k
        self.m4, self.m2 = k % 4, k % 2
        self.v = k if i is None else i * 4 + k
        self.round = k // 4 if i is None else i + k // 4

    def plus(self, j):
        if self.i is None and not 0 <= self.k + j < CHUNKS:
            return None
        return Chunk(self.i, self.k + j)


class Signal:

    def __init__(self, sem, per=1):
        self.sem, self.per = sem, per

    def at(self, c, k=None):
        return c.v * self.per + (self.per if k is None else k)


class Landings:

    def __init__(self, sems, per=1):
        self.sems, self.per = sems, per

    def of(self, c):
        return self.sems[c.m4]

    def at(self, c):
        return (c.round + 1) * (16 * self.per)


def walk(eng, step, first, last, lo, hi):
    hi = lo + (hi - lo) // 4 * 4
    for t in range(first, lo):
        step(Chunk(None, t))
    with eng.Fori(0, (hi - lo) // 4) as i:
        for r in range(4):
            step(Chunk(i, lo + r))
    for t in range(hi, last):
        step(Chunk(None, t))


class Kit:

    def __init__(self, nc, forever, ctx):
        self.nc, self.forever, self.ctx = nc, forever, ctx

    def sb(self, name, shape, dt=F32):
        return self.ctx.enter_context(self.nc.sbuf_tensor(name, shape, dt))

    def sem(self, name):
        return self.forever.enter_context(self.nc.semaphore(name))

    def landings(self, name, per=1):
        return Landings([self.sem(f"{name}{i}") for i in range(4)], per)

    def sig(self, name, per=1):
        return Signal(self.sem(name), per)


def self_attention(nc, kit, ps, w, x, x1_dram):
    x_sb = kit.sb("x_sb", [P, N, D])
    stats = kit.sb("a_stats", [P, 2, BC, 6])
    mv = kit.sb("a_mv", [P, 2, BC, 2])
    rstd = kit.sb("a_rstd", [P, 2, BC])
    xn = kit.sb("a_xn", [P, 4, BC, D + 1])
    xT = kit.sb("a_xT", [P, 2, TOK])
    yT = kit.sb("a_yT", [P, 2, TOK])
    th = kit.sb("a_th", [P, 2, TOK])
    pr = kit.sb("a_pr", [P, 2, TOK])
    rden = kit.sb("a_rden", [P, 2, BC])
    x1 = kit.sb("a_x1", [P, 2, BC, D])

    x_in = kit.landings("a_x_in")
    ones_set = kit.sem("a_ones_set")
    stat = kit.sig("a_stat", 2)
    rooted = kit.sig("a_rooted", 2)
    normed = kit.sig("a_normed")
    xT_ps, xT_sb = kit.sig("a_xT_ps"), kit.sig("a_xT_sb")
    y_ps, y_sb = kit.sig("a_y_ps"), kit.sig("a_y_sb")
    s_ps, th_sb, p_sb = kit.sig("a_s_ps"), kit.sig("a_th_sb"), kit.sig("a_p_sb")
    o_ps, den = kit.sig("a_o_ps"), kit.sig("a_den")
    x1_sb, x1_out = kit.sig("a_x1_sb"), kit.landings("a_x1_out")

    def o_bank(c):
        return 4 + 2 * c.m2

    first, last, lo, hi = -3, CHUNKS, 2, CHUNKS - 3

    with nc.Block() as block:
        @block.sync
        def _(sp):
            def step(t):
                c = t.plus(8)
                if c:
                    if c.plus(-4): sp.wait_ge(x_in.of(c.plus(-4)), x_in.at(c.plus(-4)))
                    sp.dma_start(x_sb[:, bass.ts(c.v, BC), :], x[:, bass.ts(c.v, BC), :]).then_inc(x_in.of(c), 16)
                c = t.plus(0)
                if c:
                    sp.wait_ge(x1_sb.sem, x1_sb.at(c))
                    sp.dma_start(x1_dram[:, bass.ts(c.v, BC), :], x1[:, c.m2]).then_inc(x1_out.of(c), 16)
            walk(sp, step, -8, CHUNKS, 0, CHUNKS - 8)
            for k in range(CHUNKS - 4, CHUNKS):
                sp.wait_ge(x1_out.of(Chunk(None, k)), x1_out.at(Chunk(None, k)))

        @block.gpsimd
        def _(pool):
            def step(t):
                c = t.plus(3)
                if c:
                    pool.wait_ge(stat.sem, stat.at(c))
                    if c.plus(-2): pool.wait_ge(normed.sem, normed.at(c.plus(-2)))
                    nc.gpsimd.tensor_tensor(rstd[:, c.m2, :], mv[:, c.m2, :, 1], w["ln_eps"][:], ALU.add).then_inc(rooted.sem, 1)
                    pool.wait_ge(rooted.sem, rooted.at(c, 1))
                    nc.gpsimd.tensor_tensor(rstd[:, c.m2, :], rstd[:, c.m2, :], w["neg_half"][:, 0:BC],
                                            ALU.pow).then_inc(rooted.sem, 1)
            walk(pool, step, first, last, lo, hi)

        @block.vector
        def _(dve):
            nc.vector.memset(xn[:, :, :, D:D + 1], 1.0).then_inc(ones_set, 1)

            def step(t):
                c = t.plus(3)
                if c:
                    dve.wait_ge(x_in.of(c), x_in.at(c))
                    if c.plus(-2): dve.wait_ge(stat.sem, stat.at(c.plus(-2)))
                    if c.plus(-2): dve.wait_ge(normed.sem, normed.at(c.plus(-2)))
                    if c.plus(-2): dve.wait_ge(rooted.sem, rooted.at(c.plus(-2)))
                    xc = x_sb[:, bass.ts(c.v, BC), :]
                    for b in range(BC):
                        ins = nc.vector.bn_stats(stats[:, c.m2, b, :], xc[:, b, :])
                    ins.then_inc(stat.sem, 1)
                c = t.plus(2)
                if c:
                    xc = x_sb[:, bass.ts(c.v, BC), :]
                    dve.wait_ge(rooted.sem, rooted.at(c))
                    if c.plus(-4): dve.wait_ge(o_ps.sem, o_ps.at(c.plus(-4)))
                    if c.plus(1): dve.wait_ge(stat.sem, stat.at(c.plus(1), 1))
                    for b in range(BC):
                        ins = nc.vector.tensor_scalar(xn[:, c.m4, b, 0:D], xc[:, b, :], mv[:, c.m2, b, 0:1],
                                                      rstd[:, c.m2, b:b + 1], ALU.subtract, ALU.mult)
                    ins.then_inc(normed.sem, 1)
                c = t.plus(3)
                if c:
                    if t.plus(2) is None:
                        dve.wait_ge(stat.sem, stat.at(c, 1))
                    for b in range(BC):
                        ins = nc.vector.bn_aggr(mv[:, c.m2, b, :], stats[:, c.m2, b, :])
                    ins.then_inc(stat.sem, 1)
                c = t.plus(0)
                if c:
                    dve.wait_ge(o_ps.sem, o_ps.at(c))
                    if c.plus(-2): dve.wait_ge(x1_sb.sem, x1_sb.at(c.plus(-2)))
                    o = ps[:, o_bank(c):o_bank(c) + 2, 0:2 * (D + 1)].rearrange("p a (b e) -> p a b e", b=2)
                    nc.vector.reciprocal(rden[:, c.m2, :].rearrange("p (a b) -> p a b", a=2),
                                         o[:, :, :, D]).then_inc(den.sem, 1)
                    dve.wait_ge(den.sem, den.at(c))
                    if c.plus(-2): dve.wait_ge(x1_out.of(c.plus(-2)), x1_out.at(c.plus(-2)))
                    for b in range(BC):
                        ins = nc.vector.scalar_tensor_tensor(
                            out=x1[:, c.m2, b, :], in0=o[:, b // 2, b % 2, 0:D], scalar=rden[:, c.m2, b:b + 1],
                            in1=x_sb[:, bass.ds(c.v * BC + b, 1), :].rearrange("p a d -> p (a d)"), op0=ALU.mult, op1=ALU.add)
                    ins.then_inc(x1_sb.sem, 1)
            walk(dve, step, first, last, lo, hi)

        @block.scalar
        def _(act):
            def step(t):
                c = t.plus(1)
                if c:
                    act.wait_ge(y_ps.sem, y_ps.at(c))
                    nc.scalar.activation(yT[:, c.m2, :], ps[:, 1, :], ACT.Copy).then_inc(y_sb.sem, 1)
                c = t.plus(2)
                if c:
                    act.wait_ge(xT_ps.sem, xT_ps.at(c))
                    if c.plus(-2): act.wait_ge(s_ps.sem, s_ps.at(c.plus(-2)))
                    nc.scalar.activation(xT[:, c.m2, :], ps[:, 0, :], ACT.Copy).then_inc(xT_sb.sem, 1)
                c = t.plus(1)
                if c:
                    act.wait_ge(s_ps.sem, s_ps.at(c))
                    nc.scalar.activation(th[:, c.m2, :], ps[:, 2 + c.m2, :], ACT.Tanh,
                                         scale=float(D) ** -0.5).then_inc(th_sb.sem, 1)
                    act.wait_ge(th_sb.sem, th_sb.at(c))
                    if c.plus(-2): act.wait_ge(o_ps.sem, o_ps.at(c.plus(-2)))
                    nc.scalar.activation(pr[:, c.m2, :], th[:, c.m2, :], ACT.Exp).then_inc(p_sb.sem, 1)
            walk(act, step, first, last, lo, hi)

        @block.tensor
        def _(pe):
            pe.wait_ge(ones_set, 1)

            def step(t):
                c = t.plus(1)
                if c:
                    pe.wait_ge(xT_sb.sem, xT_sb.at(c))
                    if c.plus(-1): pe.wait_ge(y_sb.sem, y_sb.at(c.plus(-1)))
                    nc.tensor.matmul(ps[:, 1, :], w["L"][:], xT[:, c.m2, :], start=True, stop=True).then_inc(y_ps.sem, 1)
                c = t.plus(0)
                if c:
                    pe.wait_ge(p_sb.sem, p_sb.at(c))
                    if c.plus(-2): pe.wait_ge(x1_sb.sem, x1_sb.at(c.plus(-2)))
                    for b in range(BC):
                        ins = nc.tensor.matmul(ps[:, o_bank(c) + b // 2, (b % 2) * (D + 1):(b % 2 + 1) * (D + 1)],
                                               pr[:, c.m2, b * P:(b + 1) * P], xn[:, c.m4, b, :],
                                               start=True, stop=True)
                    ins.then_inc(o_ps.sem, 1)
                c = t.plus(2)
                if c:
                    pe.wait_ge(normed.sem, normed.at(c))
                    if c.plus(-1): pe.wait_ge(xT_sb.sem, xT_sb.at(c.plus(-1)))
                    for b in range(BC):
                        ins = nc.tensor.transpose(ps[:, 0, b * P:(b + 1) * P], xn[:, c.m4, b, 0:D], w["ident"][:])
                    ins.then_inc(xT_ps.sem, 1)
                c = t.plus(1)
                if c:
                    pe.wait_ge(y_sb.sem, y_sb.at(c))
                    if c.plus(-2): pe.wait_ge(th_sb.sem, th_sb.at(c.plus(-2)))
                    for b in range(BC):
                        ins = nc.tensor.matmul(ps[:, 2 + c.m2, b * P:(b + 1) * P], xT[:, c.m2, b * P:(b + 1) * P],
                                               yT[:, c.m2, b * P:(b + 1) * P], start=True, stop=True)
                    ins.then_inc(s_ps.sem, 1)
            walk(pe, step, first, last, lo, hi)


def prepare(nc, kit, ps, w, a):
    for name, shape in (("ident", [P, P]), ("ones", [P, P]), ("half", [P, ES]), ("neg_half", [P, PC]), ("ln_eps", [P, PC]), ("L", [P, P]), ("wqT", [P, P]), ("wkT", [P, P]),
                        ("wvT", [P, P]), ("woT", [P, P]), ("bqk", [P, 2]), ("head_mask", [P, HEADS]), ("bv", [P, D]),
                        ("gamma", [P, D]), ("beta", [P, D]), ("mu", [P, ES]), ("scale", [P, 1]),
                        ("w1", [P, EXPERTS, HID]), ("b1", [P, 4]), ("w2", [P, 4, D]), ("b2", [P, 2, D])):
        w[name] = kit.sb("w_" + name, shape)
    with ExitStack() as ctx:
        tmp = Kit(nc, kit.forever, ctx)
        raw = {n: tmp.sb("raw_" + n, [P, P]) for n in ("aq", "ak", "q", "k", "v", "o")}
        wop = tmp.sb("raw_op", [P, P])
        by_d, bias = tmp.sb("by_d", [P, P]), tmp.sb("raw_bias", [P, 2])
        mu = tmp.sb("raw_mu", [P, ES])
        sq = tmp.sb("raw_sq", [P, ES])
        loaded, ident_made = kit.sem("w_loaded"), kit.sem("w_ident")
        dve_step, products, copied = kit.sem("w_dve"), kit.sem("w_products"), kit.sem("w_copied")
        rooted = kit.sem("w_rooted")

        loads = [(raw["aq"][:], a["L0_attn_Wq"]), (raw["ak"][:], a["L0_attn_Wk"]), (raw["q"][:], a["L0_xattn_Wq"]),
                 (raw["k"][:], a["L0_xattn_Wk"]), (raw["v"][:], a["L0_xattn_Wv"]), (raw["o"][:], a["L0_xattn_Wo"]),
                 (bias[:, 0:1], a["L0_xattn_bq"].rearrange("(p o) -> p o", o=1)),
                 (bias[:, 1:2], a["L0_xattn_bk"].rearrange("(p o) -> p o", o=1)),
                 (w["bv"][:], a["L0_xattn_bv"].rearrange("(o d) -> o d", o=1).to_broadcast([P, D])),
                 (w["gamma"][:], a["L0_ffn_ln_gamma"].rearrange("(o d) -> o d", o=1).to_broadcast([P, D])),
                 (w["beta"][:], a["L0_ffn_ln_beta"].rearrange("(o d) -> o d", o=1).to_broadcast([P, D])),
                 (w["scale"][:], a["L0_ffn_scale"].rearrange("(o d) -> o d", o=1).to_broadcast([P, 1])),
                 (mu[:], a["L0_ffn_mu"].rearrange("d e s -> d (e s)")),
                 (w["w1"][:], a["L0_ffn_w1"].rearrange("e d h -> d e h"))]
        for g in range(4):
            loads.append((w["b1"][:, g:g + 1], a["L0_ffn_b1"][4 * g:4 * g + 4, :].rearrange("c (h o) -> (c h) o", o=1)))
            loads.append((w["w2"][:, g, :], a["L0_ffn_w2"][4 * g:4 * g + 4].rearrange("c h d -> (c h) d")))
        for e in range(EXPERTS):
            loads.append((w["b2"][SLOTS * (e % 8):SLOTS * (e % 8 + 1), e // 8, :],
                          a["L0_ffn_b2"][e:e + 1, :].to_broadcast([SLOTS, D])))

        with nc.Block() as block:
            @block.sync
            def _(sp):
                for dst, src in loads:
                    sp.dma_start(dst, src).then_inc(loaded, 16)

            @block.gpsimd
            def _(pool):
                nc.gpsimd.memset(w["ident"][:], 0.0).then_inc(ident_made, 1)
                pool.wait_ge(ident_made, 1)
                nc.gpsimd.affine_select(out=w["ident"][:], in_=w["ident"][:], compare_op=ALU.not_equal, fill=1.0,
                                        base=0, pattern=[[-1, P]], channel_multiplier=1).then_inc(ident_made, 1)
                pool.wait_ge(dve_step, 9)
                nc.gpsimd.tensor_tensor(sq[:], sq[:], w["half"][:], ALU.pow).then_inc(rooted, 1)

            @block.vector
            def _(dve):
                nc.vector.memset(w["ones"][:], 1.0).then_inc(dve_step, 1)
                nc.vector.memset(w["half"][:], 0.5).then_inc(dve_step, 1)
                nc.vector.memset(w["neg_half"][:], -0.5).then_inc(dve_step, 1)
                nc.vector.memset(w["ln_eps"][:], LN_EPS).then_inc(dve_step, 1)
                dve.wait_ge(loaded, 16 * len(loads))
                nc.vector.tensor_copy(wop[:].rearrange("p (j g d) -> p j g d", j=2, g=8),
                                      raw["o"][:].rearrange("p (g j d) -> p j g d", g=8, j=2)).then_inc(dve_step, 1)
                nc.vector.tensor_tensor(sq[:], mu[:], mu[:], ALU.mult).then_inc(dve_step, 1)
                dve.wait_ge(ident_made, 2)
                nc.vector.tensor_copy(by_d[:].rearrange("p (d h) -> p d h", d=HD),
                                      w["ident"][:].rearrange("p (h d) -> p d h", d=HD)).then_inc(dve_step, 1)
                nc.vector.tensor_reduce(w["head_mask"][:], w["ident"][:].rearrange("p (d h) -> p h d", d=HD), AX_X, ALU.add).then_inc(dve_step, 1)
                dve.wait_ge(products, 2)
                nc.vector.tensor_copy(sq[:], ps[:, 1, 0:ES]).then_inc(dve_step, 1)
                dve.wait_ge(rooted, 1)
                nc.vector.tensor_scalar(sq[:], sq[:], NORM_EPS, None, ALU.max).then_inc(dve_step, 1)
                dve.wait_ge(dve_step, 10)
                nc.vector.reciprocal(sq[:], sq[:]).then_inc(dve_step, 1)
                dve.wait_ge(dve_step, 11)
                nc.vector.tensor_tensor(w["mu"][:], mu[:], sq[:], ALU.mult).then_inc(dve_step, 1)

            @block.tensor
            def _(pe):
                pe.wait_ge(loaded, 16 * len(loads))
                pe.wait_ge(ident_made, 2)
                pe.wait_ge(dve_step, 8)
                nc.tensor.matmul(ps[:, 0, 0:P], raw["aq"][:], raw["ak"][:], start=True, stop=True).then_inc(products, 1)
                nc.tensor.matmul(ps[:, 1, 0:ES], w["ones"][:], sq[:], start=True, stop=True).then_inc(products, 1)
                for i, n in enumerate(("q", "k", "v")):
                    nc.tensor.transpose(ps[:, 2 + i, 0:P], raw[n][:], w["ident"][:]).then_inc(products, 1)
                nc.tensor.transpose(ps[:, 5, 0:P], wop[:], w["ident"][:]).then_inc(products, 1)
                nc.tensor.matmul(ps[:, 6, 0:2], by_d[:], bias[:], start=True, stop=True).then_inc(products, 1)

            @block.scalar
            def _(act):
                for bank, n, k in ((0, "L", 1), (2, "wqT", 3), (3, "wkT", 4), (4, "wvT", 5), (5, "woT", 6)):
                    act.wait_ge(products, k)
                    if n in ("wqT", "wkT"):
                        nc.scalar.activation(w[n][:].rearrange("p (d h) -> p d h", d=HD),
                                             ps[:, bank, 0:P].rearrange("p (h d) -> p d h", d=HD), ACT.Copy).then_inc(copied, 1)
                    else:
                        nc.scalar.activation(w[n][:], ps[:, bank, 0:P], ACT.Copy).then_inc(copied, 1)
                act.wait_ge(products, 7)
                nc.scalar.activation(w["bqk"][:], ps[:, 6, 0:2], ACT.Copy).then_inc(copied, 1)


def cross_attention(nc, kit, ps, w, x1_dram, ctx_in, x_all):
    PRODUCTS = 6
    RUNS = ((0, 3), (3, 2), (5, 1))
    MROW = 2 * PRODUCTS * HD
    G = HEADS // 2
    HT = TOK // 2
    V1 = HD + 1
    LEAD = {"q": 2, "k": 0}
    LAST = {"q": 0, "k": 2}
    DVE_HEADS = 8

    ctx_sb = kit.sb("c_ctx", [P, 4, PC, D])
    stats = kit.sb("c_stats", [P, 2, PC, 6])
    mv = kit.sb("c_mv", [P, 2, PC, 2])
    rstd = kit.sb("c_rstd", [P, 2, PC])
    xn = kit.sb("c_xn", [P, 2, PC, D])
    xT = kit.sb("c_xT", [P, 2, TOK])
    cT = kit.sb("c_cT", [P, 4, TOK])
    full = {n: kit.sb(f"c_{n}32", [P, 2, TOK]) for n in "qk"}
    rest = {n: kit.sb(f"c_{n}rest", [P, TOK]) for n in "qk"}
    part = {n: kit.sb(f"c_{n}part", [P, 2, 3, TOK], BF16) for n in "qk"}
    part_dram = {n: nc.dram_tensor(f"{n}_parts", [CHUNKS, 3, P, TOK], BF16).ap() for n in "qk"}
    max_dram = nc.dram_tensor("maxima", [CHUNKS, PC * HEADS, P], BF16).ap()
    q_st = kit.sb("c_q_st", [P, 2, G, 2, TOK], BF16)
    k_st = kit.sb("c_k_st", [P, 2, G, TOK], BF16)
    k_bd = kit.sb("c_k_bd", [P, 2, HEADS, HT], BF16)
    mx = kit.sb("c_mx", [P, 2, HEADS, PC])
    negmax = kit.sb("c_negmax", [PC * HEADS, 2, P], BF16)
    prob = kit.sb("c_prob", [P, 2, HEADS * N])
    v_bd = kit.sb("c_v_bd", [P, 2, PC, HEADS, 2, V1])
    rden = kit.sb("c_rden", [P, 2, 4 * G])
    o_sb = kit.sb("c_o", [P, 2, PC, 2, G * HD])
    o_tok = kit.sb("c_o_tok", [P, 2, PC, D])
    oT = kit.sb("c_oT", [P, 2, TOK])

    zeroed = kit.sem("c_zeroed")
    x_in, ctx_in_s = kit.landings("c_x_in"), kit.landings("c_ctx_in")
    stat, rooted, normed = kit.sig("c_stat", 2), kit.sig("c_rooted", 2), kit.sig("c_normed")
    xT_ps, cT_ps, xcT_sb = kit.sig("c_xT_ps"), kit.sig("c_cT_ps"), kit.sig("c_xcT_sb", 2)
    q_ps, k_ps, v_ps = kit.sig("c_q_ps"), kit.sig("c_k_ps"), kit.sig("c_v_ps")
    qk_sb = kit.sig("c_qk_sb", 4)
    split = kit.sig("c_split", 6)
    parts_out = {n: kit.landings(f"c_{n}_out") for n in "qk"}
    filled = kit.landings("c_filled", 4 * len(RUNS))
    spread_dve, spread_act = kit.sig("c_spread_dve", 2), kit.sig("c_spread_act", 2)
    sc_ps, mx_sb = kit.sig("c_sc_ps", 4), kit.sig("c_mx_sb", 4)
    mT_ps, mT_sb = kit.sig("c_mT_ps"), kit.sig("c_mT_sb")
    max_out = kit.sig("c_max_out", 16)
    max_in = kit.landings("c_max_in", 2)
    st_ps, p_sb, o_ps = kit.sig("c_st_ps", 4), kit.sig("c_p_sb", 4), kit.sig("c_o_ps", 4)
    v_sb = kit.sig("c_v_sb")
    den, o_norm = kit.sig("c_den", 2), kit.sig("c_o_norm", 4)
    shuffled = kit.landings("c_shuffled", 4)
    oT_ps, oT_sb, wo_ps, x2_sb = kit.sig("c_oT_ps"), kit.sig("c_oT_sb"), kit.sig("c_wo_ps"), kit.sig("c_x2_sb")

    x1_v = x1_dram.rearrange("(c p r) n d -> c (r n) p d", p=PC, r=2)
    ctx_v = ctx_in.rearrange("(c p r) n d -> c (r n) p d", p=PC, r=2)
    first, last, lo, hi = -4, CHUNKS + 1, 3, CHUNKS - 4

    def dram(ap, c):
        return ap[bass.ds(c.v, 1)].rearrange("o a b d -> (o a) b d")

    def x_tok(c, p):
        return x_all[:, bass.ds(c.v * PC + p, 1), :].rearrange("p a d -> p (a d)")

    with nc.Block() as block:
        @block.sync
        def _(sp):
            def step(t):
                c = t.plus(8)
                if c:
                    if c.plus(-4): sp.wait_ge(x_in.of(c.plus(-4)), x_in.at(c.plus(-4)))
                    sp.dma_start(x_all[:, bass.ts(c.v, PC), :], dram(x1_v, c)).then_inc(x_in.of(c), 16)
                c = t.plus(6)
                if c:
                    if c.plus(-4): sp.wait_ge(cT_ps.sem, cT_ps.at(c.plus(-4)))
                    sp.dma_start(ctx_sb[:, c.m4], dram(ctx_v, c)).then_inc(ctx_in_s.of(c), 16)
                c = t.plus(1)
                if c:
                    sp.wait_ge(mT_sb.sem, mT_sb.at(c))
                    sp.dma_start(max_dram[bass.ds(c.v, 1)].rearrange("o a t -> (o a) t"), negmax[:, c.m2, :]).then_inc(max_out.sem, 16)
                c = t.plus(-1)
                if c:
                    if c.plus(-2): sp.wait_ge(oT_ps.sem, oT_ps.at(c.plus(-2)))
                    sp.wait_ge(o_norm.sem, o_norm.at(c))
                    for j in range(2):
                        for r in range(2):
                            sp.dma_start(o_tok[N * r:N * (r + 1), c.m2, :, G * HD * j:G * HD * (j + 1)],
                                         o_sb[N * j:N * (j + 1), c.m2, :, r, :]).then_inc(shuffled.of(c), 16)
                c = t.plus(2)
                if c:
                    for k, n in enumerate("qk"):
                        sp.wait_ge(split.sem, split.at(c, 3 * k + 3))
                        sp.dma_start(dram(part_dram[n], c).rearrange("a p t -> p a t"), part[n][:, c.m2]).then_inc(
                            parts_out[n].of(c), 16)
                c = t.plus(1)
                if c:
                    sp.wait_ge(max_out.sem, max_out.at(c))
                    for j in range(2):
                        src = max_dram[bass.ds(c.v, 1)].rearrange("o (g j p) t -> j o g (p t)", g=G, j=2)[j]
                        sp.dma_start(q_st[MROW + j:MROW + j + 1, c.m2, :, j, :], src).then_inc(max_in.of(c), 16)
                c = t.plus(2)
                if c:
                    if c.plus(-2): sp.wait_ge(st_ps.sem, st_ps.at(c.plus(-2)))
                    for n in "qk":
                        sp.wait_ge(parts_out[n].of(c), parts_out[n].at(c))
                        src = dram(part_dram[n], c)
                        for u, length in RUNS:
                            at = 3 - length if n == "q" else 0
                            for j in range(2):
                                row = j * PRODUCTS * HD + u * HD
                                dst = q_st[row:row + length * HD, c.m2, :, j, :] if n == "q" else k_st[row:row + length * HD, c.m2, :, :]
                                sp.dma_start(dst, src[at:at + length].rearrange("a (d g j) t -> j (a d) g t", d=HD, j=2)[j]).then_inc(
                                    filled.of(c), 16)
            walk(sp, step, -8, last, lo, CHUNKS - 8)

        @block.gpsimd
        def _(pool):
            nc.gpsimd.memset(q_st[:], 0.0).then_inc(zeroed, 1)

            def step(t):
                c = t.plus(4)
                if c:
                    pool.wait_ge(stat.sem, stat.at(c))
                    if c.plus(-2): pool.wait_ge(normed.sem, normed.at(c.plus(-2)))
                    nc.gpsimd.tensor_tensor(rstd[:, c.m2, :], mv[:, c.m2, :, 1], w["ln_eps"][:], ALU.add).then_inc(rooted.sem, 1)
                    pool.wait_ge(rooted.sem, rooted.at(c, 1))
                    nc.gpsimd.tensor_tensor(rstd[:, c.m2, :], rstd[:, c.m2, :], w["neg_half"][:, 0:PC],
                                            ALU.pow).then_inc(rooted.sem, 1)
                c = t.plus(3)
                if c:
                    for k, n in enumerate("qk"):
                        pool.wait_ge(qk_sb.sem, qk_sb.at(c, 2 * k + 2))
                        if c.plus(-2): pool.wait_ge(parts_out[n].of(c.plus(-2)), parts_out[n].at(c.plus(-2)))
                        if c.plus(-1): pool.wait_ge(split.sem, split.at(c.plus(-1), 3 * k + 3))
                        a, p, r = full[n][:, c.m2], part[n][:, c.m2], rest[n][:]
                        nc.gpsimd.tensor_tensor(p[:, 1], a, p[:, LEAD[n]], ALU.subtract).then_inc(split.sem, 1)
                        nc.gpsimd.tensor_tensor(r, a, p[:, LEAD[n]], ALU.subtract).then_inc(split.sem, 1)
                        pool.wait_ge(split.sem, split.at(c, 3 * k + 2))
                        nc.gpsimd.tensor_tensor(p[:, LAST[n]], r, p[:, 1], ALU.subtract).then_inc(split.sem, 1)
            walk(pool, step, first, last, lo, hi)

        @block.vector
        def _(dve):
            nc.vector.memset(k_st[MROW:MROW + 2], 1.0).then_inc(zeroed, 1)
            nc.vector.memset(v_bd[:], 0.0).then_inc(zeroed, 1)
            dve.wait_ge(zeroed, 3)
            for r in range(2):
                nc.vector.memset(v_bd[N * r:N * (r + 1), :, :, :, r, HD:V1], 1.0).then_inc(zeroed, 1)

            def spread(c, h):
                if not c:
                    return
                dve.wait_ge(qk_sb.sem, qk_sb.at(c))
                if c.plus(-1): dve.wait_ge(sc_ps.sem, sc_ps.at(c.plus(-1), 2 * h + 2))
                for head in range(DVE_HEADS):
                    ins = nc.vector.tensor_scalar(k_bd[:, h, head, :], part["k"][:, c.m2, 0, h * HT:(h + 1) * HT],
                                                  w["head_mask"][:, head:head + 1], None, ALU.mult)
                ins.then_inc(spread_dve.sem, 1)

            def row_max(c, p):
                if not c:
                    return
                if p == 0 and c.plus(-2): dve.wait_ge(mT_ps.sem, mT_ps.at(c.plus(-2)))
                dve.wait_ge(sc_ps.sem, sc_ps.at(c, p + 1))
                nc.vector.reduce_max(mx[:, c.m2, :, p],
                                     ps[:, 2:4, :].rearrange("p a (h m) -> p (a h) m", m=N), AX_X).then_inc(mx_sb.sem, 1)

            def normalise(c, h):
                if not c:
                    return
                if c.plus(-2): dve.wait_ge(shuffled.of(c.plus(-2)), shuffled.at(c.plus(-2)))
                dve.wait_ge(o_ps.sem, o_ps.at(c, 2 * h + 2))
                if c.plus(-1): dve.wait_ge(o_norm.sem, o_norm.at(c.plus(-1), 2 * h + 2))
                o = ps[:, 6 + h, 0:4 * G * V1].rearrange("p (a g r e) -> p a g r e", a=2, r=2, e=V1)
                nc.vector.reciprocal(rden[:, h], o[:, :, :, :, HD].rearrange("p a g r -> p (a g r)")).then_inc(den.sem, 1)
                dve.wait_ge(den.sem, den.at(c, h + 1))
                for p in range(2):
                    nc.vector.tensor_tensor(
                        o_sb[:, c.m2, 2 * h + p].rearrange("p r (g d) -> p g r d", g=G), o[:, p, :, :, 0:HD],
                        rden[:, h, 2 * G * p:2 * G * (p + 1)].rearrange("p (g r o) -> p g r o", r=2, o=1).to_broadcast([P, G, 2, HD]),
                        ALU.mult).then_inc(o_norm.sem, 1)

            def step(t):
                spread(t.plus(2), 1)
                normalise(t.plus(-1), 1)
                c = t.plus(4)
                if c:
                    dve.wait_ge(x_in.of(c), x_in.at(c))
                    if c.plus(-2): dve.wait_ge(stat.sem, stat.at(c.plus(-2)))
                    if c.plus(-2): dve.wait_ge(normed.sem, normed.at(c.plus(-2)))
                    for p in range(PC):
                        ins = nc.vector.bn_stats(stats[:, c.m2, p, :], x_tok(c, p))
                    ins.then_inc(stat.sem, 1)
                row_max(t.plus(2), 0)
                c = t.plus(1)
                if c:
                    if t.plus(4): dve.wait_ge(stat.sem, stat.at(t.plus(4), 1))
                    dve.wait_ge(v_ps.sem, v_ps.at(c))
                    if c.plus(-2): dve.wait_ge(o_ps.sem, o_ps.at(c.plus(-2)))
                    if c.i is None and c.k == 0: dve.wait_ge(zeroed, 5)
                    for r in range(2):
                        at = slice(N * r, N * (r + 1))
                        ins = nc.vector.tensor_tensor(
                            v_bd[at, c.m2, :, :, r, 0:HD], ps[at, 0, :].rearrange("p (a h d) -> p a h d", a=PC, d=HD),
                            w["bv"][at].rearrange("p (o h d) -> p o h d", o=1, d=HD).to_broadcast([N, PC, HEADS, HD]), ALU.add)
                    ins.then_inc(v_sb.sem, 1)
                c = t.plus(4)
                if c:
                    if not t.plus(1): dve.wait_ge(stat.sem, stat.at(c, 1))
                    for p in range(PC):
                        ins = nc.vector.bn_aggr(mv[:, c.m2, p, :], stats[:, c.m2, p, :])
                    ins.then_inc(stat.sem, 1)
                row_max(t.plus(2), 1)
                normalise(t.plus(0), 0)
                c = t.plus(4)
                if c:
                    dve.wait_ge(rooted.sem, rooted.at(c))
                    if c.plus(-2): dve.wait_ge(xT_ps.sem, xT_ps.at(c.plus(-2)))
                    for p in range(PC):
                        ins = nc.vector.tensor_scalar(xn[:, c.m2, p, :], x_tok(c, p), mv[:, c.m2, p, 0:1], rstd[:, c.m2, p:p + 1],
                                                      ALU.subtract, ALU.mult)
                    ins.then_inc(normed.sem, 1)
                row_max(t.plus(2), 2)
                spread(t.plus(3), 0)
                row_max(t.plus(2), 3)
                c = t.plus(-1)
                if c:
                    dve.wait_ge(wo_ps.sem, wo_ps.at(c))
                    nc.vector.tensor_tensor(x_all[:, bass.ts(c.v, PC), :], ps[:, 1, :].rearrange("p (a d) -> p a d", a=PC),
                                            x_all[:, bass.ts(c.v, PC), :], ALU.add).then_inc(x2_sb.sem, 1)
            walk(dve, step, first, last, lo, hi)

        @block.scalar
        def _(act):
            def exp(c, p):
                if not c:
                    return
                act.wait_ge(st_ps.sem, st_ps.at(c, p + 1))
                if p >= 2:
                    act.wait_ge(o_ps.sem, o_ps.at(c, p - 1))
                elif c.plus(-1):
                    act.wait_ge(o_ps.sem, o_ps.at(c.plus(-1), p + 3))
                nc.scalar.activation(prob[:, p % 2, :], ps[:, 4:6, :].rearrange("p a b -> p (a b)"), ACT.Exp,
                                     scale=float(HD) ** -0.5).then_inc(p_sb.sem, 1)

            def spread(c, h, head, to):
                if not c:
                    return
                if head == DVE_HEADS:
                    act.wait_ge(qk_sb.sem, qk_sb.at(c))
                    if c.plus(-1): act.wait_ge(sc_ps.sem, sc_ps.at(c.plus(-1), 2 * h + 2))
                for head in range(head, to):
                    ins = nc.scalar.activation(k_bd[:, h, head, :], part["k"][:, c.m2, 0, h * HT:(h + 1) * HT], ACT.Copy,
                                               scale=w["head_mask"][:, head:head + 1])
                if to == HEADS:
                    ins.then_inc(spread_act.sem, 1)

            def step(t):
                exp(t.plus(0), 0)
                c = t.plus(1)
                if c:
                    act.wait_ge(mT_ps.sem, mT_ps.at(c))
                    if c.plus(-2): act.wait_ge(max_out.sem, max_out.at(c.plus(-2)))
                    nc.scalar.activation(negmax[:, c.m2, :], ps[0:PC * HEADS, 0, 0:P], ACT.Copy, scale=-1.0).then_inc(mT_sb.sem, 1)
                c = t.plus(3)
                if c:
                    act.wait_ge(cT_ps.sem, cT_ps.at(c))
                    if c.plus(-4): act.wait_ge(v_ps.sem, v_ps.at(c.plus(-4)))
                    nc.scalar.activation(cT[:, c.m4, :], ps[:, 1, :], ACT.Copy).then_inc(xcT_sb.sem, 1)
                    act.wait_ge(xT_ps.sem, xT_ps.at(c))
                    if c.plus(-2): act.wait_ge(q_ps.sem, q_ps.at(c.plus(-2)))
                    nc.scalar.activation(xT[:, c.m2, :], ps[:, 0, :], ACT.Copy).then_inc(xcT_sb.sem, 1)
                exp(t.plus(0), 1)
                spread(t.plus(2), 1, DVE_HEADS, HEADS)
                c = t.plus(3)
                if c:
                    for k, (n, ready) in enumerate((("q", q_ps), ("k", k_ps))):
                        act.wait_ge(ready.sem, ready.at(c))
                        if c.plus(-2):
                            act.wait_ge(split.sem, split.at(c.plus(-2), 3 * k + 3))
                            act.wait_ge(parts_out[n].of(c.plus(-2)), parts_out[n].at(c.plus(-2)))
                            act.wait_ge(sc_ps.sem, sc_ps.at(c.plus(-2)))
                        nc.scalar.activation(full[n][:, c.m2, :], ps[:, k, :], ACT.Identity, bias=w["bqk"][:, k:k + 1]).then_inc(qk_sb.sem, 1)
                        nc.scalar.activation(part[n][:, c.m2, LEAD[n], :], ps[:, k, :], ACT.Identity, bias=w["bqk"][:, k:k + 1]).then_inc(qk_sb.sem, 1)
                        if k == 0:
                            exp(t.plus(0), 2)
                elif t.plus(0):
                    exp(t.plus(0), 2)
                c = t.plus(-1)
                if c:
                    act.wait_ge(oT_ps.sem, oT_ps.at(c))
                    if c.plus(-2): act.wait_ge(wo_ps.sem, wo_ps.at(c.plus(-2)))
                    nc.scalar.activation(oT[:, c.m2, :], ps[:, 1, :], ACT.Copy).then_inc(oT_sb.sem, 1)
                exp(t.plus(0), 3)
                spread(t.plus(3), 0, DVE_HEADS, HEADS)
            walk(act, step, first, last, lo, hi)

        @block.tensor
        def _(pe):
            pe.wait_ge(zeroed, 5)

            def scores(c, p):
                if not c:
                    return
                if p % 2 == 0:
                    pe.wait_ge(spread_dve.sem, spread_dve.at(c, p // 2 + 1))
                    pe.wait_ge(spread_act.sem, spread_act.at(c, p // 2 + 1))
                if p:
                    pe.wait_ge(mx_sb.sem, mx_sb.at(c, p))
                else:
                    pe.wait_ge(qk_sb.sem, qk_sb.at(c, 2))
                    if c.plus(-1): pe.wait_ge(mx_sb.sem, mx_sb.at(c.plus(-1)))
                for b in range(2):
                    for r in range(2):
                        at = slice((2 * p + r) * N, (2 * p + r + 1) * N)
                        of = (p % 2 * 2 + r) * N
                        ins = nc.tensor.matmul(ps[N * r:N * (r + 1), 2 + b, :].rearrange("p (h m) -> p h m", m=N),
                                               part["q"][:, c.m2, LEAD["q"], at],
                                               k_bd[:, p // 2, 8 * b:8 * b + 8, of:of + N], start=True, stop=True)
                ins.then_inc(sc_ps.sem, 1)

            def scores_T(c, p):
                if not c:
                    return
                if p:
                    pe.wait_ge(p_sb.sem, p_sb.at(c, p))
                else:
                    pe.wait_ge(filled.of(c), filled.at(c))
                    pe.wait_ge(max_in.of(c), max_in.at(c))
                    if c.plus(-1): pe.wait_ge(p_sb.sem, p_sb.at(c.plus(-1)))
                for g in range(G):
                    for r in range(2):
                        at = slice((2 * p + r) * N, (2 * p + r + 1) * N)
                        ins = nc.tensor.matmul(
                            ps[N * r:N * (r + 1), 4 + g // 4, (g % 4) * P:(g % 4 + 1) * P].rearrange("p (j n) -> p j n", j=2),
                            k_st[0:MROW + 2, c.m2, g, at], q_st[0:MROW + 2, c.m2, g, :, at], start=True, stop=True)
                ins.then_inc(st_ps.sem, 1)

            def values(c, p):
                if not c:
                    return
                pe.wait_ge(p_sb.sem, p_sb.at(c, p + 1))
                if p == 0:
                    pe.wait_ge(v_sb.sem, v_sb.at(c))
                if p % 2 == 0:
                    if c.plus(-1): pe.wait_ge(o_norm.sem, o_norm.at(c.plus(-1), p + 2))
                for g in range(G):
                    for j in range(2):
                        at = (p % 2) * 2 * G * V1 + g * 2 * V1
                        ins = nc.tensor.matmul(ps[N * j:N * (j + 1), 6 + p // 2, at:at + 2 * V1].rearrange("p (r e) -> p r e", r=2),
                                               prob[:, p % 2, (2 * g + j) * N:(2 * g + j + 1) * N],
                                               v_bd[:, c.m2, p, 2 * g + j], start=True, stop=True)
                ins.then_inc(o_ps.sem, 1)

            def step(t):
                scores_T(t.plus(0), 0)
                c = t.plus(1)
                if c:
                    pe.wait_ge(mx_sb.sem, mx_sb.at(c))
                    if c.plus(-1): pe.wait_ge(v_sb.sem, v_sb.at(c.plus(-1)))
                    elif c.plus(1): pe.wait_ge(qk_sb.sem, qk_sb.at(c.plus(1), 2))
                values(t.plus(-1), 3)
                if c:
                    nc.tensor.transpose(ps[0:PC * HEADS, 0, 0:P], mx[:, c.m2].rearrange("p h a -> p (h a)"), w["ident"][:]).then_inc(mT_ps.sem, 1)
                c = t.plus(3)
                if c:
                    pe.wait_ge(ctx_in_s.of(c), ctx_in_s.at(c))
                    if c.plus(-5): pe.wait_ge(x2_sb.sem, x2_sb.at(c.plus(-5)))
                    elif c.plus(-1): pe.wait_ge(qk_sb.sem, qk_sb.at(c.plus(-1)))
                    for p in range(PC):
                        ins = nc.tensor.transpose(ps[:, 1, p * P:(p + 1) * P], ctx_sb[:, c.m4, p, :], w["ident"][:])
                    ins.then_inc(cT_ps.sem, 1)
                    pe.wait_ge(normed.sem, normed.at(c))
                    if c.plus(-2): pe.wait_ge(mT_sb.sem, mT_sb.at(c.plus(-2)))
                    elif c.plus(-1): pe.wait_ge(qk_sb.sem, qk_sb.at(c.plus(-1), 2))
                    for p in range(PC):
                        ins = nc.tensor.transpose(ps[:, 0, p * P:(p + 1) * P], xn[:, c.m2, p, :], w["ident"][:])
                    ins.then_inc(xT_ps.sem, 1)
                scores(t.plus(2), 0)
                scores_T(t.plus(0), 1)
                values(t.plus(0), 0)
                c = t.plus(3)
                if c:
                    pe.wait_ge(xcT_sb.sem, xcT_sb.at(c))
                    nc.tensor.matmul(ps[:, 0, :], w["wqT"][:], xT[:, c.m2, :], start=True, stop=True).then_inc(q_ps.sem, 1)
                    nc.tensor.matmul(ps[:, 1, :], w["wkT"][:], cT[:, c.m4, :], start=True, stop=True).then_inc(k_ps.sem, 1)
                scores(t.plus(2), 1)
                scores_T(t.plus(0), 2)
                values(t.plus(0), 1)
                c = t.plus(1)
                if c:
                    if c.plus(2): pe.wait_ge(qk_sb.sem, qk_sb.at(c.plus(2), 2))
                    else: pe.wait_ge(mT_sb.sem, mT_sb.at(c))
                    for p in range(PC):
                        ins = nc.tensor.matmul(ps[:, 0, p * P:(p + 1) * P], cT[:, c.m4, p * P:(p + 1) * P], w["wvT"][:],
                                               start=True, stop=True)
                    ins.then_inc(v_ps.sem, 1)
                scores(t.plus(2), 2)
                c = t.plus(-1)
                if c:
                    pe.wait_ge(shuffled.of(c), shuffled.at(c))
                    if c.plus(4): pe.wait_ge(qk_sb.sem, qk_sb.at(c.plus(4)))
                    else: pe.wait_ge(x2_sb.sem, x2_sb.at(c.plus(-1)))
                    for p in range(PC):
                        ins = nc.tensor.transpose(ps[:, 1, p * P:(p + 1) * P], o_tok[:, c.m2, p, :], w["ident"][:])
                    ins.then_inc(oT_ps.sem, 1)
                scores_T(t.plus(0), 3)
                values(t.plus(0), 2)
                scores(t.plus(2), 3)
                c = t.plus(-1)
                if c:
                    pe.wait_ge(oT_sb.sem, oT_sb.at(c))
                    for p in range(PC):
                        ins = nc.tensor.matmul(ps[:, 1, p * P:(p + 1) * P], oT[:, c.m2, p * P:(p + 1) * P], w["woT"][:],
                                               start=True, stop=True)
                    ins.then_inc(wo_ps.sem, 1)
            walk(pe, step, first, last, lo, hi)


def experts_in(nc, kit, ps, w, x_all, hidden, comb_dram):
    stats = kit.sb("e_stats", [P, 2, PC, 6])
    mv = kit.sb("e_mv", [P, 2, PC, 2])
    rs = kit.sb("e_rs", [P, 2, PC])
    r1 = kit.sb("e_r1", [P, 2, PC])
    centred = kit.sb("e_centred", [P, 2, PC, D])
    xn = kit.sb("e_xn", [P, 4, PC, D])
    junk = kit.sb("e_junk", [P, PC, D])
    ss = kit.sb("e_ss", [P, 2, PC])
    sq = kit.sb("e_sq", [P, 2, PC])
    rn = kit.sb("e_rn", [P, 2, PC])
    xu = kit.sb("e_xu", [P, 2, PC, D])
    xuT = kit.sb("e_xuT", [P, 2, TOK])
    cm = kit.sb("e_cm", [P, 2, 2, SC])
    rm = kit.sb("e_rm", [P, 2, PC])
    neg_cm = kit.sb("e_neg_cm", [SC, 2, ES], BF16)
    neg_rm = kit.sb("e_neg_rm", [PC, 2, PC, P], BF16)
    sel32, sel = kit.sb("e_sel32", [SC, PC, P]), kit.sb("e_sel", [SC, PC, P], BF16)
    neg_diag = kit.sb("e_neg_diag", [PC, PC, P])
    ones4 = kit.sb("e_ones4", [PC, P], BF16)
    disp = kit.sb("e_disp", [P, 2, PC, ES])
    comb = kit.sb("e_comb", [P, 2, 2, TOK])
    slot_in = kit.sb("e_slot_in", [P, 2, SC, ES])
    rden = kit.sb("e_rden", [P, 2, 4, PC, 2, SLOTS])
    scaled = kit.sb("e_scaled", [P, 2, 4, SC * SLOTS])

    cleared, selected, ready = kit.sem("e_cleared"), kit.sem("e_selected"), kit.sem("e_ready")
    stat, root, normed = kit.sig("e_stat", 2), kit.sig("e_root", 7), kit.sig("e_normed", 2)
    squared, clamped, unit, xu_sb = kit.sig("e_squared"), kit.sig("e_clamped"), kit.sig("e_unit", 2), kit.sig("e_xu_sb")
    xuT_ps, xuT_sb = kit.sig("e_xuT_ps"), kit.sig("e_xuT_sb")
    lT_ps, lA_ps, max_sb = kit.sig("e_lT_ps"), kit.sig("e_lA_ps"), kit.sig("e_max_sb", 2)
    mT_ps, ncm_sb, nrm_sb = kit.sig("e_mT_ps"), kit.sig("e_ncm_sb"), kit.sig("e_nrm_sb")
    shA_ps, shT_ps, disp_sb, comb_sb = kit.sig("e_shA_ps"), kit.sig("e_shT_ps"), kit.sig("e_disp_sb"), kit.sig("e_comb_sb")
    in_ps, in_sb = kit.sig("e_in_ps", 2), kit.sig("e_in_sb", 2)
    den_ps, rden_sb, h_ps, h_sb, biased = kit.sig("e_den_ps"), kit.sig("e_rden_sb"), kit.sig("e_h_ps"), kit.sig("e_h_sb"), kit.sig("e_biased")
    comb_out = kit.landings("e_comb_out")
    first, last, lo, hi = -4, CHUNKS, 4, CHUNKS - 4

    def tok(c, p):
        return x_all[:, bass.ds(c.v * PC + p, 1), :].rearrange("p a d -> p (a d)")

    with nc.Block() as block:
        @block.sync
        def _(sp):
            def step(c):
                sp.wait_ge(comb_sb.sem, comb_sb.at(c))
                sp.dma_start(comb_dram[bass.ds(c.v, 1)].rearrange("o p t -> (o p) t"),
                             comb[:, c.m2].rearrange("p a t -> p (a t)")).then_inc(comb_out.of(c), 16)
            walk(sp, step, 0, CHUNKS, 4, CHUNKS)
            for k in range(CHUNKS - 4, CHUNKS):
                sp.wait_ge(comb_out.of(Chunk(None, k)), comb_out.at(Chunk(None, k)))

        @block.gpsimd
        def _(pool):
            nc.gpsimd.memset(sel32[:], 0.0).then_inc(cleared, 1)
            nc.gpsimd.memset(neg_diag[:], 0.0).then_inc(cleared, 1)
            pool.wait_ge(cleared, 2)
            nc.gpsimd.affine_select(out=sel32[:].rearrange("s p (r n) -> s p r n", r=2), in_=sel32[:].rearrange("s p (r n) -> s p r n", r=2),
                                    compare_op=ALU.not_equal, fill=1.0, base=0, pattern=[[-2, PC], [-1, 2], [0, N]],
                                    channel_multiplier=1).then_inc(selected, 1)
            nc.gpsimd.affine_select(out=neg_diag[:], in_=neg_diag[:], compare_op=ALU.not_equal, fill=-1.0, base=0,
                                    pattern=[[-1, PC], [0, P]], channel_multiplier=1).then_inc(selected, 1)

            def step(t):
                c = t.plus(4)
                if c:
                    pool.wait_ge(stat.sem, stat.at(c))
                    if c.plus(-2): pool.wait_ge(normed.sem, normed.at(c.plus(-2)))
                    v, a, b, half, eps = mv[:, c.m2, :, 1], r1[:, c.m2], rs[:, c.m2], w["neg_half"][:, 0:PC], w["ln_eps"][:]
                    for k, args in enumerate(((a, v, eps, ALU.add), (a, a, half, ALU.pow), (b, a, a, ALU.mult), (b, b, v, ALU.mult),
                                              (b, b, eps, ALU.add), (b, b, half, ALU.pow), (b, b, a, ALU.mult))):
                        if k:
                            pool.wait_ge(root.sem, root.at(c, k))
                        nc.gpsimd.tensor_tensor(*args).then_inc(root.sem, 1)
                c = t.plus(3)
                if c:
                    pool.wait_ge(clamped.sem, clamped.at(c))
                    if c.plus(-2): pool.wait_ge(xu_sb.sem, xu_sb.at(c.plus(-2)))
                    nc.gpsimd.tensor_tensor(rn[:, c.m2], sq[:, c.m2], w["neg_half"][:, 0:PC], ALU.pow).then_inc(unit.sem, 1)
                    pool.wait_ge(unit.sem, unit.at(c, 1))
                    nc.gpsimd.tensor_tensor(rn[:, c.m2], rn[:, c.m2], w["scale"][:].to_broadcast([P, PC]),
                                            ALU.mult).then_inc(unit.sem, 1)
                c = t.plus(0)
                if c:
                    pool.wait_ge(h_sb.sem, h_sb.at(c))
                    nc.gpsimd.tensor_tensor(hidden[:, :, bass.ts(c.v, SC * SLOTS)], scaled[:, c.m2],
                                            w["b1"][:].rearrange("p (g o) -> p g o", o=1).to_broadcast([P, 4, SC * SLOTS]),
                                            ALU.add).then_inc(biased.sem, 1)
            walk(pool, step, first, last, lo, hi)

        @block.vector
        def _(dve):
            nc.vector.memset(ones4[:], 1.0).then_inc(ready, 1)
            dve.wait_ge(selected, 2)
            nc.vector.tensor_copy(sel[:], sel32[:]).then_inc(ready, 1)

            def step(t):
                c = t.plus(4)
                if c:
                    if c.plus(-2): dve.wait_ge(stat.sem, stat.at(c.plus(-2)))
                    if c.plus(-2): dve.wait_ge(normed.sem, normed.at(c.plus(-2)))
                    for p in range(PC):
                        ins = nc.vector.bn_stats(stats[:, c.m2, p, :], tok(c, p))
                    ins.then_inc(stat.sem, 1)
                c = t.plus(3)
                if c:
                    dve.wait_ge(root.sem, root.at(c))
                    if c.plus(-2): dve.wait_ge(normed.sem, normed.at(c.plus(-2)))
                    if c.plus(-4): dve.wait_ge(in_ps.sem, in_ps.at(c.plus(-4)))
                    if c.plus(1): dve.wait_ge(stat.sem, stat.at(c.plus(1), 1))
                    if c.plus(-4): dve.wait_ge(xu_sb.sem, xu_sb.at(c.plus(-4)))
                    for p in range(PC):
                        ins = nc.vector.scalar_tensor_tensor(out=centred[:, c.m2, p], in0=tok(c, p), scalar=mv[:, c.m2, p, 0:1],
                                                             in1=w["gamma"][:], op0=ALU.subtract, op1=ALU.mult)
                    ins.then_inc(normed.sem, 1)
                c = t.plus(4)
                if c:
                    if not t.plus(3):
                        dve.wait_ge(stat.sem, stat.at(c, 1))
                    for p in range(PC):
                        ins = nc.vector.bn_aggr(mv[:, c.m2, p, :], stats[:, c.m2, p, :])
                    ins.then_inc(stat.sem, 1)
                c = t.plus(3)
                if c:
                    dve.wait_ge(normed.sem, normed.at(c, 1))
                    for p in range(PC):
                        ins = nc.vector.scalar_tensor_tensor(out=xn[:, c.m4, p], in0=centred[:, c.m2, p], scalar=rs[:, c.m2, p:p + 1],
                                                             in1=w["beta"][:], op0=ALU.mult, op1=ALU.add)
                    ins.then_inc(normed.sem, 1)
                c = t.plus(1)
                if c:
                    if c.plus(-2): dve.wait_ge(mT_ps.sem, mT_ps.at(c.plus(-2)))
                    dve.wait_ge(lT_ps.sem, lT_ps.at(c))
                    nc.vector.reduce_max(cm[:, c.m2].rearrange("p a s -> p (a s)"),
                                         ps[:, 3:5, :].rearrange("p a (s n) -> p (a s) n", n=N), AX_X).then_inc(max_sb.sem, 1)
                    dve.wait_ge(lA_ps.sem, lA_ps.at(c))
                    nc.vector.reduce_max(rm[:, c.m2], ps[:, 1:3, :].rearrange("p a (b e) -> p (a b) e", e=ES), AX_X).then_inc(max_sb.sem, 1)
                c = t.plus(3)
                if c:
                    dve.wait_ge(squared.sem, squared.at(c))
                    if c.plus(-2): dve.wait_ge(unit.sem, unit.at(c.plus(-2)))
                    nc.vector.tensor_scalar(sq[:, c.m2], ss[:, c.m2], NORM_EPS ** 2, None, ALU.max).then_inc(clamped.sem, 1)
                c = t.plus(1)
                if c:
                    dve.wait_ge(mT_ps.sem, mT_ps.at(c))
                    if c.plus(-2): dve.wait_ge(shT_ps.sem, shT_ps.at(c.plus(-2)))
                    nc.vector.tensor_tensor(neg_rm[:, c.m2], ps[0:PC, 5, 2 * P:3 * P].rearrange("q (o t) -> q o t", o=1).to_broadcast([PC, PC, P]),
                                            neg_diag[:], ALU.mult).then_inc(nrm_sb.sem, 1)
                c = t.plus(3)
                if c:
                    dve.wait_ge(unit.sem, unit.at(c))
                    if c.plus(-2): dve.wait_ge(xuT_ps.sem, xuT_ps.at(c.plus(-2)))
                    for p in range(PC):
                        ins = nc.vector.tensor_scalar(xu[:, c.m2, p], xn[:, c.m4, p], rn[:, c.m2, p:p + 1], None, ALU.mult)
                    ins.then_inc(xu_sb.sem, 1)
                c = t.plus(0)
                if c:
                    dve.wait_ge(den_ps.sem, den_ps.at(c))
                    if c.plus(-2): dve.wait_ge(h_sb.sem, h_sb.at(c.plus(-2)))
                    for r, bank in enumerate((0, 5)):
                        ins = nc.vector.reciprocal(rden[:, c.m2, :, :, r], ps[:, bank, 0:TOK // 2].rearrange("p (g a k) -> p g a k", g=4, a=PC))
                    ins.then_inc(rden_sb.sem, 1)
                    dve.wait_ge(rden_sb.sem, rden_sb.at(c))
                    dve.wait_ge(h_ps.sem, h_ps.at(c))
                    if c.plus(-2): dve.wait_ge(biased.sem, biased.at(c.plus(-2)))
                    nc.vector.tensor_tensor(scaled[:, c.m2], ps[:, 6, :].rearrange("p (g k) -> p g k", g=4),
                                            rden[:, c.m2].rearrange("p g a r k -> p g (a r k)"), ALU.mult).then_inc(h_sb.sem, 1)
            walk(dve, step, first, last, lo, hi)

        @block.scalar
        def _(act):
            def slots(c, h):
                if not c:
                    return
                act.wait_ge(in_ps.sem, in_ps.at(c, h + 1))
                if c.plus(-2): act.wait_ge(h_ps.sem, h_ps.at(c.plus(-2)))
                nc.scalar.activation(slot_in[:, c.m2, 4 * h:4 * h + 4].rearrange("p (a r) e -> p r a e", r=2),
                                     ps[:, 6:8, :].rearrange("p r (a e) -> p r a e", a=2), ACT.Copy).then_inc(in_sb.sem, 1)

            def step(t):
                slots(t.plus(0), 0)
                c = t.plus(3)
                if c:
                    act.wait_ge(normed.sem, normed.at(c))
                    if c.plus(-2): act.wait_ge(clamped.sem, clamped.at(c.plus(-2)))
                    if c.plus(-1): act.wait_ge(squared.sem, squared.at(c.plus(-1)))
                    for p in range(PC):
                        ins = nc.scalar.activation(junk[:, p], xn[:, c.m4, p], ACT.Square, accum_out=ss[:, c.m2, p:p + 1])
                    ins.then_inc(squared.sem, 1)
                slots(t.plus(0), 1)
                c = t.plus(1)
                if c:
                    act.wait_ge(mT_ps.sem, mT_ps.at(c))
                    if c.plus(-2): act.wait_ge(shA_ps.sem, shA_ps.at(c.plus(-2)))
                    act.wait_ge(nrm_sb.sem, nrm_sb.at(c))
                    nc.scalar.activation(neg_cm[:, c.m2], ps[0:SC, 5, 0:ES], ACT.Copy, scale=-1.0).then_inc(ncm_sb.sem, 1)
                    act.wait_ge(shA_ps.sem, shA_ps.at(c))
                    if c.plus(-2): act.wait_ge(in_ps.sem, in_ps.at(c.plus(-2)))
                    if c.plus(-2): act.wait_ge(den_ps.sem, den_ps.at(c.plus(-2)))
                    nc.scalar.activation(disp[:, c.m2].rearrange("p a e -> p (a e)"), ps[:, 1:3, :].rearrange("p a b -> p (a b)"),
                                         ACT.Exp).then_inc(disp_sb.sem, 1)
                    act.wait_ge(shT_ps.sem, shT_ps.at(c))
                    if c.plus(-2): act.wait_ge(comb_out.of(c.plus(-2)), comb_out.at(c.plus(-2)))
                    nc.scalar.activation(comb[:, c.m2].rearrange("p a e -> p (a e)"), ps[:, 3:5, :].rearrange("p a b -> p (a b)"),
                                         ACT.Exp).then_inc(comb_sb.sem, 1)
                c = t.plus(2)
                if c:
                    act.wait_ge(xuT_ps.sem, xuT_ps.at(c))
                    if c.plus(-2): act.wait_ge(lA_ps.sem, lA_ps.at(c.plus(-2)))
                    nc.scalar.activation(xuT[:, c.m2], ps[:, 0, :], ACT.Copy).then_inc(xuT_sb.sem, 1)
            walk(act, step, first, last, lo, hi)

        @block.tensor
        def _(pe):
            pe.wait_ge(ready, 2)

            def gather(c, h):
                if not c:
                    return
                pe.wait_ge(disp_sb.sem, disp_sb.at(c))
                if h:
                    pe.wait_ge(in_sb.sem, in_sb.at(c, 1))
                else:
                    if c.plus(-1): pe.wait_ge(in_sb.sem, in_sb.at(c.plus(-1)))
                    if c.plus(-1): pe.wait_ge(h_sb.sem, h_sb.at(c.plus(-1)))
                for a in range(2):
                    for r in range(2):
                        p, at = 2 * h + a, slice(N * r, N * (r + 1))
                        ins = nc.tensor.matmul(ps[:, 6 + r, a * ES:(a + 1) * ES], xn[at, c.m4, p, :], disp[at, c.m2, p, :],
                                               start=True, stop=True)
                ins.then_inc(in_ps.sem, 1)

            def step(t):
                gather(t.plus(0), 0)
                c = t.plus(1)
                if c:
                    pe.wait_ge(xuT_sb.sem, xuT_sb.at(c))
                    if c.plus(-1): pe.wait_ge(comb_sb.sem, comb_sb.at(c.plus(-1)))
                    for h in range(2):
                        ins = nc.tensor.matmul(ps[:, 3 + h, :], w["mu"][:, h * P:(h + 1) * P], xuT[:, c.m2, :],
                                               start=True, stop=False, skip_group_check=True)
                    ins.then_inc(lT_ps.sem, 1)
                    if c.plus(-1): pe.wait_ge(disp_sb.sem, disp_sb.at(c.plus(-1)))
                    for p in range(PC):
                        ins = nc.tensor.matmul(ps[:, 1 + p // 2, p % 2 * ES:(p % 2 + 1) * ES], xuT[:, c.m2, p * P:(p + 1) * P],
                                               w["mu"][:], start=p % 2 == 0, stop=False, skip_group_check=True)
                    ins.then_inc(lA_ps.sem, 1)
                gather(t.plus(0), 1)
                c = t.plus(1)
                if c:
                    pe.wait_ge(max_sb.sem, max_sb.at(c))
                    if c.plus(-2): pe.wait_ge(rden_sb.sem, rden_sb.at(c.plus(-2)))
                    for h in range(2):
                        nc.tensor.transpose(ps[0:SC, 5, h * P:(h + 1) * P], cm[:, c.m2, h, :], w["ident"][:])
                    nc.tensor.transpose(ps[0:PC, 5, 2 * P:3 * P], rm[:, c.m2, :], w["ident"][:]).then_inc(mT_ps.sem, 1)
                    pe.wait_ge(nrm_sb.sem, nrm_sb.at(c))
                    pe.wait_ge(ncm_sb.sem, ncm_sb.at(c))
                    for p in range(PC):
                        ins = nc.tensor.matmul(ps[:, 1 + p // 2, p % 2 * ES:(p % 2 + 1) * ES], sel[:, p, :], neg_cm[:, c.m2],
                                               start=False, stop=True, skip_group_check=True)
                    ins.then_inc(shA_ps.sem, 1)
                    for h in range(2):
                        ins = nc.tensor.matmul(ps[:, 3 + h, :], ones4[:], neg_rm[:, c.m2].rearrange("q a t -> q (a t)"),
                                               start=False, stop=True, skip_group_check=True)
                    ins.then_inc(shT_ps.sem, 1)
                c = t.plus(0)
                if c:
                    for r, bank in enumerate((0, 5)):
                        at = slice(N * r, N * (r + 1))
                        for p in range(PC):
                            for e in range(4):
                                ins = nc.tensor.matmul(
                                    ps[HID * e:HID * (e + 1), bank, 0:TOK // 2].rearrange("p (g a k) -> p g a k", g=4, a=PC)[:, :, p, :],
                                    w["ones"][at, 0:HID],
                                    disp[at, c.m2, p, :].rearrange("p (g e k) -> p g e k", g=4, e=4)[:, :, e, :],
                                    start=True, stop=True)
                    ins.then_inc(den_ps.sem, 1)
                    pe.wait_ge(in_sb.sem, in_sb.at(c))
                    for g in range(4):
                        for e in range(4):
                            x = 4 * g + e
                            ins = nc.tensor.matmul(ps[HID * e:HID * (e + 1), 6, g * P:(g + 1) * P].rearrange("p (s k) -> p s k", s=SC),
                                                   w["w1"][:, x, :], slot_in[:, c.m2, :, x * SLOTS:(x + 1) * SLOTS],
                                                   start=True, stop=True)
                    ins.then_inc(h_ps.sem, 1)
                c = t.plus(2)
                if c:
                    pe.wait_ge(xu_sb.sem, xu_sb.at(c))
                    if c.plus(-2): pe.wait_ge(rden_sb.sem, rden_sb.at(c.plus(-2)))
                    for p in range(PC):
                        ins = nc.tensor.transpose(ps[:, 0, p * P:(p + 1) * P], xu[:, c.m2, p, :], w["ident"][:])
                    ins.then_inc(xuT_ps.sem, 1)
            walk(pe, step, first, last, lo, hi)


def experts_out(nc, kit, ps, w, x_all, hidden, comb_dram, out):
    h_bd = kit.sb("o_h_bd", [P, 2, SC, 4, 4, SLOTS])
    slot_out = kit.sb("o_slot_out", [P, 2, SC, 2, D + 1])
    comb = kit.sb("o_comb", [P, 2, 2, TOK])
    rden = kit.sb("o_rden", [P, 2, PC])
    y = kit.sb("o_y", [P, 2, PC, D])

    zeroed = kit.sem("o_zeroed")
    act_sb = kit.sig("o_act_sb")
    s_ps, s_sb = kit.sig("o_s_ps", 4), kit.sig("o_s_sb", 4)
    comb_in = kit.landings("o_comb_in")
    y_ps, den, y_sb = kit.sig("o_y_ps", 4), kit.sig("o_den", 2), kit.sig("o_y_sb", 2)
    y_out = kit.landings("o_y_out")
    out_v = out.rearrange("(c p r) n d -> c (r n) p d", p=PC, r=2)
    first, last, lo, hi = -2, CHUNKS, 2, CHUNKS - 2

    with nc.Block() as block:
        @block.gpsimd
        def _(pool):
            nc.gpsimd.memset(h_bd[:], 0.0).then_inc(zeroed, 1)

        @block.sync
        def _(sp):
            def step(t):
                c = t.plus(2)
                if c:
                    if c.plus(-2): sp.wait_ge(y_ps.sem, y_ps.at(c.plus(-2)))
                    sp.dma_start(comb[:, c.m2].rearrange("p a t -> p (a t)"),
                                 comb_dram[bass.ds(c.v, 1)].rearrange("o p t -> (o p) t")).then_inc(comb_in.of(c), 16)
                c = t.plus(0)
                if c:
                    sp.wait_ge(y_sb.sem, y_sb.at(c))
                    sp.dma_start(out_v[bass.ds(c.v, 1)].rearrange("o a b d -> (o a) b d"), y[:, c.m2]).then_inc(y_out.of(c), 16)
            walk(sp, step, first, last, lo, hi)
            for k in range(CHUNKS - 4, CHUNKS):
                sp.wait_ge(y_out.of(Chunk(None, k)), y_out.at(Chunk(None, k)))

        @block.scalar
        def _(act):
            act.wait_ge(zeroed, 2)

            def step(t):
                c = t.plus(2)
                if c:
                    if c.plus(-2): act.wait_ge(s_ps.sem, s_ps.at(c.plus(-2)))
                    for e in range(4):
                        at = slice(HID * e, HID * (e + 1))
                        ins = nc.scalar.activation(
                            h_bd[at, c.m2, :, :, e, :].rearrange("p s g k -> p g s k"),
                            hidden[at, :, bass.ts(c.v, SC * SLOTS)].rearrange("p g (s k) -> p g s k", s=SC), ACT.Gelu)
                    ins.then_inc(act_sb.sem, 1)
            walk(act, step, first, last, lo, hi)

        @block.vector
        def _(dve):
            nc.vector.memset(slot_out[:, :, :, :, D:D + 1], 1.0).then_inc(zeroed, 1)

            def finish(c, h):
                if not c:
                    return
                dve.wait_ge(y_ps.sem, y_ps.at(c, 2 * h + 2))
                if c.plus(-2): dve.wait_ge(y_sb.sem, y_sb.at(c.plus(-2)))
                if c.plus(-2): dve.wait_ge(y_out.of(c.plus(-2)), y_out.at(c.plus(-2)))
                o = ps[:, 4 + h, 0:2 * (D + 1)].rearrange("p (a e) -> p a e", a=2)
                nc.vector.reciprocal(rden[:, c.m2, 2 * h:2 * h + 2], o[:, :, D]).then_inc(den.sem, 1)
                dve.wait_ge(den.sem, den.at(c, h + 1))
                for p in range(2):
                    q = 2 * h + p
                    ins = nc.vector.scalar_tensor_tensor(
                        out=y[:, c.m2, q], in0=o[:, p, 0:D], scalar=rden[:, c.m2, q:q + 1],
                        in1=x_all[:, bass.ds(c.v * PC + q, 1), :].rearrange("p a d -> p (a d)"), op0=ALU.mult, op1=ALU.add)
                ins.then_inc(y_sb.sem, 1)

            def step(t):
                for p in range(PC):
                    c = t.plus(1)
                    if c:
                        dve.wait_ge(s_ps.sem, s_ps.at(c, p + 1))
                        if c.plus(-2): dve.wait_ge(y_ps.sem, y_ps.at(c.plus(-2)))
                        nc.vector.tensor_tensor(slot_out[:, c.m2, 2 * p:2 * p + 2, :, 0:D],
                                                ps[:, p, :].rearrange("p (s a d) -> p s a d", s=2, a=2),
                                                w["b2"][:].rearrange("p (o a) d -> p o a d", o=1).to_broadcast([P, 2, 2, D]),
                                                ALU.add).then_inc(s_sb.sem, 1)
                    if p % 2:
                        finish(t.plus(0), p // 2)
            walk(dve, step, first, last, lo, hi)

        @block.tensor
        def _(pe):
            pe.wait_ge(zeroed, 2)

            def step(t):
                for p in range(PC):
                    c = t.plus(1)
                    if c:
                        if p == 0:
                            pe.wait_ge(act_sb.sem, act_sb.at(c))
                        if c.plus(-1): pe.wait_ge(s_sb.sem, s_sb.at(c.plus(-1), p + 1))
                        for s in range(2 * p, 2 * p + 2):
                            for g in range(4):
                                at = (s % 2) * 2 * D + (g // 2) * D
                                ins = nc.tensor.matmul(ps[64 * (g % 2):64 * (g % 2) + 64, p, at:at + D],
                                                       h_bd[:, c.m2, s, g].rearrange("p e k -> p (e k)"), w["w2"][:, g, :],
                                                       start=True, stop=True)
                        ins.then_inc(s_ps.sem, 1)
                    c = t.plus(0)
                    if c:
                        if p == 0:
                            pe.wait_ge(comb_in.of(c), comb_in.at(c))
                            pe.wait_ge(s_sb.sem, s_sb.at(c))
                        if p % 2 == 0:
                            if c.plus(-1): pe.wait_ge(y_sb.sem, y_sb.at(c.plus(-1), p // 2 + 1))
                        for r in range(2):
                            s = 2 * p + r
                            for h in range(2):
                                ins = nc.tensor.matmul(ps[N * r:N * (r + 1), 4 + p // 2, (p % 2) * (D + 1):(p % 2 + 1) * (D + 1)],
                                                       comb[:, c.m2, h, s * N:(s + 1) * N], slot_out[:, c.m2, s, h, :],
                                                       start=h == 0, stop=h == 1)
                        ins.then_inc(y_ps.sem, 1)
            walk(pe, step, first, last, lo, hi)


def build(nc, a, out):
    with ExitStack() as forever:
        ps = forever.enter_context(nc.psum_tensor("ps", [P, 8, TOK], F32))
        kit = Kit(nc, forever, forever)
        w = {}
        x1_dram = nc.dram_tensor("x1_scratch", [S, N, D], F32).ap()
        comb_dram = nc.dram_tensor("combine_scratch", [CHUNKS, P, 2 * TOK], F32).ap()
        prepare(nc, kit, ps, w, a)
        with ExitStack() as ctx:
            self_attention(nc, Kit(nc, forever, ctx), ps, w, a["x"], x1_dram)
        x_all = kit.sb("x_all", [P, S // 2, D])
        with ExitStack() as ctx:
            cross_attention(nc, Kit(nc, forever, ctx), ps, w, x1_dram, a["ctx_1024"], x_all)
        hidden = kit.sb("hidden", [P, 4, S * SLOTS])
        with ExitStack() as ctx:
            experts_in(nc, Kit(nc, forever, ctx), ps, w, x_all, hidden, comb_dram)
        with ExitStack() as ctx:
            experts_out(nc, Kit(nc, forever, ctx), ps, w, x_all, hidden, comb_dram, out)


_INS = ["x", "ctx_1024", "L0_attn_Wq", "L0_attn_Wk", "L0_xattn_Wq", "L0_xattn_bq", "L0_xattn_Wk", "L0_xattn_bk",
        "L0_xattn_Wv", "L0_xattn_bv", "L0_xattn_Wo", "L0_ffn_ln_gamma", "L0_ffn_ln_beta", "L0_ffn_mu", "L0_ffn_scale",
        "L0_ffn_w1", "L0_ffn_b1", "L0_ffn_w2", "L0_ffn_b2"]


def kernel(**inputs):
    import numpy as _np
    import concourse.bacc as _bacc
    from concourse import mybir as _mybir
    from concourse.bass_utils import run_bass_kernel_spmd as _run

    nc = _bacc.Bacc("TRN2", target_bir_lowering=False, num_devices=1)
    arrays, args = {}, {}
    for name in _INS:
        a = _np.ascontiguousarray(inputs[name])
        arrays[f"in_{name}"] = a
        args[name] = nc.dram_tensor(f"in_{name}", a.shape, _mybir.dt.from_np(a.dtype), kind="ExternalInput").ap()
    out = nc.dram_tensor("out_0", (S, N, D), F32, kind="ExternalOutput").ap()
    build(nc, args, out)
    r = _run(nc, [arrays], core_ids=[0])
    return r.results[0]["out_0"]
```

```python
from contextlib import ExitStack

import concourse.bass as bass
from concourse import mybir

F32 = mybir.dt.float32
BF16 = mybir.dt.bfloat16
ALU = mybir.AluOpType
ACT = mybir.ActivationFunctionType
AX_X = mybir.AxisListType.X

P = 128
S, N, D = 128, 64, 128
HEADS, HD = 16, 8
EXPERTS, SLOTS, HID = 16, 16, 32
ES = EXPERTS * SLOTS
LN_EPS, NORM_EPS = 1e-5, 1e-12
CHUNKS = 16
TOK = S * N // CHUNKS
BC = N // CHUNKS
SC = S // CHUNKS
PC = SC // 2


class Chunk:

    def __init__(self, i, k):
        self.i, self.k = i, k
        self.m4, self.m2 = k % 4, k % 2
        self.v = k if i is None else i * 4 + k
        self.round = k // 4 if i is None else i + k // 4

    def plus(self, j):
        if self.i is None and not 0 <= self.k + j < CHUNKS:
            return None
        return Chunk(self.i, self.k + j)


class Signal:

    def __init__(self, sem, per=1):
        self.sem, self.per = sem, per

    def at(self, c, k=None):
        return c.v * self.per + (self.per if k is None else k)


class Landings:

    def __init__(self, sems, per=1):
        self.sems, self.per = sems, per

    def of(self, c):
        return self.sems[c.m4]

    def at(self, c):
        return (c.round + 1) * (16 * self.per)


class Before:

    def __init__(self, biased, disp_sb, cleared):
        self.biased, self.disp_sb, self.cleared = biased, disp_sb, cleared


def walk(eng, step, first, last, lo, hi):
    hi = lo + (hi - lo) // 4 * 4
    for t in range(first, lo):
        step(Chunk(None, t))
    with eng.Fori(0, (hi - lo) // 4) as i:
        for r in range(4):
            step(Chunk(i, lo + r))
    for t in range(hi, last):
        step(Chunk(None, t))


class Kit:

    def __init__(self, nc, forever, ctx):
        self.nc, self.forever, self.ctx = nc, forever, ctx

    def sb(self, name, shape, dt=F32):
        return self.ctx.enter_context(self.nc.sbuf_tensor(name, shape, dt))

    def sem(self, name):
        return self.forever.enter_context(self.nc.semaphore(name))

    def landings(self, name, per=1):
        return Landings([self.sem(f"{name}{i}") for i in range(4)], per)

    def sig(self, name, per=1):
        return Signal(self.sem(name), per)


def self_attention(nc, kit, ps, w, a, x1_dram):
    x = a["x"]
    x_sb = kit.sb("x_sb", [P, N, D])
    stats = kit.sb("a_stats", [P, 2, BC, 6])
    mv = kit.sb("a_mv", [P, 2, BC, 2])
    rstd = kit.sb("a_rstd", [P, 2, BC])
    xn = kit.sb("a_xn", [P, 4, BC, D + 1])
    xT = kit.sb("a_xT", [P, 2, TOK])
    yT = kit.sb("a_yT", [P, 2, TOK])
    th = kit.sb("a_th", [P, 2, TOK])
    pr = kit.sb("a_pr", [P, 2, TOK])
    rden = kit.sb("a_rden", [P, 2, BC])
    x1 = kit.sb("a_x1", [P, 2, BC, D])

    x_in = kit.landings("a_x_in")
    ones_set = kit.sem("a_ones_set")
    stat = kit.sig("a_stat", 2)
    rooted = kit.sig("a_rooted", 2)
    normed = kit.sig("a_normed")
    xT_ps, xT_sb = kit.sig("a_xT_ps"), kit.sig("a_xT_sb")
    y_ps, y_sb = kit.sig("a_y_ps"), kit.sig("a_y_sb")
    s_ps, th_sb, p_sb = kit.sig("a_s_ps"), kit.sig("a_th_sb"), kit.sig("a_p_sb")
    o_ps, den = kit.sig("a_o_ps"), kit.sig("a_den")
    x1_sb, x1_out = kit.sig("a_x1_sb"), kit.landings("a_x1_out")

    raw = {n: kit.sb("raw_" + n, [P, P]) for n in ("aq", "ak", "q", "k", "v", "o", "op", "by_d")}
    raw.update(bias=kit.sb("raw_bias", [P, 2]), mu=kit.sb("raw_mu", [P, ES]), sq=kit.sb("raw_sq", [P, ES]),
               norm=kit.sb("raw_norm", [P, 2]), diag=kit.sb("raw_diag", [P, 2, P]))
    loads = weight_loads(raw, w, a)
    l_loaded, loaded, ident_made, constants = kit.sem("w_l_loaded"), kit.sem("w_loaded"), kit.sem("w_ident"), kit.sem("w_constants")
    l_ps, l_sb, formed, rooted_w = kit.sem("w_l_ps"), kit.sem("w_l_sb"), kit.sem("w_formed"), kit.sem("w_rooted")
    norms, turned, spread_ps, w_sb = kit.sem("w_norms"), kit.sem("w_turned"), kit.sem("w_spread_ps"), kit.sem("w_sb")

    def o_bank(c):
        return 4 + 2 * c.m2

    first, last, lo, hi = -3, CHUNKS, 2, CHUNKS - 3

    with nc.Block() as block:
        @block.sync
        def _(sp):
            sp.dma_start(raw["aq"][:], a["L0_attn_Wq"]).then_inc(l_loaded, 16)
            sp.dma_start(raw["ak"][:], a["L0_attn_Wk"]).then_inc(l_loaded, 16)

            def step(t):
                c = t.plus(8)
                if c:
                    if c.plus(-4): sp.wait_ge(x_in.of(c.plus(-4)), x_in.at(c.plus(-4)))
                    sp.dma_start(x_sb[:, bass.ts(c.v, BC), :], x[:, bass.ts(c.v, BC), :]).then_inc(x_in.of(c), 16)
                if t.i is None and t.k == -1:
                    for dst, src in loads:
                        sp.dma_start(dst, src).then_inc(loaded, 16)
                c = t.plus(0)
                if c:
                    sp.wait_ge(x1_sb.sem, x1_sb.at(c))
                    sp.dma_start(x1_dram[:, bass.ts(c.v, BC), :], x1[:, c.m2]).then_inc(x1_out.of(c), 16)
            walk(sp, step, -8, CHUNKS, 0, CHUNKS - 8)
            for k in range(CHUNKS - 4, CHUNKS):
                sp.wait_ge(x1_out.of(Chunk(None, k)), x1_out.at(Chunk(None, k)))

        @block.gpsimd
        def _(pool):
            nc.gpsimd.memset(w["ident"][:], 0.0).then_inc(ident_made, 1)
            pool.wait_ge(ident_made, 1)
            nc.gpsimd.affine_select(out=w["ident"][:], in_=w["ident"][:], compare_op=ALU.not_equal, fill=1.0,
                                    base=0, pattern=[[-1, P]], channel_multiplier=1).then_inc(ident_made, 1)
            pool.wait_ge(constants, 4)

            def step(t):
                c = t.plus(3)
                if c:
                    pool.wait_ge(stat.sem, stat.at(c))
                    if c.plus(-2): pool.wait_ge(normed.sem, normed.at(c.plus(-2)))
                    nc.gpsimd.tensor_tensor(rstd[:, c.m2, :], mv[:, c.m2, :, 1], w["ln_eps"][:], ALU.add).then_inc(rooted.sem, 1)
                    pool.wait_ge(rooted.sem, rooted.at(c, 1))
                    nc.gpsimd.tensor_tensor(rstd[:, c.m2, :], rstd[:, c.m2, :], w["neg_half"][:, 0:BC],
                                            ALU.pow).then_inc(rooted.sem, 1)
            walk(pool, step, first, last, lo, hi)
            pool.wait_ge(formed, 5)
            nc.gpsimd.tensor_tensor(raw["norm"][:], raw["norm"][:], w["half"][:], ALU.pow).then_inc(rooted_w, 1)

        @block.vector
        def _(dve):
            nc.vector.memset(xn[:, :, :, D:D + 1], 1.0).then_inc(ones_set, 1)
            nc.vector.memset(w["neg_half"][:], -0.5).then_inc(constants, 1)
            nc.vector.memset(w["ln_eps"][:], LN_EPS).then_inc(constants, 1)
            nc.vector.memset(w["half"][:], 0.5).then_inc(constants, 1)
            nc.vector.memset(w["ones"][:], 1.0).then_inc(constants, 1)

            def step(t):
                c = t.plus(3)
                if c:
                    dve.wait_ge(x_in.of(c), x_in.at(c))
                    if c.plus(-2): dve.wait_ge(stat.sem, stat.at(c.plus(-2)))
                    if c.plus(-2): dve.wait_ge(normed.sem, normed.at(c.plus(-2)))
                    if c.plus(-2): dve.wait_ge(rooted.sem, rooted.at(c.plus(-2)))
                    xc = x_sb[:, bass.ts(c.v, BC), :]
                    for b in range(BC):
                        ins = nc.vector.bn_stats(stats[:, c.m2, b, :], xc[:, b, :])
                    ins.then_inc(stat.sem, 1)
                c = t.plus(2)
                if c:
                    xc = x_sb[:, bass.ts(c.v, BC), :]
                    dve.wait_ge(rooted.sem, rooted.at(c))
                    if c.plus(-4): dve.wait_ge(o_ps.sem, o_ps.at(c.plus(-4)))
                    if c.plus(1): dve.wait_ge(stat.sem, stat.at(c.plus(1), 1))
                    for b in range(BC):
                        ins = nc.vector.tensor_scalar(xn[:, c.m4, b, 0:D], xc[:, b, :], mv[:, c.m2, b, 0:1],
                                                      rstd[:, c.m2, b:b + 1], ALU.subtract, ALU.mult)
                    ins.then_inc(normed.sem, 1)
                c = t.plus(3)
                if c:
                    if t.plus(2) is None:
                        dve.wait_ge(stat.sem, stat.at(c, 1))
                    for b in range(BC):
                        ins = nc.vector.bn_aggr(mv[:, c.m2, b, :], stats[:, c.m2, b, :])
                    ins.then_inc(stat.sem, 1)
                c = t.plus(0)
                if c:
                    dve.wait_ge(o_ps.sem, o_ps.at(c))
                    if c.plus(-2): dve.wait_ge(x1_sb.sem, x1_sb.at(c.plus(-2)))
                    o = ps[:, o_bank(c):o_bank(c) + 2, 0:2 * (D + 1)].rearrange("p a (b e) -> p a b e", b=2)
                    nc.vector.reciprocal(rden[:, c.m2, :].rearrange("p (a b) -> p a b", a=2),
                                         o[:, :, :, D]).then_inc(den.sem, 1)
                    dve.wait_ge(den.sem, den.at(c))
                    if c.plus(-2): dve.wait_ge(x1_out.of(c.plus(-2)), x1_out.at(c.plus(-2)))
                    for b in range(BC):
                        ins = nc.vector.scalar_tensor_tensor(
                            out=x1[:, c.m2, b, :], in0=o[:, b // 2, b % 2, 0:D], scalar=rden[:, c.m2, b:b + 1],
                            in1=x_sb[:, bass.ds(c.v * BC + b, 1), :].rearrange("p a d -> p (a d)"), op0=ALU.mult, op1=ALU.add)
                    ins.then_inc(x1_sb.sem, 1)
            walk(dve, step, first, last, lo, hi)
            dve.wait_ge(loaded, 16 * len(loads))
            dve.wait_ge(ident_made, 2)
            nc.vector.tensor_tensor(raw["sq"][:], raw["mu"][:], raw["mu"][:], ALU.mult).then_inc(formed, 1)
            nc.vector.tensor_copy(raw["by_d"][:].rearrange("p (d h) -> p d h", d=HD),
                                  w["ident"][:].rearrange("p (h d) -> p d h", d=HD)).then_inc(formed, 1)
            nc.vector.tensor_copy(raw["op"][:].rearrange("p (j g d) -> p j g d", j=2, g=8),
                                  raw["o"][:].rearrange("p (g j d) -> p j g d", g=8, j=2)).then_inc(formed, 1)
            nc.vector.tensor_reduce(w["head_mask"][:], w["ident"][:].rearrange("p (d h) -> p h d", d=HD), AX_X, ALU.add).then_inc(formed, 1)
            dve.wait_ge(norms, 2)
            nc.vector.tensor_copy(raw["norm"][:], ps[:, 2, 0:2]).then_inc(formed, 1)
            dve.wait_ge(rooted_w, 1)
            nc.vector.tensor_scalar(raw["norm"][:], raw["norm"][:], NORM_EPS, None, ALU.max).then_inc(formed, 1)
            dve.wait_ge(formed, 6)
            nc.vector.reciprocal(raw["norm"][:], raw["norm"][:]).then_inc(formed, 1)
            dve.wait_ge(formed, 7)
            for h in range(2):
                nc.vector.tensor_scalar(raw["diag"][:, h, :], w["ident"][:], raw["norm"][:, h:h + 1], None, ALU.mult).then_inc(formed, 1)
            dve.wait_ge(spread_ps, 1)
            nc.vector.tensor_tensor(w["mu"][:], raw["mu"][:], ps[:, 3, 0:ES], ALU.mult).then_inc(formed, 1)

        @block.scalar
        def _(act):
            act.wait_ge(l_ps, 1)
            nc.scalar.activation(w["L"][:], ps[:, 6, 0:P], ACT.Copy).then_inc(l_sb, 1)

            def step(t):
                c = t.plus(1)
                if c:
                    act.wait_ge(y_ps.sem, y_ps.at(c))
                    nc.scalar.activation(yT[:, c.m2, :], ps[:, 1, :], ACT.Copy).then_inc(y_sb.sem, 1)
                c = t.plus(2)
                if c:
                    act.wait_ge(xT_ps.sem, xT_ps.at(c))
                    if c.plus(-2): act.wait_ge(s_ps.sem, s_ps.at(c.plus(-2)))
                    nc.scalar.activation(xT[:, c.m2, :], ps[:, 0, :], ACT.Copy).then_inc(xT_sb.sem, 1)
                c = t.plus(1)
                if c:
                    act.wait_ge(s_ps.sem, s_ps.at(c))
                    nc.scalar.activation(th[:, c.m2, :], ps[:, 2 + c.m2, :], ACT.Tanh,
                                         scale=float(D) ** -0.5).then_inc(th_sb.sem, 1)
                    act.wait_ge(th_sb.sem, th_sb.at(c))
                    if c.plus(-2): act.wait_ge(o_ps.sem, o_ps.at(c.plus(-2)))
                    nc.scalar.activation(pr[:, c.m2, :], th[:, c.m2, :], ACT.Exp).then_inc(p_sb.sem, 1)
            walk(act, step, first, last, lo, hi)
            act.wait_ge(turned, 1)
            for i, n in enumerate(("wqT", "wkT", "wvT", "woT")):
                dst, src = w[n][:], ps[:, 0, i * P:(i + 1) * P]
                if i < 2:
                    dst, src = dst.rearrange("p (d h) -> p d h", d=HD), src.rearrange("p (h d) -> p d h", d=HD)
                nc.scalar.activation(dst, src, ACT.Copy).then_inc(w_sb, 1)
            nc.scalar.activation(w["bqk"][:], ps[:, 1, 0:2], ACT.Copy).then_inc(w_sb, 1)

        @block.tensor
        def _(pe):
            pe.wait_ge(l_loaded, 32)
            nc.tensor.matmul(ps[:, 6, 0:P], raw["aq"][:], raw["ak"][:], start=True, stop=True).then_inc(l_ps, 1)
            pe.wait_ge(ones_set, 1)
            pe.wait_ge(ident_made, 2)
            pe.wait_ge(l_sb, 1)

            def step(t):
                c = t.plus(1)
                if c:
                    pe.wait_ge(xT_sb.sem, xT_sb.at(c))
                    if c.plus(-1): pe.wait_ge(y_sb.sem, y_sb.at(c.plus(-1)))
                    nc.tensor.matmul(ps[:, 1, :], w["L"][:], xT[:, c.m2, :], start=True, stop=True).then_inc(y_ps.sem, 1)
                c = t.plus(0)
                if c:
                    pe.wait_ge(p_sb.sem, p_sb.at(c))
                    if c.plus(-2): pe.wait_ge(x1_sb.sem, x1_sb.at(c.plus(-2)))
                    for b in range(BC):
                        ins = nc.tensor.matmul(ps[:, o_bank(c) + b // 2, (b % 2) * (D + 1):(b % 2 + 1) * (D + 1)],
                                               pr[:, c.m2, b * P:(b + 1) * P], xn[:, c.m4, b, :],
                                               start=True, stop=True)
                    ins.then_inc(o_ps.sem, 1)
                c = t.plus(2)
                if c:
                    pe.wait_ge(normed.sem, normed.at(c))
                    if c.plus(-1): pe.wait_ge(xT_sb.sem, xT_sb.at(c.plus(-1)))
                    for b in range(BC):
                        ins = nc.tensor.transpose(ps[:, 0, b * P:(b + 1) * P], xn[:, c.m4, b, 0:D], w["ident"][:])
                    ins.then_inc(xT_ps.sem, 1)
                c = t.plus(1)
                if c:
                    pe.wait_ge(y_sb.sem, y_sb.at(c))
                    if c.plus(-2): pe.wait_ge(th_sb.sem, th_sb.at(c.plus(-2)))
                    for b in range(BC):
                        ins = nc.tensor.matmul(ps[:, 2 + c.m2, b * P:(b + 1) * P], xT[:, c.m2, b * P:(b + 1) * P],
                                               yT[:, c.m2, b * P:(b + 1) * P], start=True, stop=True)
                    ins.then_inc(s_ps.sem, 1)
            walk(pe, step, first, last, lo, hi)
            end = Chunk(None, CHUNKS - 1)
            pe.wait_ge(loaded, 16 * len(loads))
            pe.wait_ge(formed, 3)
            pe.wait_ge(th_sb.sem, th_sb.at(end))
            for h in range(2):
                nc.tensor.matmul(ps[:, 2, h:h + 1], raw["sq"][:, h * P:(h + 1) * P], w["ones"][:, 0:1], start=True, stop=True).then_inc(norms, 1)
            nc.tensor.matmul(ps[:, 1, 0:2], raw["by_d"][:], raw["bias"][:], start=True, stop=True)
            for i, n in enumerate(("q", "k", "v", "op")):
                ins = nc.tensor.transpose(ps[:, 0, i * P:(i + 1) * P], raw[n][:], w["ident"][:])
            ins.then_inc(turned, 1)
            pe.wait_ge(formed, 9)
            nc.tensor.matmul(ps[:, 3, 0:ES], w["ones"][:], raw["diag"][:].rearrange("p h q -> p (h q)"), start=True, stop=True).then_inc(spread_ps, 1)


def weight_tiles(kit, w):
    for name, shape in (("ident", [P, P]), ("ones", [P, P]), ("half", [P, 2]), ("neg_half", [P, PC]), ("ln_eps", [P, PC]),
                        ("L", [P, P]), ("wqT", [P, P]), ("wkT", [P, P]), ("wvT", [P, P]), ("woT", [P, P]), ("bqk", [P, 2]),
                        ("head_mask", [P, HEADS]), ("bv", [P, D]), ("gamma", [P, D]), ("beta", [P, D]), ("mu", [P, ES]),
                        ("scale", [P, 1]), ("w1", [P, EXPERTS, HID]), ("b1", [P, 4]), ("w2", [P, 4, D]), ("b2", [P, 2, D])):
        w[name] = kit.sb("w_" + name, shape)


def weight_loads(raw, w, a):
    def rows(name):
        return a[name].rearrange("(o d) -> o d", o=1)

    loads = [(raw[n][:], a[f"L0_xattn_W{n}"]) for n in "qkvo"]
    loads += [(raw["bias"][:, i:i + 1], a[f"L0_xattn_b{n}"].rearrange("(p o) -> p o", o=1)) for i, n in enumerate("qk")]
    loads += [(w["bv"][:], rows("L0_xattn_bv").to_broadcast([P, D])),
              (w["gamma"][:], rows("L0_ffn_ln_gamma").to_broadcast([P, D])),
              (w["beta"][:], rows("L0_ffn_ln_beta").to_broadcast([P, D])),
              (w["scale"][:], rows("L0_ffn_scale").to_broadcast([P, 1])),
              (raw["mu"][:], a["L0_ffn_mu"].rearrange("d e s -> d (e s)")),
              (w["w1"][:], a["L0_ffn_w1"].rearrange("e d h -> d e h"))]
    for g in range(4):
        loads.append((w["b1"][:, g:g + 1], a["L0_ffn_b1"][4 * g:4 * g + 4, :].rearrange("c (h o) -> (c h) o", o=1)))
        loads.append((w["w2"][:, g, :], a["L0_ffn_w2"][4 * g:4 * g + 4].rearrange("c h d -> (c h) d")))
    for e in range(EXPERTS):
        loads.append((w["b2"][SLOTS * (e % 8):SLOTS * (e % 8 + 1), e // 8, :],
                      a["L0_ffn_b2"][e:e + 1, :].to_broadcast([SLOTS, D])))
    return loads


def cross_attention(nc, kit, ps, w, x1_dram, ctx_in, x_all):
    PRODUCTS = 6
    RUNS = ((0, 3), (3, 2), (5, 1))
    MROW = 2 * PRODUCTS * HD
    G = HEADS // 2
    HT = TOK // 2
    V1 = HD + 1
    ONES_BF16 = 1 + 0x3F80 / 2 ** 23
    LEAD = {"q": 2, "k": 0}
    LAST = {"q": 0, "k": 2}
    DVE_HEADS = 11

    ctx_sb = kit.sb("c_ctx", [P, 4, PC, D])
    stats = kit.sb("c_stats", [P, 2, PC, 6])
    mv = kit.sb("c_mv", [P, 2, PC, 2])
    rstd = kit.sb("c_rstd", [P, 2, PC])
    xn = kit.sb("c_xn", [P, 2, PC, D])
    xT = kit.sb("c_xT", [P, 2, TOK])
    cT = kit.sb("c_cT", [P, 4, TOK])
    full = {n: kit.sb(f"c_{n}32", [P, 2, TOK]) for n in "qk"}
    rest = {n: kit.sb(f"c_{n}rest", [P, TOK]) for n in "qk"}
    part = {n: kit.sb(f"c_{n}part", [P, 2, 3, TOK], BF16) for n in "qk"}
    part_dram = {n: nc.dram_tensor(f"{n}_parts", [CHUNKS, 3, P, TOK], BF16).ap() for n in "qk"}
    max_dram = nc.dram_tensor("maxima", [CHUNKS, PC * HEADS, P], BF16).ap()
    q_st = kit.sb("c_q_st", [P, 2, G, 2, TOK], BF16)
    k_st = kit.sb("c_k_st", [P, 2, G, TOK], BF16)
    k_bd = kit.sb("c_k_bd", [P, 2, HEADS, HT], BF16)
    mx = kit.sb("c_mx", [P, 2, HEADS, PC])
    negmax = kit.sb("c_negmax", [PC * HEADS, 2, P], BF16)
    prob = kit.sb("c_prob", [P, 2, HEADS * N])
    v_bd = kit.sb("c_v_bd", [P, 2, PC, HEADS, 2, V1])
    rden = kit.sb("c_rden", [P, 2, 4 * G])
    o_sb = kit.sb("c_o", [P, 2, PC, 2, G * HD])
    o_tok = kit.sb("c_o_tok", [P, 2, PC, D])
    oT = kit.sb("c_oT", [P, 2, TOK])

    zeroed, v_zeroed, v_ones = kit.sem("c_zeroed"), kit.sem("c_v_zeroed"), kit.sem("c_v_ones")
    x_in, ctx_in_s = kit.landings("c_x_in"), kit.landings("c_ctx_in")
    stat, rooted, normed = kit.sig("c_stat", 2), kit.sig("c_rooted", 2), kit.sig("c_normed")
    xT_ps, cT_ps, xcT_sb = kit.sig("c_xT_ps"), kit.sig("c_cT_ps"), kit.sig("c_xcT_sb", 2)
    q_ps, k_ps, v_ps = kit.sig("c_q_ps"), kit.sig("c_k_ps"), kit.sig("c_v_ps")
    qk_sb = kit.sig("c_qk_sb", 4)
    split = kit.sig("c_split", 6)
    parts_out = {n: kit.landings(f"c_{n}_out") for n in "qk"}
    filled = kit.landings("c_filled", 4 * len(RUNS))
    spread_dve, spread_act = kit.sig("c_spread_dve", 2), kit.sig("c_spread_act", 2)
    sc_ps, mx_sb = kit.sig("c_sc_ps", 4), kit.sig("c_mx_sb", 4)
    mT_ps, mT_sb = kit.sig("c_mT_ps"), kit.sig("c_mT_sb")
    max_out = kit.sig("c_max_out", 16)
    max_in = kit.landings("c_max_in", 2)
    st_ps, p_sb, o_ps = kit.sig("c_st_ps", 4), kit.sig("c_p_sb", 4), kit.sig("c_o_ps", 4)
    v_sb = kit.sig("c_v_sb")
    den, o_norm = kit.sig("c_den", 2), kit.sig("c_o_norm", 4)
    shuffled = kit.landings("c_shuffled", 4)
    oT_ps, oT_sb, wo_ps, x2_sb = kit.sig("c_oT_ps"), kit.sig("c_oT_sb"), kit.sig("c_wo_ps"), kit.sig("c_x2_sb")

    x1_v = x1_dram.rearrange("(c p r) n d -> c (r n) p d", p=PC, r=2)
    ctx_v = ctx_in.rearrange("(c p r) n d -> c (r n) p d", p=PC, r=2)
    first, last, lo, hi = -4, CHUNKS + 1, 3, CHUNKS - 4

    def dram(ap, c):
        return ap[bass.ds(c.v, 1)].rearrange("o a b d -> (o a) b d")

    def x_tok(c, p):
        return x_all[:, bass.ds(c.v * PC + p, 1), :].rearrange("p a d -> p (a d)")

    with nc.Block() as block:
        @block.sync
        def _(sp):
            def step(t):
                c = t.plus(8)
                if c:
                    if c.plus(-4): sp.wait_ge(x_in.of(c.plus(-4)), x_in.at(c.plus(-4)))
                    sp.dma_start(x_all[:, bass.ts(c.v, PC), :], dram(x1_v, c)).then_inc(x_in.of(c), 16)
                c = t.plus(6)
                if c:
                    if c.plus(-4): sp.wait_ge(cT_ps.sem, cT_ps.at(c.plus(-4)))
                    sp.dma_start(ctx_sb[:, c.m4], dram(ctx_v, c)).then_inc(ctx_in_s.of(c), 16)
                c = t.plus(1)
                if c:
                    sp.wait_ge(mT_sb.sem, mT_sb.at(c))
                    sp.dma_start(max_dram[bass.ds(c.v, 1)].rearrange("o a t -> (o a) t"), negmax[:, c.m2, :]).then_inc(max_out.sem, 16)
                c = t.plus(-1)
                if c:
                    if c.plus(-2): sp.wait_ge(oT_ps.sem, oT_ps.at(c.plus(-2)))
                    sp.wait_ge(o_norm.sem, o_norm.at(c))
                    for j in range(2):
                        for r in range(2):
                            sp.dma_start(o_tok[N * r:N * (r + 1), c.m2, :, G * HD * j:G * HD * (j + 1)],
                                         o_sb[N * j:N * (j + 1), c.m2, :, r, :]).then_inc(shuffled.of(c), 16)
                c = t.plus(2)
                if c:
                    for k, n in enumerate("qk"):
                        sp.wait_ge(split.sem, split.at(c, 3 * k + 3))
                        sp.dma_start(dram(part_dram[n], c).rearrange("a p t -> p a t"), part[n][:, c.m2]).then_inc(
                            parts_out[n].of(c), 16)
                c = t.plus(1)
                if c:
                    sp.wait_ge(max_out.sem, max_out.at(c))
                    for j in range(2):
                        src = max_dram[bass.ds(c.v, 1)].rearrange("o (g j p) t -> j o g (p t)", g=G, j=2)[j]
                        sp.dma_start(q_st[MROW + j:MROW + j + 1, c.m2, :, j, :], src).then_inc(max_in.of(c), 16)
                c = t.plus(2)
                if c:
                    if c.plus(-2): sp.wait_ge(st_ps.sem, st_ps.at(c.plus(-2)))
                    for n in "qk":
                        sp.wait_ge(parts_out[n].of(c), parts_out[n].at(c))
                        src = dram(part_dram[n], c)
                        for u, length in RUNS:
                            at = 3 - length if n == "q" else 0
                            for j in range(2):
                                row = j * PRODUCTS * HD + u * HD
                                dst = q_st[row:row + length * HD, c.m2, :, j, :] if n == "q" else k_st[row:row + length * HD, c.m2, :, :]
                                sp.dma_start(dst, src[at:at + length].rearrange("a (d g j) t -> j (a d) g t", d=HD, j=2)[j]).then_inc(
                                    filled.of(c), 16)
            walk(sp, step, -8, last, lo, CHUNKS - 8)

        @block.gpsimd
        def _(pool):
            nc.gpsimd.memset(q_st[:].rearrange("p a g j t -> p (a g j t)").bitcast(F32), 0.0).then_inc(zeroed, 1)

            def step(t):
                c = t.plus(4)
                if c:
                    pool.wait_ge(stat.sem, stat.at(c))
                    if c.plus(-2): pool.wait_ge(normed.sem, normed.at(c.plus(-2)))
                    nc.gpsimd.tensor_tensor(rstd[:, c.m2, :], mv[:, c.m2, :, 1], w["ln_eps"][:], ALU.add).then_inc(rooted.sem, 1)
                    pool.wait_ge(rooted.sem, rooted.at(c, 1))
                    nc.gpsimd.tensor_tensor(rstd[:, c.m2, :], rstd[:, c.m2, :], w["neg_half"][:, 0:PC],
                                            ALU.pow).then_inc(rooted.sem, 1)
                c = t.plus(3)
                if c:
                    for k, n in enumerate("qk"):
                        pool.wait_ge(qk_sb.sem, qk_sb.at(c, 2 * k + 2))
                        if c.plus(-2): pool.wait_ge(parts_out[n].of(c.plus(-2)), parts_out[n].at(c.plus(-2)))
                        if c.plus(-1): pool.wait_ge(split.sem, split.at(c.plus(-1), 3 * k + 3))
                        a, p, r = full[n][:, c.m2], part[n][:, c.m2], rest[n][:]
                        nc.gpsimd.tensor_tensor(p[:, 1], a, p[:, LEAD[n]], ALU.subtract).then_inc(split.sem, 1)
                        nc.gpsimd.tensor_tensor(r, a, p[:, LEAD[n]], ALU.subtract).then_inc(split.sem, 1)
                        pool.wait_ge(split.sem, split.at(c, 3 * k + 2))
                        nc.gpsimd.tensor_tensor(p[:, LAST[n]], r, p[:, 1], ALU.subtract).then_inc(split.sem, 1)
            walk(pool, step, first, last, lo, hi)

        @block.vector
        def _(dve):
            nc.vector.memset(v_bd[:], 0.0).then_inc(v_zeroed, 1)
            nc.vector.memset(k_st[MROW:MROW + 2].rearrange("p a g t -> p (a g t)").bitcast(F32), ONES_BF16).then_inc(zeroed, 1)
            dve.wait_ge(v_zeroed, 1)
            for r in range(2):
                nc.vector.memset(v_bd[N * r:N * (r + 1), :, :, :, r, HD:V1], 1.0).then_inc(v_ones, 1)

            def spread(c, h):
                if not c:
                    return
                dve.wait_ge(qk_sb.sem, qk_sb.at(c))
                if c.plus(-1): dve.wait_ge(sc_ps.sem, sc_ps.at(c.plus(-1), 2 * h + 2))
                for head in range(DVE_HEADS):
                    ins = nc.vector.tensor_scalar(k_bd[:, h, head, :], part["k"][:, c.m2, 0, h * HT:(h + 1) * HT],
                                                  w["head_mask"][:, head:head + 1], None, ALU.mult)
                ins.then_inc(spread_dve.sem, 1)

            def row_max(c, p):
                if not c:
                    return
                if p == 0 and c.plus(-2): dve.wait_ge(mT_ps.sem, mT_ps.at(c.plus(-2)))
                dve.wait_ge(sc_ps.sem, sc_ps.at(c, p + 1))
                nc.vector.reduce_max(mx[:, c.m2, :, p],
                                     ps[:, 2:4, :].rearrange("p a (h m) -> p (a h) m", m=N), AX_X).then_inc(mx_sb.sem, 1)

            def normalise(c, h):
                if not c:
                    return
                if c.plus(-2): dve.wait_ge(shuffled.of(c.plus(-2)), shuffled.at(c.plus(-2)))
                dve.wait_ge(o_ps.sem, o_ps.at(c, 2 * h + 2))
                if c.plus(-1): dve.wait_ge(o_norm.sem, o_norm.at(c.plus(-1), 2 * h + 2))
                o = ps[:, 6 + h, 0:4 * G * V1].rearrange("p (a g r e) -> p a g r e", a=2, r=2, e=V1)
                nc.vector.reciprocal(rden[:, h], o[:, :, :, :, HD].rearrange("p a g r -> p (a g r)")).then_inc(den.sem, 1)
                dve.wait_ge(den.sem, den.at(c, h + 1))
                for p in range(2):
                    nc.vector.tensor_tensor(
                        o_sb[:, c.m2, 2 * h + p].rearrange("p r (g d) -> p g r d", g=G), o[:, p, :, :, 0:HD],
                        rden[:, h, 2 * G * p:2 * G * (p + 1)].rearrange("p (g r o) -> p g r o", r=2, o=1).to_broadcast([P, G, 2, HD]),
                        ALU.mult).then_inc(o_norm.sem, 1)

            def step(t):
                spread(t.plus(2), 1)
                normalise(t.plus(-1), 1)
                c = t.plus(4)
                if c:
                    dve.wait_ge(x_in.of(c), x_in.at(c))
                    if c.plus(-2): dve.wait_ge(stat.sem, stat.at(c.plus(-2)))
                    if c.plus(-2): dve.wait_ge(normed.sem, normed.at(c.plus(-2)))
                    for p in range(PC):
                        ins = nc.vector.bn_stats(stats[:, c.m2, p, :], x_tok(c, p))
                    ins.then_inc(stat.sem, 1)
                    dve.wait_ge(stat.sem, stat.at(c, 1))
                row_max(t.plus(2), 0)
                c = t.plus(4)
                if c:
                    for p in range(PC):
                        ins = nc.vector.bn_aggr(mv[:, c.m2, p, :], stats[:, c.m2, p, :])
                    ins.then_inc(stat.sem, 1)
                row_max(t.plus(2), 1)
                normalise(t.plus(0), 0)
                c = t.plus(1)
                if c:
                    dve.wait_ge(v_ps.sem, v_ps.at(c))
                    if c.plus(-2): dve.wait_ge(o_ps.sem, o_ps.at(c.plus(-2)))
                    if c.i is None and c.k == 0: dve.wait_ge(v_ones, 2)
                    for r in range(2):
                        at = slice(N * r, N * (r + 1))
                        ins = nc.vector.tensor_tensor(
                            v_bd[at, c.m2, :, :, r, 0:HD], ps[at, 0, :].rearrange("p (a h d) -> p a h d", a=PC, d=HD),
                            w["bv"][at].rearrange("p (o h d) -> p o h d", o=1, d=HD).to_broadcast([N, PC, HEADS, HD]), ALU.add)
                    ins.then_inc(v_sb.sem, 1)
                c = t.plus(4)
                if c:
                    dve.wait_ge(rooted.sem, rooted.at(c))
                    if c.plus(-2): dve.wait_ge(xT_ps.sem, xT_ps.at(c.plus(-2)))
                    for p in range(PC):
                        ins = nc.vector.tensor_scalar(xn[:, c.m2, p, :], x_tok(c, p), mv[:, c.m2, p, 0:1], rstd[:, c.m2, p:p + 1],
                                                      ALU.subtract, ALU.mult)
                    ins.then_inc(normed.sem, 1)
                row_max(t.plus(2), 2)
                row_max(t.plus(2), 3)
                spread(t.plus(3), 0)
                c = t.plus(-1)
                if c:
                    dve.wait_ge(wo_ps.sem, wo_ps.at(c))
                    nc.vector.tensor_tensor(x_all[:, bass.ts(c.v, PC), :], ps[:, 1, :].rearrange("p (a d) -> p a d", a=PC),
                                            x_all[:, bass.ts(c.v, PC), :], ALU.add).then_inc(x2_sb.sem, 1)
            walk(dve, step, first, last, lo, hi)

        @block.scalar
        def _(act):
            def exp(c, p):
                if not c:
                    return
                act.wait_ge(st_ps.sem, st_ps.at(c, p + 1))
                if p >= 2:
                    act.wait_ge(o_ps.sem, o_ps.at(c, p - 1))
                elif c.plus(-1):
                    act.wait_ge(o_ps.sem, o_ps.at(c.plus(-1), p + 3))
                nc.scalar.activation(prob[:, p % 2, :], ps[:, 4:6, :].rearrange("p a b -> p (a b)"), ACT.Exp,
                                     scale=float(HD) ** -0.5).then_inc(p_sb.sem, 1)

            def spread(c, h, head, to):
                if not c:
                    return
                if head == DVE_HEADS:
                    act.wait_ge(qk_sb.sem, qk_sb.at(c))
                    if c.plus(-1): act.wait_ge(sc_ps.sem, sc_ps.at(c.plus(-1), 2 * h + 2))
                for head in range(head, to):
                    ins = nc.scalar.activation(k_bd[:, h, head, :], part["k"][:, c.m2, 0, h * HT:(h + 1) * HT], ACT.Copy,
                                               scale=w["head_mask"][:, head:head + 1])
                if to == HEADS:
                    ins.then_inc(spread_act.sem, 1)

            def step(t):
                exp(t.plus(0), 0)
                c = t.plus(1)
                if c:
                    act.wait_ge(mT_ps.sem, mT_ps.at(c))
                    if c.plus(-2): act.wait_ge(max_out.sem, max_out.at(c.plus(-2)))
                    nc.scalar.activation(negmax[:, c.m2, :], ps[0:PC * HEADS, 0, 0:P], ACT.Copy, scale=-1.0).then_inc(mT_sb.sem, 1)
                c = t.plus(3)
                if c:
                    act.wait_ge(cT_ps.sem, cT_ps.at(c))
                    if c.plus(-4): act.wait_ge(v_ps.sem, v_ps.at(c.plus(-4)))
                    nc.scalar.activation(cT[:, c.m4, :], ps[:, 1, :], ACT.Copy).then_inc(xcT_sb.sem, 1)
                    act.wait_ge(xT_ps.sem, xT_ps.at(c))
                    if c.plus(-2): act.wait_ge(q_ps.sem, q_ps.at(c.plus(-2)))
                    nc.scalar.activation(xT[:, c.m2, :], ps[:, 0, :], ACT.Copy).then_inc(xcT_sb.sem, 1)
                exp(t.plus(0), 1)
                spread(t.plus(2), 1, DVE_HEADS, HEADS)
                c = t.plus(3)
                if c:
                    for k, (n, ready) in enumerate((("q", q_ps), ("k", k_ps))):
                        act.wait_ge(ready.sem, ready.at(c))
                        if c.plus(-2):
                            act.wait_ge(split.sem, split.at(c.plus(-2), 3 * k + 3))
                            act.wait_ge(parts_out[n].of(c.plus(-2)), parts_out[n].at(c.plus(-2)))
                            act.wait_ge(sc_ps.sem, sc_ps.at(c.plus(-2)))
                        nc.scalar.activation(full[n][:, c.m2, :], ps[:, k, :], ACT.Identity, bias=w["bqk"][:, k:k + 1]).then_inc(qk_sb.sem, 1)
                        nc.scalar.activation(part[n][:, c.m2, LEAD[n], :], ps[:, k, :], ACT.Identity, bias=w["bqk"][:, k:k + 1]).then_inc(qk_sb.sem, 1)
                        if k == 0:
                            exp(t.plus(0), 2)
                elif t.plus(0):
                    exp(t.plus(0), 2)
                c = t.plus(-1)
                if c:
                    act.wait_ge(oT_ps.sem, oT_ps.at(c))
                    if c.plus(-2): act.wait_ge(wo_ps.sem, wo_ps.at(c.plus(-2)))
                    nc.scalar.activation(oT[:, c.m2, :], ps[:, 1, :], ACT.Copy).then_inc(oT_sb.sem, 1)
                exp(t.plus(0), 3)
                spread(t.plus(3), 0, DVE_HEADS, HEADS)
            walk(act, step, first, last, lo, hi)

        @block.tensor
        def _(pe):
            pe.wait_ge(zeroed, 2)
            pe.wait_ge(v_ones, 2)

            def scores(c, p):
                if not c:
                    return
                if p % 2 == 0:
                    pe.wait_ge(spread_dve.sem, spread_dve.at(c, p // 2 + 1))
                    pe.wait_ge(spread_act.sem, spread_act.at(c, p // 2 + 1))
                if p:
                    pe.wait_ge(mx_sb.sem, mx_sb.at(c, p))
                else:
                    pe.wait_ge(qk_sb.sem, qk_sb.at(c, 2))
                    if c.plus(-1): pe.wait_ge(mx_sb.sem, mx_sb.at(c.plus(-1)))
                for b in range(2):
                    for r in range(2):
                        at = slice((2 * p + r) * N, (2 * p + r + 1) * N)
                        of = (p % 2 * 2 + r) * N
                        ins = nc.tensor.matmul(ps[N * r:N * (r + 1), 2 + b, :].rearrange("p (h m) -> p h m", m=N),
                                               part["q"][:, c.m2, LEAD["q"], at],
                                               k_bd[:, p // 2, 8 * b:8 * b + 8, of:of + N], start=True, stop=True)
                ins.then_inc(sc_ps.sem, 1)

            def scores_T(c, p):
                if not c:
                    return
                if p:
                    pe.wait_ge(p_sb.sem, p_sb.at(c, p))
                else:
                    pe.wait_ge(filled.of(c), filled.at(c))
                    pe.wait_ge(max_in.of(c), max_in.at(c))
                    if c.plus(-1): pe.wait_ge(p_sb.sem, p_sb.at(c.plus(-1)))
                for g in range(G):
                    for r in range(2):
                        at = slice((2 * p + r) * N, (2 * p + r + 1) * N)
                        ins = nc.tensor.matmul(
                            ps[N * r:N * (r + 1), 4 + g // 4, (g % 4) * P:(g % 4 + 1) * P].rearrange("p (j n) -> p j n", j=2),
                            k_st[0:MROW + 2, c.m2, g, at], q_st[0:MROW + 2, c.m2, g, :, at], start=True, stop=True)
                ins.then_inc(st_ps.sem, 1)

            def values(c, p):
                if not c:
                    return
                pe.wait_ge(p_sb.sem, p_sb.at(c, p + 1))
                if p == 0:
                    pe.wait_ge(v_sb.sem, v_sb.at(c))
                if p % 2 == 0:
                    if c.plus(-1): pe.wait_ge(o_norm.sem, o_norm.at(c.plus(-1), p + 2))
                for g in range(G):
                    for j in range(2):
                        at = (p % 2) * 2 * G * V1 + g * 2 * V1
                        ins = nc.tensor.matmul(ps[N * j:N * (j + 1), 6 + p // 2, at:at + 2 * V1].rearrange("p (r e) -> p r e", r=2),
                                               prob[:, p % 2, (2 * g + j) * N:(2 * g + j + 1) * N],
                                               v_bd[:, c.m2, p, 2 * g + j], start=True, stop=True)
                ins.then_inc(o_ps.sem, 1)

            def step(t):
                scores_T(t.plus(0), 0)
                c = t.plus(1)
                if c:
                    pe.wait_ge(mx_sb.sem, mx_sb.at(c))
                    if c.plus(-1): pe.wait_ge(v_sb.sem, v_sb.at(c.plus(-1)))
                    elif c.plus(1): pe.wait_ge(qk_sb.sem, qk_sb.at(c.plus(1), 2))
                values(t.plus(-1), 3)
                if c:
                    nc.tensor.transpose(ps[0:PC * HEADS, 0, 0:P], mx[:, c.m2].rearrange("p h a -> p (h a)"), w["ident"][:]).then_inc(mT_ps.sem, 1)
                c = t.plus(3)
                if c:
                    pe.wait_ge(ctx_in_s.of(c), ctx_in_s.at(c))
                    if c.plus(-5): pe.wait_ge(x2_sb.sem, x2_sb.at(c.plus(-5)))
                    elif c.plus(-1): pe.wait_ge(qk_sb.sem, qk_sb.at(c.plus(-1)))
                    for p in range(PC):
                        ins = nc.tensor.transpose(ps[:, 1, p * P:(p + 1) * P], ctx_sb[:, c.m4, p, :], w["ident"][:])
                    ins.then_inc(cT_ps.sem, 1)
                    pe.wait_ge(normed.sem, normed.at(c))
                    if c.plus(-2): pe.wait_ge(mT_sb.sem, mT_sb.at(c.plus(-2)))
                    elif c.plus(-1): pe.wait_ge(qk_sb.sem, qk_sb.at(c.plus(-1), 2))
                    for p in range(PC):
                        ins = nc.tensor.transpose(ps[:, 0, p * P:(p + 1) * P], xn[:, c.m2, p, :], w["ident"][:])
                    ins.then_inc(xT_ps.sem, 1)
                scores(t.plus(2), 0)
                scores_T(t.plus(0), 1)
                values(t.plus(0), 0)
                c = t.plus(3)
                if c:
                    pe.wait_ge(xcT_sb.sem, xcT_sb.at(c))
                    nc.tensor.matmul(ps[:, 0, :], w["wqT"][:], xT[:, c.m2, :], start=True, stop=True).then_inc(q_ps.sem, 1)
                    nc.tensor.matmul(ps[:, 1, :], w["wkT"][:], cT[:, c.m4, :], start=True, stop=True).then_inc(k_ps.sem, 1)
                scores_T(t.plus(0), 2)
                scores(t.plus(2), 1)
                values(t.plus(0), 1)
                c = t.plus(1)
                if c:
                    if c.plus(2): pe.wait_ge(qk_sb.sem, qk_sb.at(c.plus(2), 2))
                    else: pe.wait_ge(mT_sb.sem, mT_sb.at(c))
                    for p in range(PC):
                        ins = nc.tensor.matmul(ps[:, 0, p * P:(p + 1) * P], cT[:, c.m4, p * P:(p + 1) * P], w["wvT"][:],
                                               start=True, stop=True)
                    ins.then_inc(v_ps.sem, 1)
                scores(t.plus(2), 2)
                c = t.plus(-1)
                if c:
                    pe.wait_ge(shuffled.of(c), shuffled.at(c))
                    if c.plus(4): pe.wait_ge(qk_sb.sem, qk_sb.at(c.plus(4)))
                    else: pe.wait_ge(x2_sb.sem, x2_sb.at(c.plus(-1)))
                    for p in range(PC):
                        ins = nc.tensor.transpose(ps[:, 1, p * P:(p + 1) * P], o_tok[:, c.m2, p, :], w["ident"][:])
                    ins.then_inc(oT_ps.sem, 1)
                scores_T(t.plus(0), 3)
                values(t.plus(0), 2)
                scores(t.plus(2), 3)
                c = t.plus(-1)
                if c:
                    pe.wait_ge(oT_sb.sem, oT_sb.at(c))
                    for p in range(PC):
                        ins = nc.tensor.matmul(ps[:, 1, p * P:(p + 1) * P], oT[:, c.m2, p * P:(p + 1) * P], w["woT"][:],
                                               start=True, stop=True)
                    ins.then_inc(wo_ps.sem, 1)
            walk(pe, step, first, last, lo, hi)


def experts_in(nc, kit, block, ps, w, x_all, hidden, h_bd, comb_dram):
    stats = kit.sb("e_stats", [P, 2, PC, 6])
    mv = kit.sb("e_mv", [P, 2, PC, 2])
    rs = kit.sb("e_rs", [P, 2, PC])
    centred = kit.sb("e_centred", [P, 2, PC, D])
    xn = kit.sb("e_xn", [P, 4, PC, D])
    junk = kit.sb("e_junk", [P, PC, D])
    ss = kit.sb("e_ss", [P, 2, PC])
    sq = kit.sb("e_sq", [P, 2, PC])
    rn = kit.sb("e_rn", [P, 2, PC])
    xu = kit.sb("e_xu", [P, 2, PC, D])
    xuT = kit.sb("e_xuT", [P, 2, TOK])
    cm = kit.sb("e_cm", [P, 2, 2, SC])
    rm = kit.sb("e_rm", [P, 2, PC])
    neg_cm = kit.sb("e_neg_cm", [SC, 2, ES], BF16)
    neg_rm = kit.sb("e_neg_rm", [PC, 2, PC, P], BF16)
    sel32, sel = kit.sb("e_sel32", [SC, PC, P]), kit.sb("e_sel", [SC, PC, P], BF16)
    neg_diag = kit.sb("e_neg_diag", [PC, PC, P])
    ones4 = kit.sb("e_ones4", [PC, P], BF16)
    disp = kit.sb("e_disp", [P, 2, PC, 2, ES])
    comb = kit.sb("e_comb", [P, 2, 2, TOK])
    slot_in = kit.sb("e_slot_in", [P, 2, SC, ES])
    raw = kit.sb("e_raw", [P, 2, 2, TOK])
    rden = kit.sb("e_rden", [P, 2, 4, SC, SLOTS])
    scaled = kit.sb("e_scaled", [P, 2, 4, SC * SLOTS])

    cleared, selected, ready, made = kit.sem("e_cleared"), kit.sem("e_selected"), kit.sem("e_ready"), kit.sem("e_made")
    stat, root, normed = kit.sig("e_stat", 2), kit.sig("e_root", 4), kit.sig("e_normed", 2)
    squared, clamped, unit, xu_sb = kit.sig("e_squared"), kit.sig("e_clamped"), kit.sig("e_unit", 2), kit.sig("e_xu_sb")
    xuT_ps, xuT_sb = kit.sig("e_xuT_ps"), kit.sig("e_xuT_sb")
    lT_ps, lA_ps, max_sb = kit.sig("e_lT_ps"), kit.sig("e_lA_ps"), kit.sig("e_max_sb", 2)
    mT_ps, ncm_sb, nrm_sb = kit.sig("e_mT_ps"), kit.sig("e_ncm_sb"), kit.sig("e_nrm_sb")
    shA_ps, shT_ps, disp_sb, comb_sb = kit.sig("e_shA_ps"), kit.sig("e_shT_ps"), kit.sig("e_disp_sb"), kit.sig("e_comb_sb")
    in_ps, in_sb = kit.sig("e_in_ps", 2), kit.sig("e_in_sb", 2)
    h_ps, den_ps, raw_sb = kit.sig("e_h_ps"), kit.sig("e_den_ps"), kit.sig("e_raw_sb")
    rden_sb, divided, biased = kit.sig("e_rden_sb"), kit.sig("e_divided"), kit.sig("e_biased")
    comb_out = kit.landings("e_comb_out")
    first, last, lo, hi = -5, CHUNKS + 1, 3, CHUNKS - 5

    def tok(c, p):
        return x_all[:, bass.ds(c.v * PC + p, 1), :].rearrange("p a d -> p (a d)")

    @block.sync
    def _(sp):
        def step(c):
            sp.wait_ge(comb_sb.sem, comb_sb.at(c))
            sp.dma_start(comb_dram[bass.ds(c.v, 1)].rearrange("o p t -> (o p) t"),
                         comb[:, c.m2].rearrange("p a t -> p (a t)")).then_inc(comb_out.of(c), 16)
        walk(sp, step, 0, CHUNKS, 4, CHUNKS)
        for k in range(CHUNKS - 4, CHUNKS):
            sp.wait_ge(comb_out.of(Chunk(None, k)), comb_out.at(Chunk(None, k)))

    @block.gpsimd
    def _(pool):
        def step(t):
            c = t.plus(3)
            if c:
                pool.wait_ge(clamped.sem, clamped.at(c))
                if c.plus(-2): pool.wait_ge(xu_sb.sem, xu_sb.at(c.plus(-2)))
                nc.gpsimd.tensor_tensor(rn[:, c.m2], sq[:, c.m2], w["neg_half"][:, 0:PC], ALU.pow).then_inc(unit.sem, 1)
                pool.wait_ge(unit.sem, unit.at(c, 1))
                nc.gpsimd.tensor_tensor(rn[:, c.m2], rn[:, c.m2], w["scale"][:].to_broadcast([P, PC]),
                                        ALU.mult).then_inc(unit.sem, 1)
            c = t.plus(5)
            if c:
                pool.wait_ge(stat.sem, stat.at(c))
                if c.plus(-2): pool.wait_ge(normed.sem, normed.at(c.plus(-2)))
                v, rc = mv[:, c.m2, :, 1], rs[:, c.m2]
                nc.gpsimd.tensor_tensor(rc, v, w["ln_eps"][:], ALU.add).then_inc(root.sem, 1)
                pool.wait_ge(root.sem, root.at(c, 1))
                nc.gpsimd.tensor_tensor(rc, rc, w["ln_eps"][:], ALU.mult).then_inc(root.sem, 1)
                pool.wait_ge(root.sem, root.at(c, 2))
                nc.gpsimd.tensor_tensor(rc, rc, v, ALU.add).then_inc(root.sem, 1)
                pool.wait_ge(root.sem, root.at(c, 3))
                nc.gpsimd.tensor_tensor(rc, rc, w["neg_half"][:], ALU.pow).then_inc(root.sem, 1)
            if t.i is None and t.k == -4:
                nc.gpsimd.memset(sel32[:], 0.0).then_inc(cleared, 1)
                nc.gpsimd.memset(neg_diag[:], 0.0).then_inc(cleared, 1)
                pool.wait_ge(cleared, 2)
                nc.gpsimd.affine_select(out=sel32[:].rearrange("s p (r n) -> s p r n", r=2), in_=sel32[:].rearrange("s p (r n) -> s p r n", r=2),
                                        compare_op=ALU.not_equal, fill=1.0, base=0, pattern=[[-2, PC], [-1, 2], [0, N]],
                                        channel_multiplier=1).then_inc(selected, 1)
                nc.gpsimd.affine_select(out=neg_diag[:], in_=neg_diag[:], compare_op=ALU.not_equal, fill=-1.0, base=0,
                                        pattern=[[-1, PC], [0, P]], channel_multiplier=1).then_inc(selected, 1)
                pool.wait_ge(selected, 2)
                for r in range(2):
                    nc.gpsimd.memset(disp[N * r:N * (r + 1), :, :, 1 - r, :], 0.0).then_inc(ready, 1)
                pool.wait_ge(ready, 2)
                nc.gpsimd.memset(h_bd[:], 0.0).then_inc(cleared, 1)
            c = t.plus(-1)
            if c:
                pool.wait_ge(rden_sb.sem, rden_sb.at(c))
                if c.plus(-2): pool.wait_ge(biased.sem, biased.at(c.plus(-2)))
                nc.gpsimd.tensor_tensor(scaled[:, c.m2], raw[:, c.m2, 0].rearrange("p (g k) -> p g k", g=4),
                                        rden[:, c.m2].rearrange("p g s k -> p g (s k)"), ALU.mult).then_inc(divided.sem, 1)
                pool.wait_ge(divided.sem, divided.at(c))
                nc.gpsimd.tensor_tensor(hidden[:, :, bass.ts(c.v, SC * SLOTS)], scaled[:, c.m2],
                                        w["b1"][:].rearrange("p (g o) -> p g o", o=1).to_broadcast([P, 4, SC * SLOTS]),
                                        ALU.add).then_inc(biased.sem, 1)
        walk(pool, step, first, last, lo, hi)

    @block.vector
    def _(dve):

        def step(t):
            if t.i is None and t.k == -2:
                nc.vector.memset(ones4[:], 1.0).then_inc(made, 1)
                dve.wait_ge(selected, 2)
                nc.vector.tensor_copy(sel[:], sel32[:]).then_inc(made, 1)
            c = t.plus(1)
            if c:
                if c.plus(-2): dve.wait_ge(mT_ps.sem, mT_ps.at(c.plus(-2)))
                dve.wait_ge(lT_ps.sem, lT_ps.at(c))
                nc.vector.reduce_max(cm[:, c.m2].rearrange("p a s -> p (a s)"),
                                     ps[:, 3:5, :].rearrange("p a (s n) -> p (a s) n", n=N), AX_X).then_inc(max_sb.sem, 1)
                dve.wait_ge(lA_ps.sem, lA_ps.at(c))
                nc.vector.reduce_max(rm[:, c.m2], ps[:, 1:3, :].rearrange("p a (b e) -> p (a b) e", e=ES), AX_X).then_inc(max_sb.sem, 1)
            c = t.plus(3)
            if c:
                dve.wait_ge(squared.sem, squared.at(c))
                if c.plus(-2): dve.wait_ge(unit.sem, unit.at(c.plus(-2)))
                nc.vector.tensor_scalar(sq[:, c.m2], ss[:, c.m2], NORM_EPS ** 2, None, ALU.max).then_inc(clamped.sem, 1)
            c = t.plus(1)
            if c:
                dve.wait_ge(mT_ps.sem, mT_ps.at(c))
                if c.plus(-2): dve.wait_ge(shT_ps.sem, shT_ps.at(c.plus(-2)))
                nc.vector.tensor_tensor(neg_rm[:, c.m2], ps[0:PC, 5, 2 * P:3 * P].rearrange("q (o t) -> q o t", o=1).to_broadcast([PC, PC, P]),
                                        neg_diag[:], ALU.mult).then_inc(nrm_sb.sem, 1)
            c = t.plus(-1)
            if c:
                dve.wait_ge(raw_sb.sem, raw_sb.at(c))
                if c.plus(-2): dve.wait_ge(divided.sem, divided.at(c.plus(-2)))
                nc.vector.reciprocal(rden[:, c.m2], raw[:, c.m2, 1].rearrange("p (s g k) -> p g s k", s=SC, g=4)).then_inc(rden_sb.sem, 1)
            c = t.plus(5)
            if c:
                if c.plus(-2): dve.wait_ge(stat.sem, stat.at(c.plus(-2)))
                if c.plus(-2): dve.wait_ge(normed.sem, normed.at(c.plus(-2)))
                for p in range(PC):
                    ins = nc.vector.bn_stats(stats[:, c.m2, p, :], tok(c, p))
                ins.then_inc(stat.sem, 1)
            c = t.plus(4)
            if c:
                dve.wait_ge(root.sem, root.at(c))
                if c.plus(-2): dve.wait_ge(normed.sem, normed.at(c.plus(-2)))
                if c.plus(-4): dve.wait_ge(in_ps.sem, in_ps.at(c.plus(-4)))
                if c.plus(1): dve.wait_ge(stat.sem, stat.at(c.plus(1), 1))
                if c.plus(-4): dve.wait_ge(xu_sb.sem, xu_sb.at(c.plus(-4)))
                for p in range(PC):
                    ins = nc.vector.scalar_tensor_tensor(out=centred[:, c.m2, p], in0=tok(c, p), scalar=mv[:, c.m2, p, 0:1],
                                                         in1=w["gamma"][:], op0=ALU.subtract, op1=ALU.mult)
                ins.then_inc(normed.sem, 1)
            c = t.plus(5)
            if c:
                if not t.plus(4):
                    dve.wait_ge(stat.sem, stat.at(c, 1))
                for p in range(PC):
                    ins = nc.vector.bn_aggr(mv[:, c.m2, p, :], stats[:, c.m2, p, :])
                ins.then_inc(stat.sem, 1)
            c = t.plus(4)
            if c:
                dve.wait_ge(normed.sem, normed.at(c, 1))
                for p in range(PC):
                    ins = nc.vector.scalar_tensor_tensor(out=xn[:, c.m4, p], in0=centred[:, c.m2, p], scalar=rs[:, c.m2, p:p + 1],
                                                         in1=w["beta"][:], op0=ALU.mult, op1=ALU.add)
                ins.then_inc(normed.sem, 1)
            c = t.plus(3)
            if c:
                dve.wait_ge(unit.sem, unit.at(c))
                if c.plus(-2): dve.wait_ge(xuT_ps.sem, xuT_ps.at(c.plus(-2)))
                for p in range(PC):
                    ins = nc.vector.tensor_scalar(xu[:, c.m2, p], xn[:, c.m4, p], rn[:, c.m2, p:p + 1], None, ALU.mult)
                ins.then_inc(xu_sb.sem, 1)
        walk(dve, step, first, last, lo, hi)

    @block.scalar
    def _(act):
        def slots(c, h):
            if not c:
                return
            act.wait_ge(in_ps.sem, in_ps.at(c, h + 1))
            if c.plus(-2): act.wait_ge(h_ps.sem, h_ps.at(c.plus(-2)))
            nc.scalar.activation(slot_in[:, c.m2, 4 * h:4 * h + 4].rearrange("p s e -> p (s e)"),
                                 ps[:, 6:8, :].rearrange("p a b -> p (a b)"), ACT.Copy).then_inc(in_sb.sem, 1)

        def step(t):
            slots(t.plus(0), 0)
            c = t.plus(1)
            if c:
                act.wait_ge(mT_ps.sem, mT_ps.at(c))
                if c.plus(-2): act.wait_ge(shA_ps.sem, shA_ps.at(c.plus(-2)))
                act.wait_ge(nrm_sb.sem, nrm_sb.at(c))
                nc.scalar.activation(neg_cm[:, c.m2], ps[0:SC, 5, 0:ES], ACT.Copy, scale=-1.0).then_inc(ncm_sb.sem, 1)
            slots(t.plus(0), 1)
            if c:
                act.wait_ge(shT_ps.sem, shT_ps.at(c))
                if c.plus(-2): act.wait_ge(comb_out.of(c.plus(-2)), comb_out.at(c.plus(-2)))
                nc.scalar.activation(comb[:, c.m2].rearrange("p a e -> p (a e)"), ps[:, 3:5, :].rearrange("p a b -> p (a b)"),
                                     ACT.Exp).then_inc(comb_sb.sem, 1)
            c = t.plus(2)
            if c:
                act.wait_ge(xuT_ps.sem, xuT_ps.at(c))
                if c.plus(-2): act.wait_ge(lA_ps.sem, lA_ps.at(c.plus(-2)))
                nc.scalar.activation(xuT[:, c.m2], ps[:, 0, :], ACT.Copy).then_inc(xuT_sb.sem, 1)
            c = t.plus(1)
            if c:
                act.wait_ge(shA_ps.sem, shA_ps.at(c))
                if c.plus(-2): act.wait_ge(in_ps.sem, in_ps.at(c.plus(-2)))
                if c.plus(-2): act.wait_ge(den_ps.sem, den_ps.at(c.plus(-2)))
                for r in range(2):
                    at = slice(N * r, N * (r + 1))
                    ins = nc.scalar.activation(disp[at, c.m2, :, r, :], ps[at, 1:3, :].rearrange("p a (b e) -> p (a b) e", b=2), ACT.Exp)
                ins.then_inc(disp_sb.sem, 1)
            c = t.plus(0)
            if c:
                act.wait_ge(den_ps.sem, den_ps.at(c))
                if c.plus(-2): act.wait_ge(divided.sem, divided.at(c.plus(-2)))
                nc.scalar.activation(raw[:, c.m2].rearrange("p a b -> p (a b)"), ps[:, 6:8, :].rearrange("p a b -> p (a b)"),
                                     ACT.Copy).then_inc(raw_sb.sem, 1)
            c = t.plus(4)
            if c:
                act.wait_ge(normed.sem, normed.at(c))
                if c.plus(-2): act.wait_ge(clamped.sem, clamped.at(c.plus(-2)))
                if c.plus(-1): act.wait_ge(squared.sem, squared.at(c.plus(-1)))
                for p in range(PC):
                    ins = nc.scalar.activation(junk[:, p], xn[:, c.m4, p], ACT.Square, accum_out=ss[:, c.m2, p:p + 1])
                ins.then_inc(squared.sem, 1)
        walk(act, step, first, last, lo, hi)

    @block.tensor
    def _(pe):

        def gather(c, h):
            if not c:
                return
            if c.i is None and c.k == 0: pe.wait_ge(ready, 2)
            pe.wait_ge(disp_sb.sem, disp_sb.at(c))
            if h:
                pe.wait_ge(in_sb.sem, in_sb.at(c, 1))
            else:
                if c.plus(-1): pe.wait_ge(in_sb.sem, in_sb.at(c.plus(-1)))
                if c.plus(-1): pe.wait_ge(raw_sb.sem, raw_sb.at(c.plus(-1)))
            for a in range(2):
                ins = nc.tensor.matmul(ps[:, 6 + a, :], xn[:, c.m4, 2 * h + a, :],
                                       disp[:, c.m2, 2 * h + a].rearrange("p r e -> p (r e)"), start=True, stop=True)
            ins.then_inc(in_ps.sem, 1)

        def step(t):
            c = t.plus(1)
            if c:
                pe.wait_ge(xuT_sb.sem, xuT_sb.at(c))
                if c.plus(-1): pe.wait_ge(comb_sb.sem, comb_sb.at(c.plus(-1)))
                for h in range(2):
                    ins = nc.tensor.matmul(ps[:, 3 + h, :], w["mu"][:, h * P:(h + 1) * P], xuT[:, c.m2, :],
                                           start=True, stop=False, skip_group_check=True)
                ins.then_inc(lT_ps.sem, 1)
                if c.plus(-1): pe.wait_ge(disp_sb.sem, disp_sb.at(c.plus(-1)))
                for p in range(PC):
                    ins = nc.tensor.matmul(ps[:, 1 + p // 2, p % 2 * ES:(p % 2 + 1) * ES], xuT[:, c.m2, p * P:(p + 1) * P],
                                           w["mu"][:], start=p % 2 == 0, stop=False, skip_group_check=True)
                ins.then_inc(lA_ps.sem, 1)
            gather(t.plus(0), 0)
            c = t.plus(1)
            if c:
                pe.wait_ge(max_sb.sem, max_sb.at(c))
                for h in range(2):
                    nc.tensor.transpose(ps[0:SC, 5, h * P:(h + 1) * P], cm[:, c.m2, h, :], w["ident"][:])
                nc.tensor.transpose(ps[0:PC, 5, 2 * P:3 * P], rm[:, c.m2, :], w["ident"][:]).then_inc(mT_ps.sem, 1)
            gather(t.plus(0), 1)
            c = t.plus(1)
            if c:
                if t.i is None and t.k == -1: pe.wait_ge(made, 2)
                pe.wait_ge(nrm_sb.sem, nrm_sb.at(c))
                pe.wait_ge(ncm_sb.sem, ncm_sb.at(c))
                for h in range(2):
                    ins = nc.tensor.matmul(ps[:, 3 + h, :], ones4[:], neg_rm[:, c.m2].rearrange("q a t -> q (a t)"),
                                           start=False, stop=True, skip_group_check=True)
                ins.then_inc(shT_ps.sem, 1)
                for p in range(PC):
                    ins = nc.tensor.matmul(ps[:, 1 + p // 2, p % 2 * ES:(p % 2 + 1) * ES], sel[:, p, :], neg_cm[:, c.m2],
                                           start=False, stop=True, skip_group_check=True)
                ins.then_inc(shA_ps.sem, 1)
            c = t.plus(2)
            if c:
                pe.wait_ge(xu_sb.sem, xu_sb.at(c))
                if c.plus(-1): pe.wait_ge(xuT_sb.sem, xuT_sb.at(c.plus(-1)))
                for p in range(PC):
                    ins = nc.tensor.transpose(ps[:, 0, p * P:(p + 1) * P], xu[:, c.m2, p, :], w["ident"][:])
                ins.then_inc(xuT_ps.sem, 1)
            c = t.plus(0)
            if c:
                pe.wait_ge(in_sb.sem, in_sb.at(c))
                for g in range(4):
                    for e in range(4):
                        x = 4 * g + e
                        ins = nc.tensor.matmul(ps[HID * e:HID * (e + 1), 6, g * P:(g + 1) * P].rearrange("p (s k) -> p s k", s=SC),
                                               w["w1"][:, x, :], slot_in[:, c.m2, :, x * SLOTS:(x + 1) * SLOTS],
                                               start=True, stop=True)
                ins.then_inc(h_ps.sem, 1)
            c = t.plus(0)
            if c:
                for e in range(4):
                    ins = nc.tensor.matmul(
                        ps[HID * e:HID * (e + 1), 7, :].rearrange("p (s g k) -> p s g k", s=SC, g=4), w["ones"][:, 0:HID],
                        disp[:, c.m2].rearrange("p a r (g e k) -> p (a r) g e k", g=4, e=4)[:, :, :, e, :], start=True, stop=True)
                ins.then_inc(den_ps.sem, 1)
        walk(pe, step, first, last, lo, hi)
    return Before(biased, disp_sb, cleared)


def experts_out(nc, kit, block, ps, w, x_all, hidden, h_bd, comb_dram, before, out):
    slot_out = kit.sb("o_slot_out", [P, 2, SC, 2, D + 1])
    comb = kit.sb("o_comb", [P, 2, 2, TOK])
    rden = kit.sb("o_rden", [P, 2, PC])
    y = kit.sb("o_y", [P, 2, PC, D])

    zeroed = kit.sem("o_zeroed")
    act_sb = kit.sig("o_act_sb")
    s_ps, s_sb = kit.sig("o_s_ps", 4), kit.sig("o_s_sb", 4)
    comb_in = kit.landings("o_comb_in")
    y_ps, den, y_sb = kit.sig("o_y_ps", 4), kit.sig("o_den", 2), kit.sig("o_y_sb", 2)
    y_out = kit.landings("o_y_out")
    out_v = out.rearrange("(c p r) n d -> c (r n) p d", p=PC, r=2)
    first, last, lo, hi = -2, CHUNKS, 2, CHUNKS - 2

    @block.sync
    def _(sp):
        def step(t):
            c = t.plus(2)
            if c:
                if c.plus(-2): sp.wait_ge(y_ps.sem, y_ps.at(c.plus(-2)))
                sp.dma_start(comb[:, c.m2].rearrange("p a t -> p (a t)"),
                             comb_dram[bass.ds(c.v, 1)].rearrange("o p t -> (o p) t")).then_inc(comb_in.of(c), 16)
            c = t.plus(0)
            if c:
                sp.wait_ge(y_sb.sem, y_sb.at(c))
                sp.dma_start(out_v[bass.ds(c.v, 1)].rearrange("o a b d -> (o a) b d"), y[:, c.m2]).then_inc(y_out.of(c), 16)
        walk(sp, step, first, last, lo, hi)
        for k in range(CHUNKS - 4, CHUNKS):
            sp.wait_ge(y_out.of(Chunk(None, k)), y_out.at(Chunk(None, k)))

    @block.scalar
    def _(act):
        act.wait_ge(before.cleared, 3)

        def step(t):
            c = t.plus(2)
            if c:
                if c.plus(-2): act.wait_ge(s_ps.sem, s_ps.at(c.plus(-2)))
                act.wait_ge(before.biased.sem, before.biased.at(c))
                for e in range(4):
                    at = slice(HID * e, HID * (e + 1))
                    ins = nc.scalar.activation(
                        h_bd[at, c.m2, :, :, e, :].rearrange("p s g k -> p g s k"),
                        hidden[at, :, bass.ts(c.v, SC * SLOTS)].rearrange("p g (s k) -> p g s k", s=SC), ACT.Gelu)
                ins.then_inc(act_sb.sem, 1)
        walk(act, step, first, last, lo, hi)

    @block.vector
    def _(dve):
        nc.vector.memset(slot_out[:, :, :, :, D:D + 1], 1.0).then_inc(zeroed, 1)

        def finish(c, h):
            if not c:
                return
            dve.wait_ge(y_ps.sem, y_ps.at(c, 2 * h + 2))
            if c.plus(-2): dve.wait_ge(y_sb.sem, y_sb.at(c.plus(-2)))
            if c.plus(-2): dve.wait_ge(y_out.of(c.plus(-2)), y_out.at(c.plus(-2)))
            o = ps[:, 4 + h, 0:2 * (D + 1)].rearrange("p (a e) -> p a e", a=2)
            nc.vector.reciprocal(rden[:, c.m2, 2 * h:2 * h + 2], o[:, :, D]).then_inc(den.sem, 1)
            dve.wait_ge(den.sem, den.at(c, h + 1))
            for p in range(2):
                q = 2 * h + p
                ins = nc.vector.scalar_tensor_tensor(
                    out=y[:, c.m2, q], in0=o[:, p, 0:D], scalar=rden[:, c.m2, q:q + 1],
                    in1=x_all[:, bass.ds(c.v * PC + q, 1), :].rearrange("p a d -> p (a d)"), op0=ALU.mult, op1=ALU.add)
            ins.then_inc(y_sb.sem, 1)

        def step(t):
            for p in range(PC):
                c = t.plus(1)
                if c:
                    dve.wait_ge(s_ps.sem, s_ps.at(c, p + 1))
                    if c.plus(-2): dve.wait_ge(y_ps.sem, y_ps.at(c.plus(-2)))
                    nc.vector.tensor_tensor(slot_out[:, c.m2, 2 * p:2 * p + 2, :, 0:D],
                                            ps[:, p, :].rearrange("p (s a d) -> p s a d", s=2, a=2),
                                            w["b2"][:].rearrange("p (o a) d -> p o a d", o=1).to_broadcast([P, 2, 2, D]),
                                            ALU.add).then_inc(s_sb.sem, 1)
                if p % 2:
                    finish(t.plus(0), p // 2)
        walk(dve, step, first, last, lo, hi)

    @block.tensor
    def _(pe):
        end = Chunk(None, CHUNKS - 1)
        pe.wait_ge(zeroed, 1)
        pe.wait_ge(before.disp_sb.sem, before.disp_sb.at(end))

        def step(t):
            for p in range(PC):
                c = t.plus(1)
                if c:
                    if p == 0:
                        pe.wait_ge(act_sb.sem, act_sb.at(c))
                    if c.plus(-1): pe.wait_ge(s_sb.sem, s_sb.at(c.plus(-1), p + 1))
                    for s in range(2 * p, 2 * p + 2):
                        for g in range(4):
                            at = (s % 2) * 2 * D + (g // 2) * D
                            ins = nc.tensor.matmul(ps[64 * (g % 2):64 * (g % 2) + 64, p, at:at + D],
                                                   h_bd[:, c.m2, s, g].rearrange("p e k -> p (e k)"), w["w2"][:, g, :],
                                                   start=True, stop=True)
                    ins.then_inc(s_ps.sem, 1)
                c = t.plus(0)
                if c:
                    if p == 0:
                        pe.wait_ge(comb_in.of(c), comb_in.at(c))
                        pe.wait_ge(s_sb.sem, s_sb.at(c))
                    if p % 2 == 0:
                        if c.plus(-1): pe.wait_ge(y_sb.sem, y_sb.at(c.plus(-1), p // 2 + 1))
                    for r in range(2):
                        s = 2 * p + r
                        for h in range(2):
                            ins = nc.tensor.matmul(ps[N * r:N * (r + 1), 4 + p // 2, (p % 2) * (D + 1):(p % 2 + 1) * (D + 1)],
                                                   comb[:, c.m2, h, s * N:(s + 1) * N], slot_out[:, c.m2, s, h, :],
                                                   start=h == 0, stop=h == 1)
                    ins.then_inc(y_ps.sem, 1)
        walk(pe, step, first, last, lo, hi)


def build(nc, a, out):
    with ExitStack() as forever:
        ps = forever.enter_context(nc.psum_tensor("ps", [P, 8, TOK], F32))
        kit = Kit(nc, forever, forever)
        w = {}
        x1_dram = nc.dram_tensor("x1_scratch", [S, N, D], F32).ap()
        comb_dram = nc.dram_tensor("combine_scratch", [CHUNKS, P, 2 * TOK], F32).ap()
        weight_tiles(kit, w)
        with ExitStack() as ctx:
            self_attention(nc, Kit(nc, forever, ctx), ps, w, a, x1_dram)
        x_all = kit.sb("x_all", [P, S // 2, D])
        with ExitStack() as ctx:
            cross_attention(nc, Kit(nc, forever, ctx), ps, w, x1_dram, a["ctx_1024"], x_all)
        hidden = kit.sb("hidden", [P, 4, S * SLOTS])
        h_bd = kit.sb("h_bd", [P, 2, SC, 4, 4, SLOTS])
        with nc.Block() as block:
            before = experts_in(nc, kit, block, ps, w, x_all, hidden, h_bd, comb_dram)
            experts_out(nc, kit, block, ps, w, x_all, hidden, h_bd, comb_dram, before, out)


_INS = ["x", "ctx_1024", "L0_attn_Wq", "L0_attn_Wk", "L0_xattn_Wq", "L0_xattn_bq", "L0_xattn_Wk", "L0_xattn_bk",
        "L0_xattn_Wv", "L0_xattn_bv", "L0_xattn_Wo", "L0_ffn_ln_gamma", "L0_ffn_ln_beta", "L0_ffn_mu", "L0_ffn_scale",
        "L0_ffn_w1", "L0_ffn_b1", "L0_ffn_w2", "L0_ffn_b2"]


def kernel(**inputs):
    import numpy as _np
    import concourse.bacc as _bacc
    from concourse import mybir as _mybir
    from concourse.bass_utils import run_bass_kernel_spmd as _run

    nc = _bacc.Bacc("TRN2", target_bir_lowering=False, num_devices=1)
    arrays, args = {}, {}
    for name in _INS:
        a = _np.ascontiguousarray(inputs[name])
        arrays[f"in_{name}"] = a
        args[name] = nc.dram_tensor(f"in_{name}", a.shape, _mybir.dt.from_np(a.dtype), kind="ExternalInput").ap()
    out = nc.dram_tensor("out_0", (S, N, D), F32, kind="ExternalOutput").ap()
    build(nc, args, out)
    r = _run(nc, [arrays], core_ids=[0])
    return r.results[0]["out_0"]
```
